# Optimizing a Trainium2 kernel written in Bass

```python
import numpy as np
import jax
import jax.numpy as jnp

def _softmax(x, axis=-1):
    return jax.nn.softmax(x, axis=axis)

def _gelu(x):
    return jax.nn.gelu(x, approximate=True)

def _silu(x):
    return jax.nn.silu(x)

def _sigmoid(x):
    return jax.nn.sigmoid(x)

def _layernorm(x, axis=-1, eps=1e-05):
    m = jnp.mean(x, axis=axis, keepdims=True)
    v = jnp.var(x, axis=axis, keepdims=True)
    return (x - m) / jnp.sqrt(v + eps)

def _scatter_add(tgt, idx, src, axis=0):
    return tgt.at[idx].add(src)

def _segment_sum(src, seg, n):
    return jax.ops.segment_sum(src, seg, n)
kernel_name = 'mk_gnn_resnorm_d4_gnn_r32_267b1c'

def setup_inputs(seed: int=0):
    np.random.seed(seed)
    _w = jnp.asarray

    def _rec_inputs():
        import jax
        import jax.numpy as jnp
        _gk = jax.random.key(seed)
        x = -0.000202 + 1 * jax.random.normal(jax.random.fold_in(_gk, 1), (3125, 128), jnp.float32)
        _s = jax.random.randint(jax.random.fold_in(_gk, 2), (25000,), 0, 3125, jnp.int32)
        _d = jax.random.randint(jax.random.fold_in(_gk, 3), (25000,), 0, 3125, jnp.int32)
        _loop = jnp.arange(3125, dtype=jnp.int32)
        src = jnp.concatenate([_s, _d, _loop])
        dst = jnp.concatenate([_d, _s, _loop])
        _o = jnp.argsort(dst, stable=True)
        src = src[_o]
        dst = dst[_o]
        edge_type_4 = jax.random.randint(jax.random.fold_in(_gk, 13), (53125,), 0, 4, jnp.int32)
        edge_weight = jax.random.uniform(jax.random.fold_in(_gk, 14), (53125,), jnp.float32, 0.0, 1)
        return (x, src, dst, edge_type_4, edge_weight)
    x, src, dst, edge_type_4, edge_weight = _rec_inputs()

    def _L0_gnn_setup():
        import jax, jax.numpy as jnp
        import numpy as np
        N, E, D, H, HD, L = (50000, 25000, 128, 4, 32, 5)

        def _layernorm(x, g, b):
            mu = jnp.mean(x, axis=-1, keepdims=True)
            var = jnp.mean(jnp.square(x - mu), axis=-1, keepdims=True)
            return (x - mu) * jax.lax.rsqrt(var + 1e-05) * g + b

        def _conv(x, src, dst, Wq, bq, Wk, bk, Wv, bv, Ws, bs):
            n = x.shape[0]
            q = (x @ Wq + bq).reshape(n, H, HD)
            k = (x @ Wk + bk).reshape(n, H, HD)
            v = (x @ Wv + bv).reshape(n, H, HD)
            alpha = jnp.sum(q[dst] * k[src], axis=-1) / jnp.sqrt(jnp.float32(HD))
            amax = jax.ops.segment_max(alpha, dst, num_segments=n)
            ex = jnp.exp(alpha - amax[dst])
            denom = jax.ops.segment_sum(ex, dst, num_segments=n)
            attn = ex / (denom[dst] + 1e-16)
            msg = v[src] * attn[:, :, None]
            out = jax.ops.segment_sum(msg, dst, num_segments=n).reshape(n, H * HD)
            return out + x @ Ws + bs
        key = jax.random.key(seed)
        ks = jax.random.split(key, 8)
        w = 0.05
        return {'x': jax.random.normal(ks[0], (N, D), jnp.float32), 'edge_index': jax.random.randint(ks[1], (2, E), 0, N, jnp.int64), 'Wq': jax.random.normal(ks[2], (L, D, D), jnp.float32) * w, 'bq': jnp.zeros((L, D), jnp.float32), 'Wk': jax.random.normal(ks[3], (L, D, D), jnp.float32) * w, 'bk': jnp.zeros((L, D), jnp.float32), 'Wv': jax.random.normal(ks[4], (L, D, D), jnp.float32) * w, 'bv': jnp.zeros((L, D), jnp.float32), 'Ws': jax.random.normal(ks[5], (L, D, D), jnp.float32) * w, 'bs': jnp.zeros((L, D), jnp.float32), 'ln_g': jnp.ones((4, D), jnp.float32), 'ln_b': jnp.zeros((4, D), jnp.float32)}
    _L0_gnn_all = _L0_gnn_setup()
    _L0_gnn_in = {k: v for k, v in _L0_gnn_all.items() if k in ('Wq', 'bq', 'Wk', 'bk', 'Wv', 'bv', 'Ws', 'bs', 'ln_g', 'ln_b')}
    del _L0_gnn_all

    def _L1_gnn_setup():
        import jax, jax.numpy as jnp
        import numpy as np
        N_NODES = 3125
        N_EDGES = 18750
        N_REL = 4
        N_HEADS = 4
        DIM = 128
        HEAD_DIM = DIM // N_HEADS
        NEG_SLOPE = 0.2
        key = jax.random.key(seed)
        k1, k2, k3, k4, k5 = jax.random.split(key, 5)
        x = jax.random.normal(k1, (N_NODES, DIM), dtype=jnp.float32)
        edge_index = jax.random.randint(k2, (2, N_EDGES), 0, N_NODES, dtype=jnp.int64)
        edge_types = jax.random.randint(k3, (N_EDGES,), 0, N_REL, dtype=jnp.int64)
        W = jax.random.normal(k4, (N_REL, DIM, DIM), dtype=jnp.float32) * (1.0 / np.sqrt(DIM))
        attn = jax.random.normal(k5, (N_REL, N_HEADS, 2 * HEAD_DIM), dtype=jnp.float32) * 0.1
        return {'x': x, 'edge_index': edge_index, 'edge_types': edge_types, 'W': W, 'attn': attn}
    _L1_gnn_all = _L1_gnn_setup()
    _L1_gnn_in = {k: v for k, v in _L1_gnn_all.items() if k in ('W', 'attn')}
    del _L1_gnn_all

    def _L2_gnn_setup():
        import jax, jax.numpy as jnp
        import numpy as np
        N_NODES, N_EDGES, DIM = (3125, 50000, 128)

        def _gcn_norm(edge_index, n_nodes):
            loop = jnp.arange(n_nodes, dtype=edge_index.dtype)
            src = jnp.concatenate([edge_index[0], loop])
            dst = jnp.concatenate([edge_index[1], loop])
            deg = jax.ops.segment_sum(jnp.ones_like(src, jnp.float32), dst, num_segments=n_nodes)
            dinv = jnp.where(deg > 0, jax.lax.rsqrt(deg), 0.0)
            norm = dinv[src] * dinv[dst]
            return (src, dst, norm)

        def _gcn_layer(h, src, dst, norm, W, b, n_nodes):
            h = h @ W
            msg = h[src] * norm[:, None]
            out = jax.ops.segment_sum(msg, dst, num_segments=n_nodes)
            return out + b
        key = jax.random.key(seed)
        ks = jax.random.split(key, 4)
        s = 1.0 / np.sqrt(DIM)
        x = jax.random.normal(ks[0], (N_NODES, DIM), jnp.float32)
        edge_index = jax.random.randint(ks[1], (2, N_EDGES), 0, N_NODES, jnp.int32)
        W1 = jax.random.normal(ks[2], (DIM, DIM), jnp.float32) * s
        b1 = jnp.zeros((DIM,), jnp.float32)
        W2 = jax.random.normal(ks[3], (DIM, DIM), jnp.float32) * s
        b2 = jnp.zeros((DIM,), jnp.float32)
        return {'x': x, 'edge_index': edge_index, 'W1': W1, 'b1': b1, 'W2': W2, 'b2': b2}
    _L2_gnn_all = _L2_gnn_setup()
    _L2_gnn_in = {k: v for k, v in _L2_gnn_all.items() if k in ('W1', 'b1', 'W2', 'b2')}
    del _L2_gnn_all

    def _L3_gnn_setup():
        import jax, jax.numpy as jnp
        import numpy as np
        N_NODES = 3125
        N_EDGES = 50000
        D_IN = 128
        D_OUT = 128
        NEG_SLOPE = 0.01
        key = jax.random.key(seed)
        k1, k2, k3, k4, k5, k6 = jax.random.split(key, 6)
        stdv = 1.0 / np.sqrt(D_OUT)
        return {'node_features': jax.random.normal(k1, (N_NODES, D_IN), dtype=jnp.float32), 'edge_row': jax.random.randint(k2, (N_EDGES,), 0, N_NODES), 'edge_col': jax.random.randint(k3, (N_EDGES,), 0, N_NODES), 'edge_val': jax.random.uniform(k4, (N_EDGES,), dtype=jnp.float32), 'weight': jax.random.uniform(k5, (D_IN, D_OUT), dtype=jnp.float32, minval=-stdv, maxval=stdv), 'bias': jax.random.uniform(k6, (D_OUT,), dtype=jnp.float32, minval=-stdv, maxval=stdv)}
    _L3_gnn_all = _L3_gnn_setup()
    _L3_gnn_in = {k: v for k, v in _L3_gnn_all.items() if k in ('weight', 'bias')}
    del _L3_gnn_all
    return {'x': x, 'src': src, 'dst': dst, 'edge_type_4': edge_type_4, 'edge_weight': edge_weight, 'L0_gnn_Wq': _L0_gnn_in['Wq'], 'L0_gnn_bq': _L0_gnn_in['bq'], 'L0_gnn_Wk': _L0_gnn_in['Wk'], 'L0_gnn_bk': _L0_gnn_in['bk'], 'L0_gnn_Wv': _L0_gnn_in['Wv'], 'L0_gnn_bv': _L0_gnn_in['bv'], 'L0_gnn_Ws': _L0_gnn_in['Ws'], 'L0_gnn_bs': _L0_gnn_in['bs'], 'L0_gnn_ln_g': _L0_gnn_in['ln_g'], 'L0_gnn_ln_b': _L0_gnn_in['ln_b'], 'L1_gnn_W': _L1_gnn_in['W'], 'L1_gnn_attn': _L1_gnn_in['attn'], 'L2_gnn_W1': _L2_gnn_in['W1'], 'L2_gnn_b1': _L2_gnn_in['b1'], 'L2_gnn_W2': _L2_gnn_in['W2'], 'L2_gnn_b2': _L2_gnn_in['b2'], 'L3_gnn_weight': _L3_gnn_in['weight'], 'L3_gnn_bias': _L3_gnn_in['bias']}

def reference(x, src, dst, edge_type_4, edge_weight, L0_gnn_Wq, L0_gnn_bq, L0_gnn_Wk, L0_gnn_bk, L0_gnn_Wv, L0_gnn_bv, L0_gnn_Ws, L0_gnn_bs, L0_gnn_ln_g, L0_gnn_ln_b, L1_gnn_W, L1_gnn_attn, L2_gnn_W1, L2_gnn_b1, L2_gnn_W2, L2_gnn_b2, L3_gnn_weight, L3_gnn_bias):
    import jax
    import jax.numpy as jnp

    def _L0_gnn_ref(x, edge_index, Wq, bq, Wk, bk, Wv, bv, Ws, bs, ln_g, ln_b):
        import jax, jax.numpy as jnp
        import numpy as np
        N, E, D, H, HD, L = (50000, 25000, 128, 4, 32, 5)

        def _layernorm(x, g, b):
            mu = jnp.mean(x, axis=-1, keepdims=True)
            var = jnp.mean(jnp.square(x - mu), axis=-1, keepdims=True)
            return (x - mu) * jax.lax.rsqrt(var + 1e-05) * g + b

        def _conv(x, src, dst, Wq, bq, Wk, bk, Wv, bv, Ws, bs):
            n = x.shape[0]
            q = (x @ Wq + bq).reshape(n, H, HD)
            k = (x @ Wk + bk).reshape(n, H, HD)
            v = (x @ Wv + bv).reshape(n, H, HD)
            alpha = jnp.sum(q[dst] * k[src], axis=-1) / jnp.sqrt(jnp.float32(HD))
            amax = jax.ops.segment_max(alpha, dst, num_segments=n)
            ex = jnp.exp(alpha - amax[dst])
            denom = jax.ops.segment_sum(ex, dst, num_segments=n)
            attn = ex / (denom[dst] + 1e-16)
            msg = v[src] * attn[:, :, None]
            out = jax.ops.segment_sum(msg, dst, num_segments=n).reshape(n, H * HD)
            return out + x @ Ws + bs
        src, dst = (edge_index[0], edge_index[1])
        gelu = lambda t: jax.nn.gelu(t, approximate=False)
        res = x
        h = _conv(x, src, dst, Wq[0], bq[0], Wk[0], bk[0], Wv[0], bv[0], Ws[0], bs[0])
        h = gelu(_layernorm(h, ln_g[0], ln_b[0])) + res
        for i in range(1, 4):
            res = h
            h = _conv(h, src, dst, Wq[i], bq[i], Wk[i], bk[i], Wv[i], bv[i], Ws[i], bs[i])
            h = gelu(_layernorm(h, ln_g[i], ln_b[i])) + res
        h = _conv(h, src, dst, Wq[4], bq[4], Wk[4], bk[4], Wv[4], bv[4], Ws[4], bs[4])
        return gelu(h)

    def _L1_gnn_ref(x, edge_index, edge_types, W, attn):
        import jax, jax.numpy as jnp
        import numpy as np
        N_NODES = 3125
        N_EDGES = 18750
        N_REL = 4
        N_HEADS = 4
        DIM = 128
        HEAD_DIM = DIM // N_HEADS
        NEG_SLOPE = 0.2
        N = x.shape[0]
        R, H, twoD = attn.shape
        D = twoD // 2
        E = edge_types.shape[0]
        x_rel = jnp.einsum('ni,rio->rno', x, W).reshape(R, N, H, D)
        src, dst = (edge_index[0], edge_index[1])
        src_feat = x_rel[edge_types, src]
        dst_feat = x_rel[edge_types, dst]
        a = attn[edge_types]
        cat = jnp.concatenate([src_feat, dst_feat], axis=-1)
        alpha = jnp.sum(cat * a, axis=-1)
        alpha = jnp.where(alpha > 0, alpha, NEG_SLOPE * alpha)
        seg = edge_types * N + dst
        S = R * N
        m = jax.ops.segment_max(alpha, seg, num_segments=S)
        alpha_exp = jnp.exp(alpha - m[seg])
        denom = jax.ops.segment_sum(alpha_exp, seg, num_segments=S)
        w = alpha_exp / denom[seg]
        msg = (src_feat * w[..., None]).reshape(E, H * D)
        out = jax.ops.segment_sum(msg, dst, num_segments=N)
        return out

    def _L2_gnn_ref(x, edge_index, W1, b1, W2, b2):
        import jax, jax.numpy as jnp
        import numpy as np
        N_NODES, N_EDGES, DIM = (3125, 50000, 128)

        def _gcn_norm(edge_index, n_nodes):
            loop = jnp.arange(n_nodes, dtype=edge_index.dtype)
            src = jnp.concatenate([edge_index[0], loop])
            dst = jnp.concatenate([edge_index[1], loop])
            deg = jax.ops.segment_sum(jnp.ones_like(src, jnp.float32), dst, num_segments=n_nodes)
            dinv = jnp.where(deg > 0, jax.lax.rsqrt(deg), 0.0)
            norm = dinv[src] * dinv[dst]
            return (src, dst, norm)

        def _gcn_layer(h, src, dst, norm, W, b, n_nodes):
            h = h @ W
            msg = h[src] * norm[:, None]
            out = jax.ops.segment_sum(msg, dst, num_segments=n_nodes)
            return out + b
        n = x.shape[0]
        src, dst, norm = _gcn_norm(edge_index, n)
        h = jax.nn.elu(_gcn_layer(x, src, dst, norm, W1, b1, n))
        return _gcn_layer(h, src, dst, norm, W2, b2, n)

    def _L3_gnn_ref(node_features, edge_row, edge_col, edge_val, weight, bias):
        import jax, jax.numpy as jnp
        import numpy as np
        N_NODES = 3125
        N_EDGES = 50000
        D_IN = 128
        D_OUT = 128
        NEG_SLOPE = 0.01
        h = node_features @ weight
        msg = edge_val[:, None] * h[edge_col]
        out = jax.ops.segment_sum(msg, edge_row, num_segments=node_features.shape[0])
        out = out + bias
        out = jnp.where(out >= 0, out, NEG_SLOPE * out)
        return out
    edge_index = jnp.stack([src, dst])
    x = _layernorm(x + _L0_gnn_ref(x, edge_index, L0_gnn_Wq, L0_gnn_bq, L0_gnn_Wk, L0_gnn_bk, L0_gnn_Wv, L0_gnn_bv, L0_gnn_Ws, L0_gnn_bs, L0_gnn_ln_g, L0_gnn_ln_b), axis=-1)
    x = _layernorm(x + _L1_gnn_ref(x, edge_index, edge_type_4, L1_gnn_W, L1_gnn_attn), axis=-1)
    x = _layernorm(x + _L2_gnn_ref(x, edge_index, L2_gnn_W1, L2_gnn_b1, L2_gnn_W2, L2_gnn_b2), axis=-1)
    x = _layernorm(x + _L3_gnn_ref(x, src, dst, edge_weight, L3_gnn_weight, L3_gnn_bias), axis=-1)
    return x

_drawn_inputs = setup_inputs


def setup_inputs(seed=0):
    import zlib

    import numpy as np

    out = dict(_drawn_inputs(seed))
    spreads = {'L0_gnn_bq': (0.0, 0.616),
     'L0_gnn_bk': (0.0, 0.8),
     'L0_gnn_bv': (0.0, 0.1),
     'L0_gnn_bs': (0.0, 0.1),
     'L0_gnn_ln_g': (1.0, 0.2),
     'L0_gnn_ln_b': (0.0, 0.1),
     'L2_gnn_b1': (0.0, 0.1),
     'L2_gnn_b2': (0.0, 0.1)}
    factors = {'L3_gnn_bias': 2.838}
    for name, (base, spread) in spreads.items():
        noise = np.random.default_rng([zlib.crc32(name.encode()), seed]).standard_normal(out[name].shape)
        drawn = base * np.exp(spread * noise) if base else spread * noise
        out[name] = jnp.asarray(drawn.astype(out[name].dtype))
    for name, factor in factors.items():
        out[name] = (out[name] * factor).astype(out[name].dtype)
    return out
```

```python
import concourse.bass as bass
from concourse import mybir
from contextlib import ExitStack

NEG = -1.0e30
P = 128
N = 3125
D = 128
H = 4
HD = D // H
R = 4
CONVS = 5
EDGES = 53125
TG = 32
QG = TG // 4
GROUPS = -(-EDGES // (P * TG))
T = GROUPS * TG
BW = 512
NB = -(-(N + P) // BW)
NPAD = NB * BW
ROW = H * (TG + 1)
RW = D + 2 * H
NT = NPAD // P
SCALE = 1.0 / float(HD) ** 0.5
EPS = 1.0e-5


def gnn_kernel(nc, xT_in, src_c, src_row, dst_c, dst_row, prev_row, next_row, first_row, first_next, last_row,
               last_prev, type_c, type_r, ew_c, w0, b0, col0, w1, w1T, a1, w2, b2, w3, b3, out):
    f32, i32, bf16 = mybir.dt.float32, mybir.dt.int32, mybir.dt.bfloat16
    ALU, ACT, AX = mybir.AluOpType, mybir.ActivationFunctionType, mybir.AxisListType
    ds = bass.ds

    kv_tab = nc.dram_tensor("kv_tab", [NPAD, 2 * D], f32).ap()
    q_tab = nc.dram_tensor("q_tab", [NPAD, D], f32).ap()
    rel_tab = nc.dram_tensor("rel_tab", [R * NPAD, RW], f32).ap()
    adst_tab = nc.dram_tensor("adst_tab", [NPAD, R * H], f32).ap()
    h_tab = nc.dram_tensor("h_tab", [NPAD, D], f32).ap()

    sum_tab = [nc.dram_tensor(f"sum_tab{k}", [NPAD + P, D], f32).ap() for k in range(8)]

    root = ExitStack()
    sems = {}

    def sem(name):
        if name not in sems:
            sems[name] = nc.alloc_semaphore(name)
        return sems[name]

    def recycle():
        kept = [n for n in sems if n.startswith(("rows", "settled"))]
        nc.clear_and_free_semaphores([s for n, s in sems.items() if n not in kept])
        for n in list(sems):
            if n not in kept:
                del sems[n]
        with nc.Block():
            pass

    def settle(eng):
        eng.sem_inc(sem(f"settled_{eng.engine.name}"), 1)

    def bases(eng, first):
        _, v = nc.values_load_multi_w_load_instructions(
            base_i[0:1, ds(first, 4)], engines=[eng.engine], min_val=0, max_val=N,
            skip_runtime_bounds_check_because="a destination is at most N, the one of the padding")
        return v

    with root:
        def gsb(name, shape, dt=f32):
            return root.enter_context(nc.sbuf_tensor(name, shape, dt))

        xT = gsb("xT", [P, NPAD])
        src_all = gsb("src_all", [P, T], i32)
        base_i = gsb("base_i", [1, T], i32)
        rel = gsb("rel", [P, T])
        iota_row = gsb("iota_row", [P, P])
        ident = gsb("ident", [P, P])
        ones = gsb("ones", [P, P])
        mean_w = gsb("mean_w", [P, P])
        head_sel = gsb("head_sel", [P, P])
        eps_col = gsb("eps_col", [P, 1])
        rstF = gsb("rstF", [P, GROUPS * P], bf16)
        rstB = gsb("rstB", [P, GROUPS * P], bf16)
        rowrF = gsb("rowrF", [R, GROUPS * H * (TG + 1)], bf16)
        rowrB = gsb("rowrB", [R, GROUPS * H * (TG + 1)], bf16)

        with ExitStack() as scope:
            def sb(name, shape, dt=f32):
                return scope.enter_context(nc.sbuf_tensor(name, shape, dt))

            dst_ci = sb("dst_ci", [P, T], i32)
            first_b = sb("first_b", [P, T], i32)
            dst_f = sb("dst_f", [P, T])
            first_f = sb("first_f", [P, T])
            seg_i = sb("seg_i", [P, 3, GROUPS * P], i32)
            seg_f = sb("seg_f", [P, 3, GROUPS * P])
            edge_i = sb("edge_i", [R, 4, T], i32)
            edge_f = sb("edge_f", [R, 4, T])
            iota_i = sb("iota_i", [P, P], i32)
            part_i = sb("part_i", [P, P], i32)
            part_f = sb("part_f", [P, P])
            in_sem = sem("setup_in")
            iota_done = sem("setup_iota")
            ch = sem("setup_chain")
            with nc.Block() as block:
                @block.sync
                def _(sp):
                    sp.dma_start(xT[:, :], xT_in).then_inc(in_sem, 16)
                    sp.dma_start(src_all[:, :], src_c).then_inc(in_sem, 16)
                    sp.dma_start(dst_ci[:, :], dst_c).then_inc(in_sem, 16)
                    sp.dma_start(base_i[:, :], first_row).then_inc(in_sem, 16)
                    sp.dma_start(first_b[:, :], first_row.to_broadcast([P, T])).then_inc(in_sem, 16)
                    for h in range(H):
                        for k, rows in enumerate((dst_row, prev_row, next_row)):
                            sp.dma_start(seg_i[h * TG:(h + 1) * TG, k, :], rows).then_inc(in_sem, 16)
                    for k, row in enumerate((first_row, first_next, last_row, last_prev)):
                        sp.dma_start(edge_i[:, k, :], row.to_broadcast([R, T])).then_inc(in_sem, 16)

                @block.gpsimd
                def _(pool):
                    nc.gpsimd.iota(iota_i[:, :], pattern=[[1, P]], base=0, channel_multiplier=0)
                    nc.gpsimd.iota(part_i[:, :], pattern=[[0, P]], base=0,
                                   channel_multiplier=1).then_inc(iota_done, 1)

                @block.vector
                def _(dve):
                    v = nc.vector
                    n = [0]

                    def link(ins):
                        n[0] += 1
                        ins.then_inc(ch, 1)
                        dve.wait_ge(ch, n[0])

                    v.memset(ones[:, :], 1.0)
                    v.memset(mean_w[:, :], 1.0 / D)
                    v.memset(eps_col[:, :], EPS)
                    v.memset(rowrF[:, :], NEG)
                    link(v.memset(rowrB[:, :], NEG))
                    dve.wait_ge(iota_done, 1)
                    v.tensor_copy(iota_row[:, :], iota_i[:, :])
                    link(v.tensor_copy(part_f[:, :], part_i[:, :]))
                    link(v.tensor_tensor(ident[:, :], iota_row[:, :], part_f[:, :], ALU.is_equal))
                    for h in range(H):
                        last = v.tensor_scalar(head_sel[:, h * HD:(h + 1) * HD], part_f[:, 0:HD], float(h * TG),
                                               None, ALU.is_equal)
                    link(last)
                    dve.wait_ge(in_sem, 16 * (5 + 3 * H + 4))
                    v.tensor_copy(dst_f[:, :], dst_ci[:, :])
                    v.tensor_copy(seg_f[:, :, :], seg_i[:, :, :])
                    v.tensor_copy(edge_f[:, :, :], edge_i[:, :, :])
                    link(v.tensor_copy(first_f[:, :], first_b[:, :]))
                    link(v.tensor_tensor(rel[:, :], dst_f[:, :], first_f[:, :], ALU.subtract))
                    def blocks(t, n):
                        return t.rearrange("p (g e) -> p g e", e=n)

                    for o, k in ((blocks(rstF[:, :], P), 1), (blocks(rstB[:, :], P)[:, :, ::-1], 2)):
                        link(v.tensor_tensor(o, blocks(seg_f[:, 0, :], P), blocks(seg_f[:, k, :], P), ALU.not_equal))
                    for o in (rstF, rstB):
                        link(v.tensor_scalar(o[:, :], o[:, :], NEG, None, ALU.mult))
                    for o, a, b in ((blocks(rowrF[:, :], ROW), 2, 3), (blocks(rowrB[:, :], ROW)[:, :, ::-1], 0, 1)):
                        for h in range(H):
                            at = h * (TG + 1) + (1 if a == 2 else 0)
                            link(v.tensor_tensor(o[:, :, at:at + TG], blocks(edge_f[:, a, :], TG),
                                                 blocks(edge_f[:, b, :], TG), ALU.not_equal))
                            link(v.tensor_scalar(o[:, :, at:at + TG], o[:, :, at:at + TG], NEG, None, ALU.mult))

        def softmax_buffers(sb, C):
            return dict(C=C, L=sb("sm_L", [P, P]), Lc=sb("sm_Lc", [P, C, P] if C > 1 else [P, 1]),
                        pen=sb("sm_pen", [P, C, P] if C > 1 else [P, 1]), F=sb("sm_F", [P, C, P]),
                        B=sb("sm_B", [P, C, P]), rowF=sb("sm_rowF", [C, H, TG + 1]),
                        rowB=sb("sm_rowB", [C, H, TG + 1]), CF=sb("sm_CF", [C, H, TG + 1]),
                        CB=sb("sm_CB", [C, H, TG + 1]), ini_row=sb("sm_ini_row", [C, 2, P]),
                        ini=sb("sm_ini", [P, 2, C]), m=sb("sm_m", [P, P]), d=sb("sm_d", [P, P]),
                        df=sb("sm_df", [P, C]), f=sb("sm_f", [P, C]), alpha=sb("alpha", [P, H, TG]),
                        exE=sb("exE", [P, 2, H, TG]))

        CHAIN = {1: 9, R: 14}

        def softmax_vector(dve, b, tag, g, G, pM, pen):
            v, C = nc.vector, b["C"]
            n = [0]
            ch = sem(tag + "sm_chain")

            def link(ins):
                n[0] += 1
                ins.then_inc(ch, 1)
                dve.wait_ge(ch, G * CHAIN[C] + n[0])

            L, F, B = b["L"], b["F"], b["B"]
            dve.wait_ge(sem(tag + "L_ready"), G + 1)
            if C > 1:
                for c in range(C):
                    last = v.tensor_scalar(b["pen"][:, c, :], pen[:, ds(g * P, P)], float(c), NEG, ALU.not_equal, ALU.mult)
                link(last)
                link(v.tensor_tensor(b["Lc"][:, :, :], b["pen"][:, :, :],
                                     L[:, :].unsqueeze(1).to_broadcast([P, C, P]), ALU.add))
            for c in range(C):
                data = b["Lc"][:, c, :] if C > 1 else L[:, :]
                v.tensor_tensor_scan(out=F[:, c, :], data0=rstF[:, ds(g * P, P)], data1=data, initial=NEG,
                                     op0=ALU.add, op1=ALU.max)
                last = v.tensor_tensor_scan(out=B[:, c, ::-1], data0=rstB[:, ds(g * P, P)], data1=data[:, ::-1],
                                            initial=NEG, op0=ALU.add, op1=ALU.max)
            last.then_inc(sem(tag + "tails_ready"), 1)
            dve.wait_ge(sem(tag + "rows_ready"), G + 1)
            v.tensor_copy(b["rowF"][:, :, 1:TG + 1], pM[0:C, 128:256].rearrange("c (h t) -> c h t", h=H))
            link(v.tensor_copy(b["rowB"][:, :, 0:TG], pM[0:C, 256:384].rearrange("c (h t) -> c h t", h=H)))

            def flat(a):
                return a.rearrange("c h t -> c (h t)")

            v.tensor_tensor_scan(out=flat(b["CF"][:, :, :]), data0=rowrF[0:C, ds(g * ROW, ROW)],
                                 data1=flat(b["rowF"][:, :, :]), initial=NEG, op0=ALU.add, op1=ALU.max)
            link(v.tensor_tensor_scan(out=flat(b["CB"][:, :, :])[:, ::-1],
                                      data0=rowrB[0:C, ds(g * ROW, ROW)],
                                      data1=flat(b["rowB"][:, :, :])[:, ::-1], initial=NEG, op0=ALU.add, op1=ALU.max))
            v.tensor_copy(b["rowF"][:, :, 0:1], b["CF"][:, :, TG:TG + 1])
            v.tensor_copy(b["ini_row"][:, 0, :].rearrange("c (h t) -> c h t", h=H), b["CF"][:, :, 0:TG])
            link(v.tensor_copy(b["ini_row"][:, 1, :].rearrange("c (h t) -> c h t", h=H), b["CB"][:, :, 1:TG + 1]))
            dve.sem_inc(sem(tag + "ini_rows"), 1)
            dve.wait_ge(sem(tag + "ini_ready"), G + 1)
            link(v.tensor_copy(b["ini"][:, :, :], pM[:, 384:384 + 2 * C].rearrange("p (k c) -> p k c", k=2)))
            for c in range(C):
                data = b["Lc"][:, c, :] if C > 1 else L[:, :]
                v.tensor_tensor_scan(out=F[:, c, :], data0=rstF[:, ds(g * P, P)], data1=data,
                                     initial=b["ini"][:, 0, c:c + 1], op0=ALU.add, op1=ALU.max)
                last = v.tensor_tensor_scan(out=B[:, c, ::-1], data0=rstB[:, ds(g * P, P)], data1=data[:, ::-1],
                                            initial=b["ini"][:, 1, c:c + 1], op0=ALU.add, op1=ALU.max)
            link(last)
            link(v.tensor_tensor(F[:, :, :], F[:, :, :], B[:, :, :], ALU.max))
            link(v.tensor_tensor(b["df"][:, :], b["ini"][:, 0, :], F[:, :, 0:1].rearrange("p c o -> p (c o)"), ALU.subtract))
            link(v.tensor_scalar(b["df"][:, :], b["df"][:, :], 0.0, None, ALU.min))
            if C > 1:
                link(v.tensor_tensor(F[:, :, :], F[:, :, :], b["pen"][:, :, :], ALU.add))
                link(v.tensor_tensor(B[:, 0:2, :], F[:, 0:2, :], F[:, 2:4, :], ALU.max))
                link(v.tensor_tensor(b["m"][:, :], B[:, 0, :], B[:, 1, :], ALU.max))
                top = b["m"][:, :]
            else:
                top = F[:, 0, :]
            link(v.tensor_tensor(b["d"][:, :], L[:, :], top, ALU.subtract))
            dve.sem_inc(sem(tag + "d_ready"), 1)
            assert n[0] == CHAIN[C], (C, n[0])

        def softmax_tensor_1(pe, b, tag, G, pM):
            C = b["C"]
            pe.wait_ge(sem(tag + "alpha"), (G + 1) * QG)
            nc.tensor.transpose(pM[:, 0:128], b["alpha"][:, :, :].rearrange("p h t -> p (h t)"),
                                ident[:, :]).then_inc(sem(tag + "lt"), 1)
            pe.wait_ge(sem(tag + "tails_ready"), G + 1)
            nc.tensor.matmul(pM[0:C, 128:256], b["F"][:, :, P - 1], ident[:, :], start=True, stop=True)
            nc.tensor.matmul(pM[0:C, 256:384], b["B"][:, :, 0], ident[:, :], start=True,
                             stop=True).then_inc(sem(tag + "rows_ready"), 1)
            pe.wait_ge(sem(tag + "ini_rows"), G + 1)
            nc.tensor.matmul(pM[:, 384:384 + C], b["ini_row"][:, 0, :], ident[0:C, 0:C], start=True, stop=True)
            nc.tensor.matmul(pM[:, 384 + C:384 + 2 * C], b["ini_row"][:, 1, :], ident[0:C, 0:C], start=True,
                             stop=True).then_inc(sem(tag + "ini_ready"), 1)

        def softmax_scalar(act, b, tag, par, G, pM, pX, scale):
            a = nc.scalar
            act.wait_ge(sem(tag + "lt"), G + 1)
            a.activation(b["L"][:, :], pM[:, 0:128], ACT.Copy).then_inc(sem(tag + "L_ready"), 1)
            act.wait_ge(sem(tag + "d_ready"), G + 1)
            a.activation(b["f"][:, :], b["df"][:, :], ACT.Exp, scale=scale)
            a.activation(b["m"][:, :], b["d"][:, :], ACT.Exp, scale=scale).then_inc(sem(tag + "ex_ready"), 1)
            act.wait_ge(sem(tag + "ex_turned"), G + 1)
            a.activation(b["exE"][:, par, :, :], pX[:, 0:128].rearrange("p (h t) -> p h t", h=H),
                         ACT.Copy).then_inc(sem(tag + "exE"), 1)

        def turn_ex(pe, b, tag, G, pX):
            C = b["C"]
            pe.wait_ge(sem(tag + "ex_ready"), G + 1)
            nc.tensor.matmul(pX[:, 128:128 + C], head_sel[:, :], b["f"][:, :], start=True, stop=True)
            nc.tensor.transpose(pX[:, 0:128], b["m"][:, :], ident[:, :]).then_inc(sem(tag + "ex_turned"), 1)

        def gather_group(pool, tag, l, g, par, tab, idx_all, idx_now, rows, read="alpha", used="msg"):
            if isinstance(g, int) and g < 2:
                pass
            else:
                pool.wait_ge(sem(tag + read), (l * GROUPS + g - 1) * QG)
                settle(pool)
            nc.gpsimd.tensor_copy(idx_now[:, par, :], idx_all[:, ds(g * TG, TG)]).then_inc(sem(tag + "idx"), 1)
            pool.wait_ge(sem(tag + "idx"), l * GROUPS + g + 1)
            settle(pool)
            for q in range(QG):
                if not (isinstance(g, int) and g < 2):
                    pool.wait_ge(sem(tag + used), (l * GROUPS + g - 2) * QG + q + 1)
                    settle(pool)
                for j in range(4):
                    t = 4 * q + j
                    nc.gpsimd.indirect_dma_start(
                        rows[:, par * TG + t, :], None, tab,
                        bass.IndirectOffsetOnAxis(ap=idx_now[:, par, t:t + 1], axis=0)
                    ).then_inc(sem(f"rows{par}_{q}"), 16)

        def take_group(dve, tag, l, g, pairs):
            for now, whole, per in pairs:
                last = nc.vector.tensor_copy(now, whole[:, ds(g * (TG * per), TG * per)])
            last.then_inc(sem(tag + "taken"), 1)
            dve.wait_ge(sem(tag + "taken"), l * GROUPS + g + 1)
            settle(dve)

        def rows_there(eng, turn, half, par, q):
            eng.wait_ge(sem(f"rows{par}_{q}"), 64 * (turn * ((GROUPS + 1) // 2 - par) + half + 1))

        def gather_all(pool, group):
            group(0, 0)
            group(1, 1)
            with pool.Fori(0, (GROUPS - 3) // 2) as k:
                group(2 * k + 2, 0)
                group(2 * k + 3, 1)
            group(GROUPS - 1, 0)

        def conv_project(l, sb, pb):
            w = sb("w", [P, 4 * D])
            brow = sb("brow", [1, 3 * D])
            stage = sb("stage", [P, 2, 4, 3 * D])
            pp = [pb(f"pp{i}", [P, 512]) for i in range(4)]
            loaded, prod, copied = sem("proj_w"), sem("proj_prod"), sem("proj_copied")
            stored = [sem("proj_stored0"), sem("proj_stored1")]
            nt = NPAD // P
            even, odd = (NB + 1) // 2, NB // 2
            with nc.Block() as block:
                @block.sync
                def _(sp):
                    sp.dma_start(w[:, :], w0[ds(l, 1), :, :].rearrange("l p n -> (l p) n")).then_inc(loaded, 16)
                    sp.dma_start(brow[:, :], b0[ds(l, 1), :]).then_inc(loaded, 16)
                    for b in range(NB):
                        sp.wait_ge(copied, l * nt + 4 * (b + 1))
                        rows = slice(b * BW, (b + 1) * BW)
                        sp.dma_start(kv_tab[rows, :].rearrange("(j p) f -> p j f", p=P),
                                     stage[:, b % 2, :, 0:2 * D]).then_inc(stored[b % 2], 16)
                        sp.dma_start(q_tab[rows, :].rearrange("(j p) f -> p j f", p=P),
                                     stage[:, b % 2, :, 2 * D:3 * D]).then_inc(stored[b % 2], 16)
                    sp.wait_ge(stored[0], (l + 1) * 32 * even)
                    settle(sp)
                    sp.wait_ge(stored[1], (l + 1) * 32 * odd)
                    settle(sp)

                @block.tensor
                def _(pe):
                    pe.wait_ge(loaded, 32 * (l + 1))
                    for t in range(nt):
                        if t >= 4:
                            pe.wait_ge(copied, l * nt + t - 3)
                        nc.tensor.matmul(pp[t % 4][:, 0:3 * D], xT[:, t * P:(t + 1) * P], w[:, 0:3 * D],
                                         start=True, stop=False)
                        nc.tensor.matmul(pp[t % 4][:, 0:3 * D], ones[0:1, :], brow[:, :], start=False,
                                         stop=True).then_inc(prod, 1)

                @block.scalar
                def _(act):
                    for t in range(nt):
                        b = t // 4
                        if t % 4 == 0 and b >= 2:
                            n = even if b % 2 == 0 else odd
                            act.wait_ge(stored[b % 2], l * 32 * n + 32 * (b // 2))
                        act.wait_ge(prod, l * nt + t + 1)
                        nc.scalar.activation(stage[:, b % 2, t % 4, :], pp[t % 4][:, 0:3 * D],
                                             ACT.Copy).then_inc(copied, 1)
            return w

        def conv_edges(l, sb, pb, acc):
            tag = "c_"
            kv = sb("kv", [P, 2 * TG, 2 * D])
            S = sb("S", [P, 2 * TG, P])
            ST = sb("ST", [P, 2, 4, P])
            qwin = sb("qwin", [P, 2, 4, D])
            prodb = sb("prodb", [P, 4, D])
            exb = sb("exb", [P, 2, 4, D])
            msg = sb("msg", [P, 2, 4, D])
            idx_now = sb("idx_now", [P, 2, TG], i32)
            rel_now = sb("rel_now", [P, TG])
            sm = softmax_buffers(sb, 1)
            pT = [pb(f"pT{i}", [P, 4, P]) for i in range(2)]
            pQ = [pb(f"pQ{i}", [P, 4, D]) for i in range(2)]
            pA = [pb(f"pA{i}", [P, 2, 2, P]) for i in range(2)]
            pM = pb("pM", [P, 512])
            pX = pb("pX", [P, 512])

            def quad(g, q):
                return (l * GROUPS + g) * QG + q

            def skip(g):
                return isinstance(g, int) and g == 0

            with nc.Block() as block:
                @block.gpsimd
                def _(pool):
                    gather_all(pool, lambda g, par: gather_group(pool, tag, l, g, par, kv_tab, src_all, idx_now, kv))

                @block.sync
                def _(sp):
                    def group(g, par):
                        for q in range(QG):
                            n = quad(g, q)
                            at = bases(sp, g * TG + 4 * q)
                            if not (skip(g) and q < 2):
                                sp.wait_ge(sem(tag + "qx"), n - 1)
                                settle(sp)
                            for j in range(4):
                                sp.dma_start(qwin[:, q % 2, j, :], q_tab[ds(at[j], P), :]
                                             ).then_inc(sem(f"{tag}qwin{q % 2}"), 16)
                    group(0, 0)
                    with sp.Fori(1, GROUPS) as g:
                        group(g, None)

                @block.tensor
                def _(pe):
                    def scores_turn(g, q, par):
                        n = quad(g, q)
                        pe.wait_ge(sem(tag + "S"), n + 1)
                        if not (skip(g) and q < 2):
                            pe.wait_ge(sem(tag + "ST"), n - 1)
                        for j in range(4):
                            last = nc.tensor.transpose(pT[q % 2][:, j, :], S[:, par * TG + 4 * q + j, :], ident[:, :])
                        last.then_inc(sem(tag + "turned"), 1)

                    def scores(g, q):
                        n = quad(g, q)
                        pe.wait_ge(sem(tag + "ST"), n + 1)
                        pe.wait_ge(sem(f"{tag}qwin{q % 2}"), 64 * ((l * GROUPS + g) * (QG // 2) + q // 2 + 1))
                        if not (skip(g) and q < 2):
                            pe.wait_ge(sem(tag + "prod"), n - 1)
                        for j in range(4):
                            last = nc.tensor.matmul(pQ[q % 2][:, j, :], ST[:, q % 2, j, :], qwin[:, q % 2, j, :],
                                                    start=True, stop=True)
                        last.then_inc(sem(tag + "qx"), 1)

                    def sums(g, q, par):
                        m = quad(g, q)
                        pe.wait_ge(sem(tag + "msg"), m + 1)
                        for u in range(2):
                            if not (skip(g) and q == 0):
                                pe.wait_ge(sem(tag + "acc"), 4 * m - 2 + 2 * u)
                            for k in range(2):
                                j = 2 * u + k
                                s = S[:, par * TG + 4 * q + j, :]
                                nc.tensor.matmul(pA[u][:, k, 0, :], msg[:, q % 2, j, :], s, start=True, stop=True)
                                last = nc.tensor.matmul(pA[u][:, k, 1, :], exb[:, q % 2, j, :], s, start=True, stop=True)
                            last.then_inc(sem(tag + "agg"), 1)

                    def group(g, par):
                        for q in range(QG):
                            scores_turn(g, q, par)
                            if not skip(g):
                                sums(g - 1, q, 1 - par)
                            scores(g, q)
                        softmax_tensor_1(pe, sm, tag, l * GROUPS + g, pM)
                        turn_ex(pe, sm, tag, l * GROUPS + g, pX)
                    group(0, 0)
                    group(1, 1)
                    group(2, 0)
                    with pe.Fori(1, (GROUPS - 1) // 2) as k:
                        group(2 * k + 1, 1)
                        group(2 * k + 2, 0)
                    for q in range(QG):
                        sums(GROUPS - 1, q, 0)

                @block.scalar
                def _(act):
                    def st_copy(g, q):
                        n = quad(g, q)
                        act.wait_ge(sem(tag + "turned"), n + 1)
                        if not (skip(g) and q < 2):
                            act.wait_ge(sem(tag + "qx"), n - 1)
                        nc.scalar.activation(ST[:, q % 2, :, :], pT[q % 2][:, :, :], ACT.Copy
                                             ).then_inc(sem(tag + "ST"), 1)

                    def spread(g, q, par):
                        m = quad(g, q)
                        if q == 0:
                            act.wait_ge(sem(tag + "exE"), l * GROUPS + g + 1)
                        if not (skip(g) and q < 2):
                            act.wait_ge(sem(tag + "agg"), 2 * (m - 1))
                        src = sm["exE"][:, par, :, 4 * q:4 * q + 4].rearrange("p h t -> p t h")
                        nc.scalar.activation(exb[:, q % 2, :, :].rearrange("p t (h f) -> p t h f", h=H),
                                             src.unsqueeze(3).to_broadcast([P, 4, H, HD]), ACT.Copy
                                             ).then_inc(sem(tag + "exb"), 1)

                    def group(g, par):
                        for q in range(QG):
                            if not skip(g):
                                spread(g - 1, q, 1 - par)
                            st_copy(g, q)
                        softmax_scalar(act, sm, tag, par, l * GROUPS + g, pM, pX, SCALE)
                    group(0, 0)
                    group(1, 1)
                    group(2, 0)
                    with act.Fori(1, (GROUPS - 1) // 2) as k:
                        group(2 * k + 1, 1)
                        group(2 * k + 2, 0)
                    for q in range(QG):
                        spread(GROUPS - 1, q, 0)

                @block.vector
                def _(dve):
                    v = nc.vector

                    def build(g, q, par):
                        if not (isinstance(g, int) and g < 2):
                            dve.wait_ge(sem(tag + "agg"), 2 * (quad(g, q) - 2 * QG + 1))
                        for j in range(4):
                            last = v.tensor_scalar(S[:, par * TG + 4 * q + j, :], iota_row[:, :],
                                                   rel_now[:, 4 * q + j:4 * q + j + 1], None, ALU.is_equal)
                        last.then_inc(sem(tag + "S"), 1)

                    def weigh(g, q, par):
                        m = quad(g, q)
                        dve.wait_ge(sem(tag + "exb"), m + 1)
                        if not (skip(g) and q < 2):
                            dve.wait_ge(sem(tag + "agg"), 2 * (m - 1))
                        s = par * TG + 4 * q
                        v.tensor_tensor(msg[:, q % 2, :, :], kv[:, s:s + 4, D:2 * D], exb[:, q % 2, :, :],
                                        ALU.mult).then_inc(sem(tag + "msg"), 1)

                    def add(g, q):
                        m = quad(g, q)
                        at = bases(dve, g * TG + 4 * q)
                        for j in range(4):
                            dve.wait_ge(sem(tag + "agg"), 2 * m + j // 2 + 1)
                            if not (skip(g) and q == 0 and j == 0):
                                dve.wait_ge(sem(tag + "acc"), 4 * m + j)
                            win = acc[:, :, ds(at[j], P)]
                            v.tensor_tensor(win, win, pA[j // 2][:, j % 2, :, :], ALU.add).then_inc(sem(tag + "acc"), 1)

                    def score(g, q, par):
                        n = quad(g, q)
                        dve.wait_ge(sem(tag + "qx"), n + 1)
                        rows_there(dve, l, uses(g, par), par, q)
                        s = par * TG + 4 * q
                        if not (skip(g) and q == 0):
                            dve.wait_ge(sem(tag + "alpha"), n)
                        v.tensor_tensor(prodb[:, :, :], kv[:, s:s + 4, 0:D], pQ[q % 2][:, :, :],
                                        ALU.mult).then_inc(sem(tag + "prod"), 1)
                        dve.wait_ge(sem(tag + "prod"), n + 1)
                        v.tensor_reduce(sm["alpha"][:, :, 4 * q:4 * q + 4].rearrange("p h t -> p t h"),
                                        prodb[:, :, :].rearrange("p t (h f) -> p t h f", h=H), AX.X,
                                        ALU.add).then_inc(sem(tag + "alpha"), 1)

                    def uses(g, par):
                        return g // 2 if isinstance(g, int) else kk[0] + (1 - par)

                    def rescale(g):
                        G = l * GROUPS + g
                        _, at = nc.values_load_multi_w_load_instructions(
                            base_i[0:1, ds(g * TG, 1)], engines=[dve.engine], min_val=0, max_val=N,
                            skip_runtime_bounds_check_because="a destination")
                        dve.wait_ge(sem(tag + "exE"), G + 1)
                        if not skip(g):
                            dve.wait_ge(sem(tag + "acc"), 4 * QG * G)
                        col = acc[:, :, ds(at[0], 1)]
                        v.tensor_scalar(col, col, pX[:, 128:129], None, ALU.mult).then_inc(sem(tag + "scaled"), 1)
                        dve.wait_ge(sem(tag + "scaled"), G + 1)
                        settle(dve)

                    def group(g, par):
                        take_group(dve, tag, l, g, [(rel_now[:, :], rel, 1)])
                        for q in range(QG):
                            build(g, q, par)
                            if not skip(g):
                                weigh(g - 1, q, 1 - par)
                                if q > 0:
                                    add(g - 1, q - 1)
                            score(g, q, par)
                        if not skip(g):
                            add(g - 1, QG - 1)
                        softmax_vector(dve, sm, tag, g, l * GROUPS + g, pM, None)
                        rescale(g)

                    kk = [None]
                    v.memset(acc[:, :, :], 0.0).then_inc(sem(tag + "clear"), 1)
                    v.memset(sm["rowF"][:, :, :], NEG)
                    v.memset(sm["rowB"][:, :, :], NEG).then_inc(sem(tag + "clear"), 1)
                    dve.wait_ge(sem(tag + "clear"), 2 * (l + 1))
                    settle(dve)
                    group(0, 0)
                    group(1, 1)
                    group(2, 0)
                    with dve.Fori(1, (GROUPS - 1) // 2) as k:
                        kk[0] = k
                        group(2 * k + 1, 1)
                        group(2 * k + 2, 0)
                    for q in range(QG):
                        weigh(GROUPS - 1, q, 0)
                        add(GROUPS - 1, q)

        def node_stage(tag, l, kind, sb, pb, acc, extra):
            h = sb("ns_h", [P, NPAD])
            s = sb("ns_s", [P, NPAD])
            ps = [pb(f"ns_p{i}", [P, BW]) for i in range(3)]
            pm = [pb(f"ns_m{i}", [P, BW]) for i in range(4)]
            cols = sb("ns_cols", [P, 3])
            w = extra.get("w")
            v, a = nc.vector, nc.scalar
            S_ = lambda n: sem(tag + n)
            o = l * NB
            blk = lambda b: slice(b * BW, (b + 1) * BW)
            attn = kind in ("conv", "last")

            with nc.Block() as block:
                @block.sync
                def _(sp):
                    sp.dma_start(cols[:, :], extra["cols"]).then_inc(S_("cols"), 16)
                    sp.wait_ge(S_("cols"), 16 * (l + 1))
                    settle(sp)
                    if "fetch" in extra:
                        extra["fetch"](sp, S_)
                    if kind == "last":
                        sp.wait_ge(S_("skip"), o + NB)
                        sp.dma_start(xT[:, :], xT_in).then_inc(S_("x_again"), 16)
                        sp.wait_ge(S_("x_again"), 16)

                @block.tensor
                def _(pe):
                    if "pre" in extra:
                        extra["pre"](pe, "tensor", ps, S_, o, blk)
                    for b in range(NB):
                        pe.wait_ge(S_("h"), o + b + 1)
                        if b >= 4:
                            pe.wait_ge(S_("cent"), o + b - 3)
                        nc.tensor.matmul(pm[b % 4][:, :], mean_w[:, :], h[:, blk(b)], start=True,
                                         stop=True).then_inc(S_("mean"), 1)
                    for b in range(NB):
                        pe.wait_ge(S_("sq"), o + b + 1)
                        pe.wait_ge(S_("cent"), o + NB)
                        if b >= 4:
                            pe.wait_ge(S_("sd"), o + b - 3)
                        nc.tensor.matmul(pm[b % 4][:, :], mean_w[:, :], s[:, blk(b)], start=True,
                                         stop=True).then_inc(S_("var"), 1)

                @block.scalar
                def _(act):
                    if "pre" in extra:
                        extra["pre"](act, "scalar", ps, S_, o, blk)
                    for b in range(NB):
                        act.wait_ge(S_("cent"), o + b + 1)
                        a.activation(s[:, blk(b)], h[:, blk(b)], ACT.Square).then_inc(S_("sq"), 1)
                    for b in range(NB):
                        act.wait_ge(S_("var"), o + b + 1)
                        a.activation(s[:, blk(b)], pm[b % 4][:, :], ACT.Sqrt, bias=eps_col[:, :]).then_inc(S_("sd"), 1)
                    if kind == "conv":
                        for b in range(NB):
                            act.wait_ge(S_("cols"), 16 * (l + 1))
                            act.wait_ge(S_("norm"), o + b + 1)
                            a.activation(s[:, blk(b)], h[:, blk(b)], ACT.Gelu, bias=cols[:, 2:3],
                                         scale=cols[:, 1:2]).then_inc(S_("act"), 1)

                @block.vector
                def _(dve):
                    dve.wait_ge(S_("cols"), 16 * (l + 1))
                    extra["form"](dve, h, s, ps, cols, S_, o, blk)
                    for b in range(NB):
                        dve.wait_ge(S_("mean"), o + b + 1)
                        v.tensor_tensor(h[:, blk(b)], h[:, blk(b)], pm[b % 4][:, :], ALU.subtract).then_inc(S_("cent"), 1)
                    for b in range(NB):
                        dve.wait_ge(S_("sd"), o + b + 1)
                        v.reciprocal(s[:, blk(b)], s[:, blk(b)]).then_inc(S_("rs"), 1)
                        dve.wait_ge(S_("rs"), o + b + 1)
                        to = h if kind == "conv" else xT
                        v.tensor_tensor(to[:, blk(b)], h[:, blk(b)], s[:, blk(b)], ALU.mult).then_inc(S_("norm"), 1)
                    if kind == "conv":
                        for b in range(NB):
                            dve.wait_ge(S_("act"), o + b + 1)
                            v.tensor_tensor(xT[:, blk(b)], xT[:, blk(b)], s[:, blk(b)], ALU.add).then_inc(S_("x"), 1)

        def conv_nodes(l, kind, sb, pb, acc, w):
            tag = "n0_"
            v, a = nc.vector, nc.scalar

            def pre(eng, what, ps, S_, o, blk):
                if what == "tensor":
                    for b in range(NB):
                        if b >= 3:
                            eng.wait_ge(S_("sum"), o + b - 2)
                        nc.tensor.matmul(ps[b % 3][:, :], w[:, 3 * D:4 * D], xT[:, blk(b)], start=True,
                                         stop=True).then_inc(S_("skip"), 1)
                elif kind == "last":
                    for b in range(NB):
                        eng.wait_ge(S_("sum"), o + b + 1)
                        a.activation(acc[:, 0, blk(b)], acc[:, 0, blk(b)], ACT.Gelu).then_inc(S_("gelu"), 1)

            def form(dve, h, s, ps, cols, S_, o, blk):
                out_ = acc[:, 0, :] if kind == "last" else h
                for b in range(NB):
                    den, num = acc[:, 1, blk(b)], acc[:, 0, blk(b)]
                    v.tensor_scalar(den, den, 1e-16, None, ALU.add).then_inc(S_("d1"), 1)
                    dve.wait_ge(S_("d1"), 2 * (o + b) + 1)
                    v.reciprocal(den, den).then_inc(S_("d1"), 1)
                    dve.wait_ge(S_("d1"), 2 * (o + b) + 2)
                    v.tensor_tensor(num, num, den, ALU.mult).then_inc(S_("att"), 1)
                for b in range(NB):
                    dve.wait_ge(S_("skip"), o + b + 1)
                    dve.wait_ge(S_("att"), o + b + 1)
                    v.scalar_tensor_tensor(out=out_[:, blk(b)], in0=ps[b % 3][:, :], scalar=cols[:, 0:1],
                                           in1=acc[:, 0, blk(b)], op0=ALU.add, op1=ALU.add
                                           ).then_inc(S_("sum"), 1)
                    if kind == "conv":
                        dve.wait_ge(S_("sum"), o + b + 1)
                        dve.sem_inc(S_("h"), 1)
                if kind == "last":
                    dve.wait_ge(S_("x_again"), 16)
                    for b in range(NB):
                        dve.wait_ge(S_("gelu"), b + 1)
                        v.tensor_tensor(h[:, blk(b)], acc[:, 0, blk(b)], xT[:, blk(b)], ALU.add).then_inc(S_("h"), 1)

            node_stage(tag, l, kind, sb, pb, acc, dict(
                cols=col0[ds(l, 1), :, :].rearrange("l p n -> (l p) n"), pre=pre, form=form))

        def maker(scope, space, suffix):
            return lambda name, shape, dt=f32: scope.enter_context(space(name + suffix, shape, dt))

        def conv_layer(l, kind):
            with ExitStack() as keep:
                acc = maker(keep, nc.sbuf_tensor, kind)("acc", [P, 2, NPAD])
                with ExitStack() as part:
                    wide = maker(keep, nc.sbuf_tensor, kind)
                    narrow = maker(part, nc.sbuf_tensor, kind)
                    w = conv_project(l, lambda name, *a: (wide if name == "w" else narrow)(name, *a),
                                     maker(part, nc.psum_tensor, kind))
                with ExitStack() as part:
                    conv_edges(l, maker(part, nc.sbuf_tensor, kind), maker(part, nc.psum_tensor, kind), acc)
                with ExitStack() as part:
                    conv_nodes(l, kind, maker(part, nc.sbuf_tensor, kind), maker(part, nc.psum_tensor, kind), acc, w)

        def rel_project(sb, pb):
            wcat = sb("wcat", [P, R, RW])
            wt = sb("wt", [P, R, P])
            at = sb("at", [P, R, 2 * H])
            stage = sb("stage", [P, 2, 4, R, RW])
            ad = sb("ad", [P, 2, 4, R * H])
            pw = pb("pw", [P, R, 2 * H])
            pr = [pb(f"pr{i}", [P, 2, RW]) for i in range(4)]
            v, a = nc.vector, nc.scalar
            loaded, folded, put, prod = sem("rp_w"), sem("rp_folded"), sem("rp_put"), sem("rp_prod")
            copied, dsts = sem("rp_copied"), sem("rp_dsts")
            stored = [sem("rp_stored0"), sem("rp_stored1")]
            with nc.Block() as block:
                @block.sync
                def _(sp):
                    sp.dma_start(wcat[:, :, 0:D], w1).then_inc(loaded, 16)
                    sp.dma_start(wt[:, :, :], w1T).then_inc(loaded, 16)
                    sp.dma_start(at[:, :, :], a1.rearrange("o r k h -> o r (k h)")).then_inc(loaded, 16)
                    for b in range(NB):
                        sp.wait_ge(copied, 8 * (b + 1))
                        for r in range(R):
                            first = r * NPAD + b * BW
                            sp.dma_start(rel_tab[first:first + BW, :].rearrange("(j p) f -> p j f", p=P),
                                         stage[:, b % 2, :, r, :]).then_inc(stored[b % 2], 16)
                        sp.wait_ge(dsts, b + 1)
                        sp.dma_start(adst_tab[b * BW:(b + 1) * BW, :].rearrange("(j p) f -> p j f", p=P),
                                     ad[:, b % 2, :, :]).then_inc(stored[b % 2], 16)
                    sp.wait_ge(stored[0], 80 * ((NB + 1) // 2))
                    sp.wait_ge(stored[1], 80 * (NB // 2))

                @block.tensor
                def _(pe):
                    pe.wait_ge(loaded, 48)
                    for r in range(R):
                        last = nc.tensor.matmul(pw[:, r, :], wt[:, r, :], at[:, r, :], start=True, stop=True)
                    last.then_inc(folded, 1)
                    pe.wait_ge(put, 1)
                    for t in range(NT):
                        for u in range(2):
                            n = 2 * t + u
                            if n >= 4:
                                pe.wait_ge(copied, n - 3)
                            nc.tensor.matmul(pr[n % 4][:, :, :], xT[:, t * P:(t + 1) * P], wcat[:, 2 * u:2 * u + 2, :],
                                             start=True, stop=True).then_inc(prod, 1)

                @block.scalar
                def _(act):
                    act.wait_ge(folded, 1)
                    a.activation(wcat[:, :, D:RW], pw[:, :, :], ACT.Copy).then_inc(put, 1)
                    for n in range(2 * NT):
                        b = n // 8
                        if n % 8 == 0 and b >= 2:
                            act.wait_ge(stored[b % 2], 80 * (b // 2))
                            act.wait_ge(dsts, b - 1)
                        act.wait_ge(prod, n + 1)
                        u = n % 2
                        a.activation(stage[:, b % 2, (n // 2) % 4, 2 * u:2 * u + 2, :], pr[n % 4][:, :, :],
                                     ACT.Copy).then_inc(copied, 1)

                @block.vector
                def _(dve):
                    for b in range(NB):
                        dve.wait_ge(copied, 8 * (b + 1))
                        if b >= 2:
                            dve.wait_ge(stored[b % 2], 80 * (b // 2))
                        v.tensor_copy(ad[:, b % 2, :, :].rearrange("p j (r h) -> p j r h", h=H),
                                      stage[:, b % 2, :, :, D + H:RW]).then_inc(dsts, 1)

        def rel_edges(sb, pb, acc, den, type_f, tm, idx1):
            tag = "r_"
            rows = sb("rows", [P, 2 * TG, RW])
            S = sb("S", [P, 2, 4, P])
            S2 = sb("S2", [P, 4, P])
            St = sb("St", [P, 4, R, P])
            ST = sb("ST", [P, 2, 4, P])
            awin = sb("awin", [P, 2, 4, R * H])
            picked = sb("picked", [P, 4, R, H])
            al = sb("al", [P, 4, H])
            exb = sb("exb", [P, 2, 4, D])
            msg = sb("msg", [P, 2, 4, D])
            exm = sb("exm", [P, 2, 4, R * H + 1])
            idx_now = sb("idx_now", [P, 2, TG], i32)
            val_i = sb("val_i", [R * H, R], i32)
            val_f = sb("val_f", [R * H, R])
            csel = sb("csel", [R * H, R])
            hsel = sb("hsel", [P, R, H])
            fac = sb("fac", [R * H, R])
            fac1 = sb("fac1", [R * H, 1])
            rel_now = sb("rel_now", [P, 2, TG])
            tm_now = sb("tm_now", [P, 2, TG * R])
            sm = softmax_buffers(sb, R)
            pT = pb("pT", [P, 4, P])
            pQ = [pb(f"pQ{i}", [P, 4, R * H]) for i in range(2)]
            pA = [pb(f"pA{i}", [P, R, P]) for i in range(2)]
            pD = pb("pD", [R * H + 1, 4, P])
            pM = pb("pM", [P, 512])
            pX = pb("pX", [P, 512])
            quad = lambda g, q: g * QG + q
            skip = lambda g: isinstance(g, int) and g == 0

            with nc.Block() as block:
                @block.gpsimd
                def _(pool):
                    nc.gpsimd.iota(val_i[:, :], pattern=[[-H, R]], base=0, channel_multiplier=1
                                   ).then_inc(sem(tag + "iota"), 1)
                    gather_all(pool, lambda g, par: gather_group(pool, tag, 0, g, par, rel_tab, idx1, idx_now, rows))

                @block.sync
                def _(sp):
                    def group(g):
                        for q in range(QG):
                            n = quad(g, q)
                            at = bases(sp, g * TG + 4 * q)
                            if not (skip(g) and q < 2):
                                sp.wait_ge(sem(tag + "qx"), n - 1)
                                settle(sp)
                            for j in range(4):
                                sp.dma_start(awin[:, q % 2, j, :], adst_tab[ds(at[j], P), :]
                                             ).then_inc(sem(f"{tag}qwin{q % 2}"), 16)
                    group(0)
                    with sp.Fori(1, GROUPS) as g:
                        group(g)

                @block.tensor
                def _(pe):
                    def turn(g, q):
                        n = quad(g, q)
                        pe.wait_ge(sem(tag + "S"), n + 1)
                        if not (skip(g) and q == 0):
                            pe.wait_ge(sem(tag + "ST"), n)
                        for j in range(4):
                            last = nc.tensor.transpose(pT[:, j, :], S[:, q % 2, j, :], ident[:, :])
                        last.then_inc(sem(tag + "turned"), 1)

                    def scores(g, q):
                        n = quad(g, q)
                        pe.wait_ge(sem(tag + "ST"), n + 1)
                        pe.wait_ge(sem(f"{tag}qwin{q % 2}"), 64 * (g * (QG // 2) + q // 2 + 1))
                        if not (skip(g) and q < 2):
                            pe.wait_ge(sem(tag + "prod"), n - 1)
                        for j in range(4):
                            last = nc.tensor.matmul(pQ[q % 2][:, j, :], ST[:, q % 2, j, :], awin[:, q % 2, j, :],
                                                    start=True, stop=True)
                        last.then_inc(sem(tag + "qx"), 1)

                    def sums(g, q):
                        m = quad(g, q)
                        pe.wait_ge(sem(tag + "built"), m + 1)
                        if not (skip(g) and q == 0):
                            pe.wait_ge(sem(tag + "den"), 4 * m)
                        for j in range(4):
                            last = nc.tensor.matmul(pD[:, j, :], exm[:, q % 2, j, :], S2[:, j, :], start=True, stop=True)
                        last.then_inc(sem(tag + "counted"), 1)
                        for j in range(4):
                            if not (skip(g) and q == 0 and j < 2):
                                pe.wait_ge(sem(tag + "acc"), 4 * m + j - 1)
                            nc.tensor.matmul(pA[j % 2][:, :, :], msg[:, q % 2, j, :], St[:, j, :, :], start=True,
                                             stop=True).then_inc(sem(tag + "agg"), 1)

                    def group(g):
                        for q in range(QG):
                            turn(g, q)
                            scores(g, q)
                            if not skip(g):
                                sums(g - 1, q)
                        softmax_tensor_1(pe, sm, tag, g, pM)
                        pe.wait_ge(sem(tag + "ex_ready"), g + 1)
                        nc.tensor.matmul(pX[0:R * H, 136:136 + R], hsel[:, :, :].rearrange("p c h -> p (c h)"), sm["f"][:, :],
                                         start=True, stop=True)
                        turn_ex(pe, sm, tag, g, pX)
                    pe.wait_ge(sem(tag + "made"), 1)
                    group(0)
                    group(1)
                    with pe.Fori(2, GROUPS) as g:
                        group(g)
                    for q in range(QG):
                        sums(GROUPS - 1, q)

                @block.scalar
                def _(act):
                    def st_copy(g, q):
                        n = quad(g, q)
                        act.wait_ge(sem(tag + "turned"), n + 1)
                        if not (skip(g) and q < 2):
                            act.wait_ge(sem(tag + "qx"), n - 1)
                        nc.scalar.activation(ST[:, q % 2, :, :], pT[:, :, :], ACT.Copy).then_inc(sem(tag + "ST"), 1)

                    def spread(g, q, par):
                        m = quad(g, q)
                        if q == 0:
                            act.wait_ge(sem(tag + "exE"), g + 1)
                        if not (skip(g) and q < 2):
                            act.wait_ge(sem(tag + "built"), m - 1)
                        src = sm["exE"][:, par, :, 4 * q:4 * q + 4].rearrange("p h t -> p t h")
                        nc.scalar.activation(exb[:, q % 2, :, :].rearrange("p t (h f) -> p t h f", h=H),
                                             src.unsqueeze(3).to_broadcast([P, 4, H, HD]), ACT.Copy
                                             ).then_inc(sem(tag + "exb"), 1)

                    def group(g, par):
                        for q in range(QG):
                            st_copy(g, q)
                            if not skip(g):
                                spread(g - 1, q, 1 - par)
                        softmax_scalar(act, sm, tag, par, g, pM, pX, 1.0)
                    group(0, 0)
                    group(1, 1)
                    group(2, 0)
                    with act.Fori(1, (GROUPS - 1) // 2) as k:
                        group(2 * k + 1, 1)
                        group(2 * k + 2, 0)
                    for q in range(QG):
                        spread(GROUPS - 1, q, 0)

                @block.vector
                def _(dve):
                    v = nc.vector
                    kk = [None]

                    def build(g, q, par):
                        if not (skip(g) and q < 2):
                            dve.wait_ge(sem(tag + "turned"), quad(g, q) - 1)
                        for j in range(4):
                            last = v.tensor_scalar(S[:, q % 2, j, :], iota_row[:, :],
                                                   rel_now[:, par, 4 * q + j:4 * q + j + 1], None, ALU.is_equal)
                        last.then_inc(sem(tag + "S"), 1)

                    def mask(q, par):
                        return tm_now[:, par, 4 * q * R:4 * (q + 1) * R].rearrange("p (t c) -> p t c", c=R)

                    def weigh(g, q, par):
                        m = quad(g, q)
                        if not (skip(g) and q == 0):
                            dve.wait_ge(sem(tag + "agg"), 4 * m)
                        for j in range(4):
                            t = 4 * q + j
                            v.tensor_scalar(S2[:, j, :], iota_row[:, :], rel_now[:, par, t:t + 1], None, ALU.is_equal)
                            for c in range(R):
                                v.tensor_scalar(St[:, j, c, :], iota_row[:, :], rel_now[:, par, t:t + 1],
                                                tm_now[:, par, t * R + c:t * R + c + 1], ALU.is_equal, ALU.mult)
                        dve.wait_ge(sem(tag + "exE"), g + 1)
                        ex = sm["exE"][:, par, :, 4 * q:4 * q + 4].rearrange("p h t -> p t h")
                        v.tensor_tensor(exm[:, q % 2, :, 0:R * H].rearrange("p t (c h) -> p t c h", c=R),
                                        ex.unsqueeze(2).to_broadcast([P, 4, R, H]),
                                        mask(q, par).unsqueeze(3).to_broadcast([P, 4, R, H]), ALU.mult)
                        dve.wait_ge(sem(tag + "exb"), m + 1)
                        s = par * TG + 4 * q
                        v.tensor_tensor(msg[:, q % 2, :, :], rows[:, s:s + 4, 0:D], exb[:, q % 2, :, :],
                                        ALU.mult).then_inc(sem(tag + "msg"), 1)
                        dve.wait_ge(sem(tag + "msg"), m + 1)
                        dve.sem_inc(sem(tag + "built"), 1)

                    def add(g, q):
                        m = quad(g, q)
                        at = bases(dve, g * TG + 4 * q)
                        dve.wait_ge(sem(tag + "counted"), m + 1)
                        for j in range(4):
                            if not (skip(g) and q == 0 and j == 0):
                                dve.wait_ge(sem(tag + "den"), 4 * m + j)
                            win = den[:, ds(at[j], P)]
                            v.tensor_tensor(win, win, pD[:, j, :], ALU.add).then_inc(sem(tag + "den"), 1)
                        for j in range(4):
                            dve.wait_ge(sem(tag + "agg"), 4 * m + j + 1)
                            if not (skip(g) and q == 0 and j == 0):
                                dve.wait_ge(sem(tag + "acc"), 4 * m + j)
                            win = acc[:, :, ds(at[j], P)]
                            v.tensor_tensor(win, win, pA[j % 2][:, :, :], ALU.add).then_inc(sem(tag + "acc"), 1)

                    def score(g, q, par):
                        n = quad(g, q)
                        dve.wait_ge(sem(tag + "qx"), n + 1)
                        if not (skip(g) and q == 0):
                            dve.wait_ge(sem(tag + "alpha"), n)
                        v.tensor_tensor(picked[:, :, :, :], pQ[q % 2][:, :, :].rearrange("p t (c h) -> p t c h", c=R),
                                        mask(q, par).unsqueeze(3).to_broadcast([P, 4, R, H]), ALU.mult
                                        ).then_inc(sem(tag + "prod"), 1)
                        dve.wait_ge(sem(tag + "prod"), n + 1)
                        v.tensor_reduce(al[:, :, :], picked[:, :, :, :].rearrange("p t c h -> p t h c"), AX.X,
                                        ALU.add).then_inc(sem(tag + "al"), 1)
                        dve.wait_ge(sem(tag + "al"), 2 * n + 1)
                        half = g // 2 if isinstance(g, int) else kk[0] + (1 - par)
                        rows_there(dve, CONVS, half, par, q)
                        s = par * TG + 4 * q
                        v.tensor_tensor(al[:, :, :], al[:, :, :], rows[:, s:s + 4, D:D + H], ALU.add
                                        ).then_inc(sem(tag + "al"), 1)
                        dve.wait_ge(sem(tag + "al"), 2 * n + 2)
                        v.scalar_tensor_tensor(out=sm["alpha"][:, :, 4 * q:4 * q + 4].rearrange("p h t -> p t h"),
                                               in0=al[:, :, :], scalar=0.2, in1=al[:, :, :], op0=ALU.mult,
                                               op1=ALU.max).then_inc(sem(tag + "alpha"), 1)

                    def rescale(g):
                        _, at = nc.values_load_multi_w_load_instructions(
                            base_i[0:1, ds(g * TG, 1)], engines=[dve.engine], min_val=0, max_val=N,
                            skip_runtime_bounds_check_because="a destination")
                        dve.wait_ge(sem(tag + "exE"), g + 1)
                        if not skip(g):
                            dve.wait_ge(sem(tag + "acc"), 4 * QG * g)
                        col = acc[:, :, ds(at[0], 1)]
                        v.tensor_tensor(col, col, pX[:, 128:128 + R].unsqueeze(2), ALU.mult)
                        v.tensor_tensor(fac[:, :], pX[0:R * H, 136:136 + R], csel[:, :], ALU.mult).then_inc(sem(tag + "scaled"), 1)
                        dve.wait_ge(sem(tag + "scaled"), 3 * g + 1)
                        v.tensor_reduce(fac1[:, :], fac[:, :], AX.X, ALU.add).then_inc(sem(tag + "scaled"), 1)
                        dve.wait_ge(sem(tag + "scaled"), 3 * g + 2)
                        if not skip(g):
                            dve.wait_ge(sem(tag + "den"), 4 * QG * g)
                        col = den[0:R * H, ds(at[0], 1)]
                        v.tensor_scalar(col, col, fac1[:, :], None, ALU.mult).then_inc(sem(tag + "scaled"), 1)
                        dve.wait_ge(sem(tag + "scaled"), 3 * g + 3)
                        settle(dve)

                    def group(g, par):
                        take_group(dve, tag, 0, g, [(rel_now[:, par, :], rel, 1), (tm_now[:, par, :], tm, R)])
                        for q in range(QG):
                            build(g, q, par)
                            if not skip(g):
                                weigh(g - 1, q, 1 - par)
                            score(g, q, par)
                            if not skip(g):
                                add(g - 1, q)
                        softmax_vector(dve, sm, tag, g, g, pM, type_f)
                        rescale(g)

                    v.memset(acc[:, :, :], 0.0)
                    v.memset(den[:, :], 0.0)
                    v.memset(exm[:, :, :, R * H], 1.0)
                    v.memset(sm["rowF"][:, :, :], NEG)
                    v.memset(sm["rowB"][:, :, :], NEG)
                    for c in range(R):
                        for h in range(H):
                            v.tensor_copy(hsel[:, c, h:h + 1], head_sel[:, h * HD:h * HD + 1])
                    dve.wait_ge(sem(tag + "iota"), 1)
                    v.tensor_copy(val_f[:, :], val_i[:, :]).then_inc(sem(tag + "made0"), 1)
                    dve.wait_ge(sem(tag + "made0"), 1)
                    v.tensor_scalar(csel[:, :], val_f[:, :], 0.0, None, ALU.is_ge)
                    v.tensor_scalar(val_f[:, :], val_f[:, :], float(H - 1), None, ALU.is_le).then_inc(sem(tag + "made0"), 1)
                    dve.wait_ge(sem(tag + "made0"), 2)
                    v.tensor_tensor(csel[:, :], csel[:, :], val_f[:, :], ALU.mult).then_inc(sem(tag + "made"), 1)
                    dve.wait_ge(sem(tag + "made"), 1)
                    group(0, 0)
                    group(1, 1)
                    group(2, 0)
                    with dve.Fori(1, (GROUPS - 1) // 2) as k:
                        kk[0] = k
                        group(2 * k + 1, 1)
                        group(2 * k + 2, 0)
                    for q in range(QG):
                        weigh(GROUPS - 1, q, 0)
                        add(GROUPS - 1, q)

        def rel_prepare(sb, type_f, tm, idx1):
            tc_i = sb("tc_i", [P, T], i32)
            tr_i = sb("tr_i", [P, GROUPS * P], i32)
            t_f = sb("t_f", [P, T])
            s_f = sb("s_f", [P, T])
            with nc.Block() as block:
                @block.sync
                def _(sp):
                    sp.dma_start(tc_i[:, :], type_c).then_inc(sem("rt_in"), 16)
                    for h in range(H):
                        sp.dma_start(tr_i[h * TG:(h + 1) * TG, :], type_r).then_inc(sem("rt_in"), 16)

                @block.vector
                def _(dve):
                    v = nc.vector
                    dve.wait_ge(sem("rt_in"), 16 * (1 + H))
                    v.tensor_copy(type_f[:, :], tr_i[:, :])
                    v.tensor_copy(t_f[:, :], tc_i[:, :])
                    v.tensor_copy(s_f[:, :], src_all[:, :]).then_inc(sem("rt"), 1)
                    dve.wait_ge(sem("rt"), 1)
                    for c in range(R):
                        v.tensor_scalar(tm[:, :].rearrange("p (t c) -> p t c", c=R)[:, :, c], t_f[:, :], float(c), None, ALU.is_equal)
                    v.scalar_tensor_tensor(out=idx1[:, :], in0=t_f[:, :], scalar=float(NPAD), in1=s_f[:, :],
                                           op0=ALU.mult, op1=ALU.add)

        def rel_nodes(sb, pb, acc, den, dinv_f, dinv_n):
            tag = "n1_"
            v, a = nc.vector, nc.scalar
            K = R * H + 1
            sel_i = sb("sel_i", [K, R + 1, P], i32)
            sel = sb("sel", [K, R + 1, P])
            rden = sb("rden", [K, NPAD])
            pn = pb("pn", [P, NT])

            with nc.Block() as block:
                @block.gpsimd
                def _(pool):
                    nc.gpsimd.iota(sel_i[:, 0:R, :].rearrange("k c (h f) -> k c h f", h=H), pattern=[[H, R], [1, H], [0, HD]],
                                   base=0, channel_multiplier=-1)
                    nc.gpsimd.iota(sel_i[:, R, :], pattern=[[0, P]], base=R * H, channel_multiplier=-1
                                   ).then_inc(sem("rn_iota"), 1)

                @block.vector
                def _(dve):
                    dve.wait_ge(sem("rn_iota"), 1)
                    v.tensor_copy(sel[:, :, :], sel_i[:, :, :]).then_inc(sem("rn_sel"), 1)
                    dve.wait_ge(sem("rn_sel"), 1)
                    v.tensor_scalar(sel[:, :, :], sel[:, :, :], 0.0, None, ALU.is_equal).then_inc(sem("rn_sel"), 1)
                    v.tensor_scalar(rden[:, :], den[:, :], 1e-30, None, ALU.max).then_inc(sem("rn_max"), 1)
                    dve.wait_ge(sem("rn_max"), 1)
                    v.reciprocal(rden[:, :], rden[:, :]).then_inc(sem("rn_max"), 1)
                    dve.wait_ge(sem("rn_sd"), 2)
                    v.reciprocal(dinv_n[:, :], dinv_n[:, :])
                    v.reciprocal(dinv_f[:, :], dinv_f[:, :])

                @block.tensor
                def _(pe):
                    pe.wait_ge(sem("rn_sel"), 2)
                    for t in range(NT):
                        last = nc.tensor.matmul(pn[:, t:t + 1], den[:, t * P:(t + 1) * P], sel[:, R, 0:1], start=True, stop=True)
                    last.then_inc(sem("rn_n"), 1)
                    for b in range(NB):
                        if b >= 2:
                            pe.wait_ge(sem("rn_cnt"), b - 1)
                        nc.tensor.matmul(cnt_p[b % 2][:, :], sel[:, R, :], den[:, b * BW:(b + 1) * BW], start=True,
                                         stop=True).then_inc(sem("rn_f"), 1)

                @block.scalar
                def _(act):
                    act.wait_ge(sem("rn_n"), 1)
                    a.activation(dinv_n[:, :], pn[:, :], ACT.Sqrt, bias=ones[:, 0:1]).then_inc(sem("rn_sd"), 1)
                    for b in range(NB):
                        act.wait_ge(sem("rn_f"), b + 1)
                        last = a.activation(dinv_f[:, b * BW:(b + 1) * BW], cnt_p[b % 2][:, :], ACT.Sqrt,
                                            bias=ones[:, 0:1]).then_inc(sem("rn_cnt"), 1)
                    act.wait_ge(sem("rn_cnt"), NB)
                    act.sem_inc(sem("rn_sd"), 1)

            def pre(eng, what, ps, S_, o, blk):
                if what == "tensor":
                    for b in range(NB):
                        for c in range(R):
                            n = b * R + c
                            if n >= 3:
                                eng.wait_ge(S_("quot"), n - 2)
                            nc.tensor.matmul(ps[n % 3][:, :], sel[:, c, :], rden[:, blk(b)], start=True,
                                             stop=True).then_inc(S_("rden"), 1)

            def form(dve, h, s, ps, cols, S_, o, blk):
                for b in range(NB):
                    for c in range(R):
                        n = b * R + c
                        dve.wait_ge(S_("rden"), n + 1)
                        v.tensor_tensor(acc[:, c, blk(b)], acc[:, c, blk(b)], ps[n % 3][:, :], ALU.mult
                                        ).then_inc(S_("quot"), 1)
                    dve.wait_ge(S_("quot"), R * (b + 1))
                    v.tensor_tensor(acc[:, 0, blk(b)], acc[:, 0, blk(b)], acc[:, 1, blk(b)], ALU.add)
                    v.tensor_tensor(acc[:, 2, blk(b)], acc[:, 2, blk(b)], acc[:, 3, blk(b)], ALU.add).then_inc(S_("two"), 1)
                    dve.wait_ge(S_("two"), 2 * b + 1)
                    v.tensor_tensor(acc[:, 0, blk(b)], acc[:, 0, blk(b)], acc[:, 2, blk(b)], ALU.add).then_inc(S_("two"), 1)
                    dve.wait_ge(S_("two"), 2 * b + 2)
                    v.tensor_tensor(h[:, blk(b)], acc[:, 0, blk(b)], xT[:, blk(b)], ALU.add).then_inc(S_("h"), 1)
            return dict(cols=col0[0], pre=pre, form=form)

        def rel_layer(dinv_f, dinv_n):
            with ExitStack() as part:
                rel_project(maker(part, nc.sbuf_tensor, "_r"), maker(part, nc.psum_tensor, "_r"))
            with ExitStack() as keep:
                wide = maker(keep, nc.sbuf_tensor, "_r")
                acc = wide("acc", [P, R, NPAD])
                den = wide("den", [R * H + 1, NPAD])
                with ExitStack() as mid:
                    m = maker(mid, nc.sbuf_tensor, "_r")
                    type_f, tm, idx1 = m("type_f", [P, GROUPS * P], bf16), m("tm", [P, T * R]), m("idx1", [P, T], i32)
                    with ExitStack() as part:
                        rel_prepare(maker(part, nc.sbuf_tensor, "_r"), type_f, tm, idx1)
                    with ExitStack() as part:
                        rel_edges(maker(part, nc.sbuf_tensor, "_r"), maker(part, nc.psum_tensor, "_r"), acc, den,
                                  type_f, tm, idx1)
                with ExitStack() as part:
                    sb, pb = maker(part, nc.sbuf_tensor, "_r"), maker(part, nc.psum_tensor, "_r")
                    with ExitStack() as few:
                        cnt_p[:] = [maker(few, nc.psum_tensor, "_r")(f"cnt{i}", [P, BW]) for i in range(2)]
                        extra = rel_nodes(sb, maker(few, nc.psum_tensor, "_r"), acc, den, dinv_f, dinv_n)
                    node_stage("n1_", 0, "rel", sb, pb, acc, extra)

        cnt_p = []

        def plain_project(tag, x, w, dinv_n, sb, pb):
            stage = sb("stage", [P, 2, 4, D])
            pp = [pb(f"pp{i}", [P, D]) for i in range(4)]
            prod, copied = sem(tag + "prod"), sem(tag + "copied")
            stored = [sem(tag + "stored0"), sem(tag + "stored1")]
            with nc.Block() as block:
                @block.sync
                def _(sp):
                    for b in range(NB):
                        sp.wait_ge(copied, 4 * (b + 1))
                        sp.dma_start(h_tab[b * BW:(b + 1) * BW, :].rearrange("(j p) f -> p j f", p=P),
                                     stage[:, b % 2, :, :]).then_inc(stored[b % 2], 16)
                    sp.wait_ge(stored[0], 16 * ((NB + 1) // 2))
                    sp.wait_ge(stored[1], 16 * (NB // 2))

                @block.tensor
                def _(pe):
                    for t in range(NT):
                        if t >= 4:
                            pe.wait_ge(copied, t - 3)
                        nc.tensor.matmul(pp[t % 4][:, :], x[:, t * P:(t + 1) * P], w[:, :], start=True,
                                         stop=True).then_inc(prod, 1)

                @block.scalar
                def _(act):
                    for t in range(NT):
                        b = t // 4
                        if t % 4 == 0 and b >= 2:
                            act.wait_ge(stored[b % 2], 16 * (b // 2))
                        act.wait_ge(prod, t + 1)
                        scale = dinv_n[:, t:t + 1] if dinv_n is not None else 1.0
                        nc.scalar.activation(stage[:, b % 2, t % 4, :], pp[t % 4][:, :], ACT.Copy,
                                             scale=scale).then_inc(copied, 1)

        def plain_edges(tag, turn, acc, sb, pb):
            rows = sb("rows", [P, 2 * TG, D])
            S = sb("S", [P, 2, 4, P])
            idx_now = sb("idx_now", [P, 2, TG], i32)
            rel_now = sb("rel_now", [P, TG])
            lists = [(rel_now[:, :], rel, 1)]
            pA = [pb(f"pA{i}", [P, 4, P]) for i in range(2)]
            quad = lambda g, q: g * QG + q
            skip = lambda g: isinstance(g, int) and g == 0
            with nc.Block() as block:
                @block.gpsimd
                def _(pool):
                    gather_all(pool, lambda g, par: gather_group(pool, tag, 0, g, par, h_tab, src_all, idx_now, rows,
                                                                 "agg", "agg"))

                @block.tensor
                def _(pe):
                    def group(g, par, half):
                        for q in range(QG):
                            n = quad(g, q)
                            pe.wait_ge(sem(tag + "S"), n + 1)
                            rows_there(pe, turn, half, par, q)
                            if not (skip(g) and q < 2):
                                pe.wait_ge(sem(tag + "acc"), 4 * (n - 1))
                            for j in range(4):
                                last = nc.tensor.matmul(pA[q % 2][:, j, :], rows[:, par * TG + 4 * q + j, :],
                                                        S[:, q % 2, j, :], start=True, stop=True)
                            last.then_inc(sem(tag + "agg"), 1)
                    group(0, 0, 0)
                    with pe.Fori(0, (GROUPS - 1) // 2) as k:
                        group(2 * k + 1, 1, k)
                        group(2 * k + 2, 0, k + 1)

                @block.vector
                def _(dve):
                    v = nc.vector

                    def build(g, q):
                        if not (skip(g) and q < 2):
                            dve.wait_ge(sem(tag + "agg"), quad(g, q) - 1)
                        for j in range(4):
                            t = 4 * q + j
                            last = v.tensor_scalar(S[:, q % 2, j, :], iota_row[:, :], rel_now[:, t:t + 1], None,
                                                   ALU.is_equal)
                        last.then_inc(sem(tag + "S"), 1)

                    def add(g, q, first):
                        n = quad(g, q)
                        at = bases(dve, g * TG + 4 * q)
                        dve.wait_ge(sem(tag + "agg"), n + 1)
                        for j in range(4):
                            if not (first and j == 0):
                                dve.wait_ge(sem(tag + "acc"), 4 * n + j)
                            win = acc[:, ds(at[j], P)]
                            v.tensor_tensor(win, win, pA[q % 2][:, j, :], ALU.add).then_inc(sem(tag + "acc"), 1)

                    v.memset(acc[:, :], 0.0).then_inc(sem(tag + "clear"), 1)
                    dve.wait_ge(sem(tag + "clear"), 1)
                    take_group(dve, tag, 0, 0, lists)
                    build(0, 0)
                    for q in range(1, QG):
                        build(0, q)
                        add(0, q - 1, q == 1)
                    with dve.Fori(1, GROUPS) as g:
                        take_group(dve, tag, 0, g, lists)
                        for q in range(QG):
                            build(g, q)
                            if q:
                                add(g, q - 1, False)
                            else:
                                add(g - 1, QG - 1, False)
                    add(GROUPS - 1, QG - 1, False)

        def load(tag, pairs):
            with nc.Block() as block:
                @block.sync
                def _(sp):
                    for to, source in pairs:
                        sp.dma_start(to, source).then_inc(sem(tag), 16)
                    sp.wait_ge(sem(tag), 16 * len(pairs))

        def gcn_form(w, acc, dinv_f):
            v = nc.vector

            def own(eng, x, ps, S_, blk):
                for b in range(NB):
                    if b >= 3:
                        eng.wait_ge(S_("own_read"), b - 2)
                    nc.tensor.matmul(ps[b % 3][:, :], w[:, :], x[:, blk(b)], start=True, stop=True).then_inc(S_("own"), 1)

            def combine(dve, b, ps, cols, S_, blk):
                dve.wait_ge(S_("own"), b + 1)
                t = acc[:, blk(b)]
                v.tensor_tensor(tmp[0][:, blk(b)], ps[b % 3][:, :], dinv_f[:, blk(b)], ALU.mult).then_inc(S_("own_read"), 1)
                dve.wait_ge(S_("own_read"), b + 1)
                v.tensor_tensor(t, t, tmp[0][:, blk(b)], ALU.add).then_inc(S_("gc"), 1)
                dve.wait_ge(S_("gc"), 3 * b + 1)
                v.tensor_tensor(t, t, dinv_f[:, blk(b)], ALU.mult).then_inc(S_("gc"), 1)
                dve.wait_ge(S_("gc"), 3 * b + 2)
                v.tensor_scalar(t, t, cols[:, 0:1], None, ALU.add).then_inc(S_("gc"), 1)
                dve.wait_ge(S_("gc"), 3 * b + 3)
            return own, combine

        tmp = [None]

        def gcn_layer(dinv_f, dinv_n):
            v, a = nc.vector, nc.scalar
            blk = lambda b: slice(b * BW, (b + 1) * BW)
            with ExitStack() as keep:
                wide = maker(keep, nc.sbuf_tensor, "_g")
                acc, y = wide("acc", [P, NPAD]), wide("y", [P, NPAD])
                wa, wb, cols1 = wide("wa", [P, D]), wide("wb", [P, D]), wide("cols1", [P, 3])
                tmp[0] = wide("tmp", [P, NPAD])
                load("g_in", [(wa[:, :], w2[0]), (wb[:, :], w2[1]), (cols1[:, :], b2[0])])
                for tag, x, w in (("g1_", xT, wa), ("g2_", y, wb)):
                    with ExitStack() as part:
                        plain_project(tag + "p", x, w, dinv_n, maker(part, nc.sbuf_tensor, tag), maker(part, nc.psum_tensor, tag))
                    with ExitStack() as part:
                        plain_edges(tag, CONVS + 1 + (tag == "g2_"), acc, maker(part, nc.sbuf_tensor, tag), maker(part, nc.psum_tensor, tag))
                    with ExitStack() as part:
                        sb, pb = maker(part, nc.sbuf_tensor, tag), maker(part, nc.psum_tensor, tag)
                        own, combine = gcn_form(w, acc, dinv_f)
                        if tag == "g1_":
                            ps = [pb(f"po{i}", [P, BW]) for i in range(3)]
                            S_ = lambda n: sem("g1n_" + n)
                            with nc.Block() as block:
                                @block.tensor
                                def _(pe):
                                    own(pe, xT, ps, S_, blk)

                                @block.vector
                                def _(dve):
                                    for b in range(NB):
                                        combine(dve, b, ps, cols1, S_, blk)
                                        v.tensor_scalar(tmp[0][:, blk(b)], acc[:, blk(b)], 0.0, None, ALU.min
                                                        ).then_inc(S_("neg"), 1)
                                    for b in range(NB):
                                        dve.wait_ge(S_("exp"), b + 1)
                                        v.scalar_tensor_tensor(out=acc[:, blk(b)], in0=acc[:, blk(b)], scalar=0.0,
                                                               in1=tmp[0][:, blk(b)], op0=ALU.max, op1=ALU.add
                                                               ).then_inc(S_("elu"), 1)
                                        dve.wait_ge(S_("elu"), b + 1)
                                        v.tensor_scalar(y[:, blk(b)], acc[:, blk(b)], -1.0, None, ALU.add)

                                @block.scalar
                                def _(act):
                                    for b in range(NB):
                                        act.wait_ge(S_("neg"), b + 1)
                                        a.activation(tmp[0][:, blk(b)], tmp[0][:, blk(b)], ACT.Exp).then_inc(S_("exp"), 1)
                        else:
                            def pre(eng, what, ps, S_, o, blk):
                                if what == "tensor":
                                    own(eng, y, ps, S_, blk)

                            def form(dve, h, s, ps, cols, S_, o, blk):
                                for b in range(NB):
                                    combine(dve, b, ps, cols, S_, blk)
                                    v.tensor_tensor(h[:, blk(b)], acc[:, blk(b)], xT[:, blk(b)], ALU.add
                                                    ).then_inc(S_("h"), 1)
                            node_stage("n2_", 0, "gcn", sb, pb, acc, dict(cols=b2[1], pre=pre, form=form))

        def scatter_edges(ew, sb, pb):
            tag = "s_"
            v, a = nc.vector, nc.scalar
            Sw = sb("Sw", [P, 2, 4, P])
            same = sb("same", [P, 2, 4, P])
            before = sb("before", [P, P])
            ahead = sb("ahead", [P, 4, P])
            cnt = sb("cnt", [P, 4])
            part_i = sb("part_i", [P, 1], i32)
            own_row = sb("own_row", [P, 1])
            src_f = sb("src_f", [P, T])
            src_d = sb("src_d", [P, T])
            srcb = sb("srcb", [P, 2, 4 * P], i32)
            hwin = sb("hwin", [P, 2, 4, D])
            Gs = sb("Gs", [P, 2, 4, P])
            ys = sb("ys", [P, TG, D])
            idx = sb("idx", [P, TG], i32)
            now = {k: sb(k + "_now", [P, TG]) for k in ("rel", "ew", "src", "srd")}
            pG = [pb(f"pG{i}", [P, 4, P]) for i in range(2)]
            pY = [pb(f"pY{i}", [P, 4, D]) for i in range(2)]
            quad = lambda g, q: g * QG + q
            skip = lambda g: isinstance(g, int) and g == 0

            def groups(eng, group):
                group(0)
                with eng.Fori(1, GROUPS) as g:
                    group(g)

            with nc.Block() as block:
                @block.gpsimd
                def _(pool):
                    nc.gpsimd.iota(part_i[:, :], pattern=[[0, 1]], base=NPAD, channel_multiplier=1
                                   ).then_inc(sem(tag + "iota"), 1)

                    def group(g):
                        for q in range(QG):
                            n = quad(g, q)
                            pool.wait_ge(sem(tag + "y_out"), n + 1)
                            pool.wait_ge(sem(tag + "idx"), n + 1)
                            settle(pool)
                            if not (skip(g) and q < 2):
                                pool.wait_ge(sem(f"{tag}added{(q - 2) % QG}"), 64 * (g + (1 if q >= 2 else 0)))
                                settle(pool)
                            for j in range(4):
                                t = 4 * q + j
                                nc.gpsimd.indirect_dma_start(
                                    sum_tab[q % 2 * 4 + j], bass.IndirectOffsetOnAxis(ap=idx[:, t:t + 1], axis=0),
                                    ys[:, t, :], None, compute_op=ALU.add).then_inc(sem(f"{tag}added{q}"), 16)
                    groups(pool, group)
                    for q in range(QG):
                        pool.wait_ge(sem(f"{tag}added{q}"), 64 * GROUPS)

                @block.sync
                def _(sp):
                    def group(g):
                        for q in range(QG):
                            n = quad(g, q)
                            at = bases(sp, g * TG + 4 * q)
                            if not (skip(g) and q < 2):
                                sp.wait_ge(sem(tag + "y"), n - 1)
                                settle(sp)
                                sp.wait_ge(sem(tag + "cnt"), n - 1)
                                settle(sp)
                            for j in range(4):
                                sp.dma_start(hwin[:, q % 2, j, :], h_tab[ds(at[j], P), :]
                                             ).then_inc(sem(f"{tag}in{q % 2}"), 16)
                            sp.dma_start(srcb[:, q % 2, :], src_row[:, ds((g * TG + 4 * q) * P, 4 * P)].to_broadcast([P, 4 * P])
                                         ).then_inc(sem(f"{tag}in{q % 2}"), 16)
                    groups(sp, group)

                @block.tensor
                def _(pe):
                    def group(g):
                        for q in range(QG):
                            n = quad(g, q)
                            pe.wait_ge(sem(tag + "built"), n + 1)
                            if not (skip(g) and q < 2):
                                pe.wait_ge(sem(tag + "g_out"), n - 1)
                            for j in range(4):
                                last = nc.tensor.matmul(pG[q % 2][:, j, :], Sw[:, q % 2, j, :], same[:, q % 2, j, :],
                                                        start=True, stop=True)
                            last.then_inc(sem(tag + "g"), 1)
                            pe.wait_ge(sem(tag + "g_out"), n + 1)
                            pe.wait_ge(sem(f"{tag}in{q % 2}"), 80 * (g * (QG // 2) + q // 2 + 1))
                            if not (skip(g) and q < 2):
                                pe.wait_ge(sem(tag + "y_out"), n - 1)
                            for j in range(4):
                                last = nc.tensor.matmul(pY[q % 2][:, j, :], Gs[:, q % 2, j, :], hwin[:, q % 2, j, :],
                                                        start=True, stop=True)
                            last.then_inc(sem(tag + "y"), 1)
                    groups(pe, group)

                @block.scalar
                def _(act):
                    def group(g):
                        for q in range(QG):
                            n = quad(g, q)
                            act.wait_ge(sem(tag + "g"), n + 1)
                            if not (skip(g) and q < 2):
                                act.wait_ge(sem(tag + "y"), n - 1)
                            a.activation(Gs[:, q % 2, :, :], pG[q % 2][:, :, :], ACT.Copy).then_inc(sem(tag + "g_out"), 1)
                            act.wait_ge(sem(tag + "y"), n + 1)
                            if not skip(g):
                                act.wait_ge(sem(f"{tag}added{q}"), 64 * g)
                            a.activation(ys[:, 4 * q:4 * q + 4, :], pY[q % 2][:, :, :], ACT.Copy).then_inc(sem(tag + "y_out"), 1)
                    groups(act, group)

                @block.vector
                def _(dve):
                    def group(g):
                        take_group(dve, tag, 0, g, [(now["rel"][:, :], rel, 1), (now["ew"][:, :], ew, 1),
                                                    (now["src"][:, :], src_f, 1), (now["srd"][:, :], src_d, 1)])
                        for q in range(QG):
                            n = quad(g, q)
                            dve.wait_ge(sem(f"{tag}in{q % 2}"), 80 * (g * (QG // 2) + q // 2 + 1))
                            if not (skip(g) and q < 2):
                                dve.wait_ge(sem(tag + "g"), n - 1)
                            for j in range(4):
                                t = 4 * q + j
                                v.tensor_scalar(Sw[:, q % 2, j, :], iota_row[:, :], now["rel"][:, t:t + 1],
                                                now["ew"][:, t:t + 1], ALU.is_equal, ALU.mult)
                                last = v.tensor_scalar(same[:, q % 2, j, :], srcb[:, q % 2, j * P:(j + 1) * P],
                                                       now["src"][:, t:t + 1], None, ALU.is_equal)
                            last.then_inc(sem(tag + "built"), 1)
                            dve.wait_ge(sem(tag + "built"), n + 1)
                            if not (skip(g) and q == 0):
                                dve.wait_ge(sem(tag + "cnt"), n)
                            v.tensor_tensor(ahead[:, :, :], same[:, q % 2, :, :],
                                            before[:, :].unsqueeze(1).to_broadcast([P, 4, P]), ALU.mult
                                            ).then_inc(sem(tag + "ahead"), 1)
                            dve.wait_ge(sem(tag + "ahead"), n + 1)
                            if not (skip(g) and q == 0):
                                dve.wait_ge(sem(tag + "first"), n)
                            v.tensor_reduce(cnt[:, :], ahead[:, :, :], AX.X, ALU.add).then_inc(sem(tag + "cnt"), 1)
                            dve.wait_ge(sem(tag + "cnt"), n + 1)
                            v.scalar_tensor_tensor(out=cnt[:, :], in0=cnt[:, :], scalar=0.0,
                                                   in1=now["srd"][:, 4 * q:4 * q + 4], op0=ALU.is_equal,
                                                   op1=ALU.mult).then_inc(sem(tag + "first"), 1)
                            dve.wait_ge(sem(tag + "first"), n + 1)
                            if not skip(g):
                                dve.wait_ge(sem(f"{tag}added{q}"), 64 * g)
                            v.tensor_scalar(idx[:, 4 * q:4 * q + 4], cnt[:, :], own_row[:, :], None, ALU.add
                                            ).then_inc(sem(tag + "idx"), 1)
                            dve.wait_ge(sem(tag + "idx"), n + 1)
                            settle(dve)
                    dve.wait_ge(sem(tag + "iota"), 1)
                    v.tensor_copy(own_row[:, :], part_i[:, :])
                    v.tensor_copy(src_f[:, :], src_all[:, :]).then_inc(sem(tag + "prep"), 1)
                    dve.wait_ge(sem(tag + "prep"), 1)
                    v.tensor_scalar(before[:, :], iota_row[:, :], float(NPAD), own_row[:, :], ALU.add, ALU.is_lt)
                    v.tensor_scalar(src_d[:, :], src_f[:, :], own_row[:, :], None, ALU.subtract).then_inc(sem(tag + "prep"), 1)
                    dve.wait_ge(sem(tag + "prep"), 2)
                    groups(dve, group)

        def scatter_layer():
            v = nc.vector
            tag = "w_"
            with ExitStack() as keep:
                wide = maker(keep, nc.sbuf_tensor, "_w")
                w, ew, zero = wide("w", [P, D]), wide("ew", [P, T]), wide("zero", [P, 4, D])
                with nc.Block() as block:
                    @block.vector
                    def _(dve):
                        v.memset(zero[:, :, :], 0.0).then_inc(sem("w_zero"), 1)

                    @block.sync
                    def _(sp):
                        sp.dma_start(w[:, :], w3).then_inc(sem("w_in"), 16)
                        sp.dma_start(ew[:, :], ew_c).then_inc(sem("w_in"), 16)
                        sp.wait_ge(sem("w_zero"), 1)
                        for tab in sum_tab:
                            for b in range(NB):
                                sp.dma_start(tab[b * BW:(b + 1) * BW, :].rearrange("(j p) f -> p j f", p=P), zero[:, :, :]
                                             ).then_inc(sem("w_in"), 16)
                            sp.dma_start(tab[NPAD:NPAD + P, :], zero[:, 0, :]).then_inc(sem("w_in"), 16)
                        sp.wait_ge(sem("w_in"), 16 * (2 + 8 * (NB + 1)))
                with ExitStack() as part:
                    plain_project(tag + "p", xT, w, None, maker(part, nc.sbuf_tensor, tag), maker(part, nc.psum_tensor, tag))
                with ExitStack() as part:
                    scatter_edges(ew, maker(part, nc.sbuf_tensor, tag), maker(part, nc.psum_tensor, tag))
                with ExitStack() as part:
                    sb = maker(part, nc.sbuf_tensor, tag)
                    parts = sb("parts", [P, 2, 8, 4, D])

                    def fetch(sp, S_):
                        for b in range(NB):
                            if b >= 2:
                                sp.wait_ge(S_("summed"), b - 1)
                            for k in range(8):
                                sp.dma_start(parts[:, b % 2, k, :, :],
                                             sum_tab[k][b * BW:(b + 1) * BW, :].rearrange("(j p) f -> p j f", p=P)
                                             ).then_inc(S_(f"parts{b % 2}"), 16)

                    def pre(eng, what, ps, S_, o, blk):
                        if what != "tensor":
                            return
                        for b in range(NB):
                            eng.wait_ge(S_(f"parts{b % 2}"), 128 * (b // 2 + 1))
                            if b >= 3:
                                eng.wait_ge(S_("z"), 2 * (b - 3) + 1)
                            for j in range(4):
                                for k in range(8):
                                    last = nc.tensor.matmul(ps[b % 3][:, j * P:(j + 1) * P], parts[:, b % 2, k, j, :],
                                                            ident[:, :], start=k == 0, stop=k == 7)
                            last.then_inc(S_("summed"), 1)

                    def form(dve, h, s, ps, cols, S_, o, blk):
                        for b in range(NB):
                            t = h[:, blk(b)]
                            dve.wait_ge(S_("summed"), b + 1)
                            v.tensor_scalar(t, ps[b % 3][:, :], cols[:, 0:1], None, ALU.add).then_inc(S_("z"), 1)
                            dve.wait_ge(S_("z"), 2 * b + 1)
                            v.scalar_tensor_tensor(out=t, in0=t, scalar=0.01, in1=t, op0=ALU.mult, op1=ALU.max
                                                   ).then_inc(S_("z"), 1)
                            dve.wait_ge(S_("z"), 2 * b + 2)
                            v.tensor_tensor(t, t, xT[:, blk(b)], ALU.add).then_inc(S_("h"), 1)
                    node_stage("n3_", 0, "weighted", sb, maker(part, nc.psum_tensor, tag), None,
                               dict(cols=b3, pre=pre, form=form, fetch=fetch))

        with nc.Fori(0, CONVS - 1) as l:
            conv_layer(l, "conv")
        conv_layer(CONVS - 1, "last")
        recycle()
        with ExitStack() as scope:
            dinv_f = scope.enter_context(nc.sbuf_tensor("dinv_f", [P, NPAD], f32))
            dinv_n = scope.enter_context(nc.sbuf_tensor("dinv_n", [P, NT], f32))
            rel_layer(dinv_f, dinv_n)
            recycle()
            gcn_layer(dinv_f, dinv_n)
            recycle()
        scatter_layer()
        with nc.Block() as block:
            @block.sync
            def _(sp):
                sp.dma_start(out, xT[:, 0:N]).then_inc(sem("stored"), 16)
                sp.wait_ge(sem("stored"), 16)


_INS = ["xT_in", "src_c", "src_row", "dst_c", "dst_row", "prev_row", "next_row", "first_row", "first_next", "last_row",
        "last_prev", "type_c", "type_r", "ew_c", "w0", "b0", "col0", "w1", "w1T", "a1", "w2", "b2", "w3", "b3"]


def kernel(**inputs):
    import numpy as np
    import concourse.bacc as bacc
    from concourse import mybir as mb
    from concourse.bass_utils import run_bass_kernel_spmd as run

    z = {k: np.asarray(v) for k, v in inputs.items()}
    pad = T * P - EDGES
    src = np.concatenate([z["src"], np.zeros(pad, np.int32)])
    dst = np.concatenate([z["dst"], np.full(pad, N, np.int32)])
    typ = np.concatenate([z["edge_type_4"], np.zeros(pad, np.int32)])
    ew = np.concatenate([z["edge_weight"], np.zeros(pad, np.float32)])
    prev = np.concatenate([np.full(1, -1, np.int32), dst[:-1]])
    nxt = np.concatenate([dst[1:], np.full(1, -1, np.int32)])

    def cols(a):
        return a.reshape(T, P).T

    def rows(a):
        return a.reshape(GROUPS, TG, P).transpose(1, 0, 2).reshape(TG, GROUPS * P)

    ln_g = np.concatenate([z["L0_gnn_ln_g"], np.ones((1, D), np.float32)])
    ln_b = np.concatenate([z["L0_gnn_ln_b"], np.zeros((1, D), np.float32)])
    a1 = np.zeros((R, 2, H, D), np.float32)
    for h in range(H):
        a1[:, :, h, h * HD:(h + 1) * HD] = z["L1_gnn_attn"].reshape(R, H, 2, HD)[:, h]
    zero = np.zeros((D, 2), np.float32)
    arrays = {
        "xT_in": np.concatenate([z["x"], np.zeros((NPAD - N, D), np.float32)]).T,
        "src_c": cols(src), "src_row": src.reshape(1, T * P), "dst_c": cols(dst), "dst_row": rows(dst), "prev_row": rows(prev), "next_row": rows(nxt),
        "first_row": dst[0::P].reshape(1, T), "first_next": np.concatenate([dst[P::P], [-1]]).reshape(1, T).astype(np.int32),
        "last_row": dst[P - 1::P].reshape(1, T), "last_prev": prev[0::P].reshape(1, T),
        "type_c": cols(typ), "type_r": rows(typ), "ew_c": cols(ew),
        "w0": np.concatenate([z["L0_gnn_Wk"], z["L0_gnn_Wv"], z["L0_gnn_Wq"], z["L0_gnn_Ws"]], axis=2),
        "b0": np.concatenate([z["L0_gnn_bk"], z["L0_gnn_bv"], z["L0_gnn_bq"]], axis=1),
        "col0": np.stack([z["L0_gnn_bs"], ln_g, ln_b], axis=2),
        "w1": z["L1_gnn_W"].transpose(1, 0, 2), "w1T": z["L1_gnn_W"].transpose(2, 0, 1),
        "a1": a1.transpose(3, 0, 1, 2),
        "w2": np.stack([z["L2_gnn_W1"], z["L2_gnn_W2"]]),
        "b2": np.stack([np.concatenate([z["L2_gnn_b1"][:, None], zero], 1), np.concatenate([z["L2_gnn_b2"][:, None], zero], 1)]),
        "w3": z["L3_gnn_weight"], "b3": np.concatenate([z["L3_gnn_bias"][:, None], zero], 1),
    }
    arrays = {k: np.ascontiguousarray(v) for k, v in arrays.items()}
    nc = bacc.Bacc("TRN2", target_bir_lowering=False, num_devices=1)
    args = [nc.dram_tensor("in_" + k, arrays[k].shape, mb.dt.from_np(arrays[k].dtype), kind="ExternalInput").ap()
            for k in _INS]
    args.append(nc.dram_tensor("out_0", (D, N), mb.dt.float32, kind="ExternalOutput").ap())
    gnn_kernel(nc, *args)
    r = run(nc, [{"in_" + k: v for k, v in arrays.items()}], core_ids=[0])
    return np.ascontiguousarray(r.results[0]["out_0"].T)
```

```python
import concourse.bass as bass
from concourse import mybir
from contextlib import ExitStack

NEG = -1.0e30
P = 128
N = 3125
D = 128
H = 4
HD = D // H
R = 4
CONVS = 5
EDGES = 53125
TG = 32
QG = TG // 4
GROUPS = -(-EDGES // (P * TG))
T = GROUPS * TG
BW = 512
NB = -(-(N + P) // BW)
NPAD = NB * BW
ROW = H * (TG + 1)
RW = D + 2 * H
NT = NPAD // P
SCALE = 1.0 / float(HD) ** 0.5
EPS = 1.0e-5


def gnn_kernel(nc, xT_in, src_c, src_row, dst_c, dst_row, prev_row, next_row, first_row, first_next, last_row,
               last_prev, type_c, type_r, ew_c, w0, b0, col0, w1, w1T, a1, w2, b2, w3, b3, out):
    f32, i32, bf16 = mybir.dt.float32, mybir.dt.int32, mybir.dt.bfloat16
    ALU, ACT, AX = mybir.AluOpType, mybir.ActivationFunctionType, mybir.AxisListType
    ds = bass.ds

    kv_tab = nc.dram_tensor("kv_tab", [NPAD, 2 * D], f32).ap()
    q_tab = nc.dram_tensor("q_tab", [NPAD, D], f32).ap()
    rel_tab = nc.dram_tensor("rel_tab", [R * NPAD, RW], f32).ap()
    adst_tab = nc.dram_tensor("adst_tab", [NPAD, R * H], f32).ap()
    h_tab = nc.dram_tensor("h_tab", [NPAD, D], f32).ap()

    sum_tab = [nc.dram_tensor(f"sum_tab{k}", [NPAD + P, D], f32).ap() for k in range(8)]

    root = ExitStack()
    sems = {}

    def sem(name):
        if name not in sems:
            sems[name] = nc.alloc_semaphore(name)
        return sems[name]

    def recycle():
        kept = [n for n in sems if n.startswith(("rows", "settled"))]
        nc.clear_and_free_semaphores([s for n, s in sems.items() if n not in kept])
        for n in list(sems):
            if n not in kept:
                del sems[n]
        with nc.Block():
            pass

    def settle(eng):
        eng.sem_inc(sem(f"settled_{eng.engine.name}"), 1)

    def bases(eng, first):
        _, v = nc.values_load_multi_w_load_instructions(
            base_i[0:1, ds(first, 4)], engines=[eng.engine], min_val=0, max_val=N,
            skip_runtime_bounds_check_because="a destination is at most N, the one of the padding")
        return v

    with root:
        def gsb(name, shape, dt=f32):
            return root.enter_context(nc.sbuf_tensor(name, shape, dt))

        xT = gsb("xT", [P, NPAD])
        src_all = gsb("src_all", [P, T], i32)
        base_i = gsb("base_i", [1, T], i32)
        rel = gsb("rel", [P, T])
        iota_row = gsb("iota_row", [P, P])
        ident = gsb("ident", [P, P])
        ones = gsb("ones", [P, P])
        mean_w = gsb("mean_w", [P, P])
        head_sel = gsb("head_sel", [P, P])
        eps_col = gsb("eps_col", [P, 1])
        rstF = gsb("rstF", [P, GROUPS * P], bf16)
        rstB = gsb("rstB", [P, GROUPS * P], bf16)
        rowrF = gsb("rowrF", [R, GROUPS * H * (TG + 1)], bf16)
        rowrB = gsb("rowrB", [R, GROUPS * H * (TG + 1)], bf16)

        with ExitStack() as scope:
            def sb(name, shape, dt=f32):
                return scope.enter_context(nc.sbuf_tensor(name, shape, dt))

            dst_ci = sb("dst_ci", [P, T], i32)
            first_b = sb("first_b", [P, T], i32)
            dst_f = sb("dst_f", [P, T])
            first_f = sb("first_f", [P, T])
            seg_i = sb("seg_i", [P, 3, GROUPS * P], i32)
            seg_f = sb("seg_f", [P, 3, GROUPS * P])
            edge_i = sb("edge_i", [R, 4, T], i32)
            edge_f = sb("edge_f", [R, 4, T])
            iota_i = sb("iota_i", [P, P], i32)
            part_i = sb("part_i", [P, P], i32)
            part_f = sb("part_f", [P, P])
            in_sem = sem("setup_in")
            iota_done = sem("setup_iota")
            ch = sem("setup_chain")
            with nc.Block() as block:
                @block.sync
                def _(sp):
                    sp.dma_start(xT[:, :], xT_in).then_inc(in_sem, 16)
                    sp.dma_start(src_all[:, :], src_c).then_inc(in_sem, 16)
                    sp.dma_start(dst_ci[:, :], dst_c).then_inc(in_sem, 16)
                    sp.dma_start(base_i[:, :], first_row).then_inc(in_sem, 16)
                    sp.dma_start(first_b[:, :], first_row.to_broadcast([P, T])).then_inc(in_sem, 16)
                    for h in range(H):
                        for k, rows in enumerate((dst_row, prev_row, next_row)):
                            sp.dma_start(seg_i[h * TG:(h + 1) * TG, k, :], rows).then_inc(in_sem, 16)
                    for k, row in enumerate((first_row, first_next, last_row, last_prev)):
                        sp.dma_start(edge_i[:, k, :], row.to_broadcast([R, T])).then_inc(in_sem, 16)

                @block.gpsimd
                def _(pool):
                    nc.gpsimd.iota(iota_i[:, :], pattern=[[1, P]], base=0, channel_multiplier=0)
                    nc.gpsimd.iota(part_i[:, :], pattern=[[0, P]], base=0,
                                   channel_multiplier=1).then_inc(iota_done, 1)

                @block.vector
                def _(dve):
                    v = nc.vector
                    n = [0]

                    def link(ins):
                        n[0] += 1
                        ins.then_inc(ch, 1)
                        dve.wait_ge(ch, n[0])

                    v.memset(ones[:, :], 1.0)
                    v.memset(mean_w[:, :], 1.0 / D)
                    v.memset(eps_col[:, :], EPS)
                    v.memset(rowrF[:, :], NEG)
                    link(v.memset(rowrB[:, :], NEG))
                    dve.wait_ge(iota_done, 1)
                    v.tensor_copy(iota_row[:, :], iota_i[:, :])
                    link(v.tensor_copy(part_f[:, :], part_i[:, :]))
                    link(v.tensor_tensor(ident[:, :], iota_row[:, :], part_f[:, :], ALU.is_equal))
                    for h in range(H):
                        last = v.tensor_scalar(head_sel[:, h * HD:(h + 1) * HD], part_f[:, 0:HD], float(h * TG),
                                               None, ALU.is_equal)
                    link(last)
                    dve.wait_ge(in_sem, 16 * (5 + 3 * H + 4))
                    v.tensor_copy(dst_f[:, :], dst_ci[:, :])
                    v.tensor_copy(seg_f[:, :, :], seg_i[:, :, :])
                    v.tensor_copy(edge_f[:, :, :], edge_i[:, :, :])
                    link(v.tensor_copy(first_f[:, :], first_b[:, :]))
                    link(v.tensor_tensor(rel[:, :], dst_f[:, :], first_f[:, :], ALU.subtract))
                    def blocks(t, n):
                        return t.rearrange("p (g e) -> p g e", e=n)

                    for o, k in ((blocks(rstF[:, :], P), 1), (blocks(rstB[:, :], P)[:, :, ::-1], 2)):
                        link(v.tensor_tensor(o, blocks(seg_f[:, 0, :], P), blocks(seg_f[:, k, :], P), ALU.not_equal))
                    for o in (rstF, rstB):
                        link(v.tensor_scalar(o[:, :], o[:, :], NEG, None, ALU.mult))
                    for o, a, b in ((blocks(rowrF[:, :], ROW), 2, 3), (blocks(rowrB[:, :], ROW)[:, :, ::-1], 0, 1)):
                        for h in range(H):
                            at = h * (TG + 1) + (1 if a == 2 else 0)
                            link(v.tensor_tensor(o[:, :, at:at + TG], blocks(edge_f[:, a, :], TG),
                                                 blocks(edge_f[:, b, :], TG), ALU.not_equal))
                            link(v.tensor_scalar(o[:, :, at:at + TG], o[:, :, at:at + TG], NEG, None, ALU.mult))

        def softmax_buffers(sb, C):
            return dict(C=C, L=sb("sm_L", [P, P]), Lc=sb("sm_Lc", [P, C, P] if C > 1 else [P, 1]),
                        pen=sb("sm_pen", [P, C, P] if C > 1 else [P, 1]), F=sb("sm_F", [P, C, P]),
                        B=sb("sm_B", [P, C, P]), rowF=sb("sm_rowF", [C, H, TG + 1]),
                        rowB=sb("sm_rowB", [C, H, TG + 1]), CF=sb("sm_CF", [C, H, TG + 1]),
                        CB=sb("sm_CB", [C, H, TG + 1]), ini_row=sb("sm_ini_row", [C, 2, P]),
                        ini=sb("sm_ini", [P, 2, C]), m=sb("sm_m", [P, P]), d=sb("sm_d", [P, P]), ex=sb("sm_ex", [P, P]),
                        df=sb("sm_df", [P, C]), f=sb("sm_f", [P, C]), alpha=sb("alpha", [P, 2, H, TG]),
                        exE=sb("exE", [P, 2, H, TG]))

        CHAIN = {1: 9, R: 14}
        LAG = QG + 4

        def linker(dve, tag, C, G, n):
            count = [n]

            def link(ins):
                count[0] += 1
                ins.then_inc(sem(tag + "sm_chain"), 1)
                dve.wait_ge(sem(tag + "sm_chain"), G * CHAIN[C] + count[0])
            return link

        def segment_scans(b, c, g, starts):
            v = nc.vector
            data = b["Lc"][:, c, :] if b["C"] > 1 else b["L"][:, :]
            v.tensor_tensor_scan(out=b["F"][:, c, :], data0=rstF[:, ds(g * P, P)], data1=data, initial=starts[0],
                                 op0=ALU.add, op1=ALU.max)
            return v.tensor_tensor_scan(out=b["B"][:, c, ::-1], data0=rstB[:, ds(g * P, P)], data1=data[:, ::-1],
                                        initial=starts[1], op0=ALU.add, op1=ALU.max)

        def softmax_tails(dve, b, tag, g, G, types):
            v, C = nc.vector, b["C"]
            link = linker(dve, tag, C, G, 0)
            dve.wait_ge(sem(tag + "L_ready"), G + 1)
            if C > 1:
                for c in range(C):
                    last = v.tensor_scalar(b["pen"][:, c, :], types[:, ds(g * P, P)], float(c), NEG, ALU.not_equal, ALU.mult)
                link(last)
                link(v.tensor_tensor(b["Lc"][:, :, :], b["pen"][:, :, :],
                                     b["L"][:, :].unsqueeze(1).to_broadcast([P, C, P]), ALU.add))
            for c in range(C):
                last = segment_scans(b, c, g, (NEG, NEG))
            last.then_inc(sem(tag + "tails_ready"), 1)

        def softmax_carries(dve, b, tag, g, G, pM):
            v, C = nc.vector, b["C"]
            link = linker(dve, tag, C, G, 2 if C > 1 else 0)
            dve.wait_ge(sem(tag + "rows_ready"), G + 1)
            v.tensor_copy(b["rowF"][:, :, 1:TG + 1], pM[0:C, 128:256].rearrange("c (h t) -> c h t", h=H))
            link(v.tensor_copy(b["rowB"][:, :, 0:TG], pM[0:C, 256:384].rearrange("c (h t) -> c h t", h=H)))

            def flat(a):
                return a.rearrange("c h t -> c (h t)")

            v.tensor_tensor_scan(out=flat(b["CF"][:, :, :]), data0=rowrF[0:C, ds(g * ROW, ROW)],
                                 data1=flat(b["rowF"][:, :, :]), initial=NEG, op0=ALU.add, op1=ALU.max)
            link(v.tensor_tensor_scan(out=flat(b["CB"][:, :, :])[:, ::-1], data0=rowrB[0:C, ds(g * ROW, ROW)],
                                      data1=flat(b["rowB"][:, :, :])[:, ::-1], initial=NEG, op0=ALU.add, op1=ALU.max))
            v.tensor_copy(b["rowF"][:, :, 0:1], b["CF"][:, :, TG:TG + 1])
            v.tensor_copy(b["ini_row"][:, 0, :].rearrange("c (h t) -> c h t", h=H), b["CF"][:, :, 0:TG])
            link(v.tensor_copy(b["ini_row"][:, 1, :].rearrange("c (h t) -> c h t", h=H), b["CB"][:, :, 1:TG + 1]))
            dve.sem_inc(sem(tag + "ini_rows"), 1)

        def softmax_maxima(dve, b, tag, g, G, pM):
            v, C, F, B = nc.vector, b["C"], b["F"], b["B"]
            link = linker(dve, tag, C, G, 5 if C > 1 else 3)
            dve.wait_ge(sem(tag + "ini_ready"), G + 1)
            link(v.tensor_copy(b["ini"][:, :, :], pM[:, 384:384 + 2 * C].rearrange("p (k c) -> p k c", k=2)))
            for c in range(C):
                last = segment_scans(b, c, g, (b["ini"][:, 0, c:c + 1], b["ini"][:, 1, c:c + 1]))
            link(last)
            link(v.tensor_tensor(F[:, :, :], F[:, :, :], B[:, :, :], ALU.max))
            link(v.tensor_tensor(b["df"][:, :], b["ini"][:, 0, :], F[:, :, 0:1].rearrange("p c o -> p (c o)"), ALU.subtract))
            link(v.tensor_scalar(b["df"][:, :], b["df"][:, :], 0.0, None, ALU.min))
            top = F[:, 0, :]
            if C > 1:
                link(v.tensor_tensor(F[:, :, :], F[:, :, :], b["pen"][:, :, :], ALU.add))
                link(v.tensor_tensor(B[:, 0:2, :], F[:, 0:2, :], F[:, 2:4, :], ALU.max))
                link(v.tensor_tensor(b["m"][:, :], B[:, 0, :], B[:, 1, :], ALU.max))
                top = b["m"][:, :]
            link(v.tensor_tensor(b["d"][:, :], b["L"][:, :], top, ALU.subtract))
            dve.sem_inc(sem(tag + "d_ready"), 1)

        def turn_alpha(pe, b, tag, par, G, pM):
            pe.wait_ge(sem(tag + "alpha"), (G + 1) * QG)
            nc.tensor.transpose(pM[:, 0:128], b["alpha"][:, par, :, :].rearrange("p h t -> p (h t)"),
                                ident[:, :]).then_inc(sem(tag + "lt"), 1)

        def turn_tails(pe, b, tag, G, pM):
            C = b["C"]
            pe.wait_ge(sem(tag + "tails_ready"), G + 1)
            nc.tensor.matmul(pM[0:C, 128:256], b["F"][:, :, P - 1], ident[:, :], start=True, stop=True)
            nc.tensor.matmul(pM[0:C, 256:384], b["B"][:, :, 0], ident[:, :], start=True,
                             stop=True).then_inc(sem(tag + "rows_ready"), 1)

        def turn_carries(pe, b, tag, G, pM):
            C = b["C"]
            pe.wait_ge(sem(tag + "ini_rows"), G + 1)
            nc.tensor.matmul(pM[:, 384:384 + C], b["ini_row"][:, 0, :], ident[0:C, 0:C], start=True, stop=True)
            nc.tensor.matmul(pM[:, 384 + C:384 + 2 * C], b["ini_row"][:, 1, :], ident[0:C, 0:C], start=True,
                             stop=True).then_inc(sem(tag + "ini_ready"), 1)

        def copy_alpha(act, b, tag, G, pM):
            act.wait_ge(sem(tag + "lt"), G + 1)
            nc.scalar.activation(b["L"][:, :], pM[:, 0:128], ACT.Copy).then_inc(sem(tag + "L_ready"), 1)

        def exps(act, b, tag, par, G, pX, scale):
            a = nc.scalar
            act.wait_ge(sem(tag + "d_ready"), G + 1)
            a.activation(b["f"][:, :], b["df"][:, :], ACT.Exp, scale=scale)
            a.activation(b["ex"][:, :], b["d"][:, :], ACT.Exp, scale=scale).then_inc(sem(tag + "ex_ready"), 1)
            act.wait_ge(sem(tag + "ex_turned"), G + 1)
            a.activation(b["exE"][:, par, :, :], pX[:, 0:128].rearrange("p (h t) -> p h t", h=H),
                         ACT.Copy).then_inc(sem(tag + "exE"), 1)

        def turn_ex(pe, b, tag, G, pX):
            C = b["C"]
            pe.wait_ge(sem(tag + "ex_ready"), G + 1)
            nc.tensor.matmul(pX[:, 128:128 + C], head_sel[:, :], b["f"][:, :], start=True, stop=True)
            nc.tensor.transpose(pX[:, 0:128], b["ex"][:, :], ident[:, :]).then_inc(sem(tag + "ex_turned"), 1)

        def parts(g, q, par):
            fixed = isinstance(g, int)
            after = (g, q + 1, par) if q < QG - 1 else (g + 1, 0, 1 - par)
            late = (g - 2, q + 4, par) if q < 4 else (g - 1, q - 4, 1 - par)
            if fixed and after[0] >= GROUPS:
                after = None
            if fixed and late[0] < 0:
                late = None
            return after, late

        def started(g):
            return not isinstance(g, int) or 1 <= g <= GROUPS

        def scored(g):
            return not isinstance(g, int) or g < GROUPS

        def halved(g, par):
            return (g - par) // 2

        LAST = GROUPS - 1

        def all_turns(eng, turn):
            def group(g, par):
                for q in range(QG):
                    turn(g, q, par)
            for g in range(3):
                group(g, g % 2)
            with eng.Fori(1, (GROUPS - 1) // 2 - 1) as k:
                group(2 * k + 1, 1)
                group(2 * k + 2, 0)
            group(GROUPS - 2, 1)
            group(LAST, 0)
            for q in range(LAG):
                turn(GROUPS + q // QG, q % QG, (1 + q // QG) % 2)

        def gather_group(pool, tag, l, g, par, tab, idx_all, idx_now, rows, read="alpha", used="msg"):
            if isinstance(g, int) and g < 2:
                pass
            else:
                pool.wait_ge(sem(tag + read), (l * GROUPS + g - 1) * QG)
                settle(pool)
            nc.gpsimd.tensor_copy(idx_now[:, par, :], idx_all[:, ds(g * TG, TG)]).then_inc(sem(tag + "idx"), 1)
            pool.wait_ge(sem(tag + "idx"), l * GROUPS + g + 1)
            settle(pool)
            for q in range(QG):
                if not (isinstance(g, int) and g < 2):
                    pool.wait_ge(sem(tag + used), (l * GROUPS + g - 2) * QG + q + 1)
                    settle(pool)
                for j in range(4):
                    t = 4 * q + j
                    nc.gpsimd.indirect_dma_start(
                        rows[:, par * TG + t, :], None, tab,
                        bass.IndirectOffsetOnAxis(ap=idx_now[:, par, t:t + 1], axis=0)
                    ).then_inc(sem(f"rows{par}_{q}"), 16)

        def take_group(dve, tag, l, g, pairs):
            for now, whole, per in pairs:
                last = nc.vector.tensor_copy(now, whole[:, ds(g * (TG * per), TG * per)])
            last.then_inc(sem(tag + "taken"), 1)
            dve.wait_ge(sem(tag + "taken"), l * GROUPS + g + 1)
            settle(dve)

        def rows_there(eng, turn, half, par, q):
            eng.wait_ge(sem(f"rows{par}_{q}"), 64 * (turn * ((GROUPS + 1) // 2 - par) + half + 1))

        def gather_all(pool, group):
            group(0, 0)
            group(1, 1)
            with pool.Fori(0, (GROUPS - 3) // 2) as k:
                group(2 * k + 2, 0)
                group(2 * k + 3, 1)
            group(GROUPS - 1, 0)

        def conv_project(l, sb, pb):
            w = sb("w", [P, 4 * D])
            brow = sb("brow", [1, 3 * D])
            stage = sb("stage", [P, 2, 4, 3 * D])
            pp = [pb(f"pp{i}", [P, 512]) for i in range(4)]
            loaded, prod, copied = sem("proj_w"), sem("proj_prod"), sem("proj_copied")
            stored = [sem("proj_stored0"), sem("proj_stored1")]
            nt = NPAD // P
            even, odd = (NB + 1) // 2, NB // 2
            with nc.Block() as block:
                @block.sync
                def _(sp):
                    sp.dma_start(w[:, :], w0[ds(l, 1), :, :].rearrange("l p n -> (l p) n")).then_inc(loaded, 16)
                    sp.dma_start(brow[:, :], b0[ds(l, 1), :]).then_inc(loaded, 16)
                    for b in range(NB):
                        sp.wait_ge(copied, l * nt + 4 * (b + 1))
                        rows = slice(b * BW, (b + 1) * BW)
                        sp.dma_start(kv_tab[rows, :].rearrange("(j p) f -> p j f", p=P),
                                     stage[:, b % 2, :, 0:2 * D]).then_inc(stored[b % 2], 16)
                        sp.dma_start(q_tab[rows, :].rearrange("(j p) f -> p j f", p=P),
                                     stage[:, b % 2, :, 2 * D:3 * D]).then_inc(stored[b % 2], 16)
                    sp.wait_ge(stored[0], (l + 1) * 32 * even)
                    settle(sp)
                    sp.wait_ge(stored[1], (l + 1) * 32 * odd)
                    settle(sp)

                @block.tensor
                def _(pe):
                    pe.wait_ge(loaded, 32 * (l + 1))
                    for t in range(nt):
                        if t >= 4:
                            pe.wait_ge(copied, l * nt + t - 3)
                        nc.tensor.matmul(pp[t % 4][:, 0:3 * D], xT[:, t * P:(t + 1) * P], w[:, 0:3 * D],
                                         start=True, stop=False)
                        nc.tensor.matmul(pp[t % 4][:, 0:3 * D], ones[0:1, :], brow[:, :], start=False,
                                         stop=True).then_inc(prod, 1)

                @block.scalar
                def _(act):
                    for t in range(nt):
                        b = t // 4
                        if t % 4 == 0 and b >= 2:
                            n = even if b % 2 == 0 else odd
                            act.wait_ge(stored[b % 2], l * 32 * n + 32 * (b // 2))
                        act.wait_ge(prod, l * nt + t + 1)
                        nc.scalar.activation(stage[:, b % 2, t % 4, :], pp[t % 4][:, 0:3 * D],
                                             ACT.Copy).then_inc(copied, 1)
            return w

        def conv_edges(l, sb, pb, acc):
            tag = "c_"
            kv = sb("kv", [P, 2 * TG, 2 * D])
            S = sb("S", [P, 2 * TG, P])
            ST = sb("ST", [P, 2, 4, P])
            qwin = sb("qwin", [P, 2, 4, D])
            prodb = sb("prodb", [P, 4, D])
            exb = sb("exb", [P, 2, 4, D])
            msg = sb("msg", [P, 2, 4, D])
            idx_now = sb("idx_now", [P, 2, TG], i32)
            rel_now = sb("rel_now", [P, TG])
            sm = softmax_buffers(sb, 1)
            pT = [pb(f"pT{i}", [P, 4, P]) for i in range(2)]
            pQ = [pb(f"pQ{i}", [P, 4, D]) for i in range(2)]
            pA = [pb(f"pA{i}", [P, 2, 2, P]) for i in range(2)]
            pM = pb("pM", [P, 512])
            pX = pb("pX", [P, 512])

            def quad(g, q):
                return (l * GROUPS + g) * QG + q

            def skip(g):
                return isinstance(g, int) and g == 0

            with nc.Block() as block:
                @block.gpsimd
                def _(pool):
                    gather_all(pool, lambda g, par: gather_group(pool, tag, l, g, par, kv_tab, src_all, idx_now, kv))

                @block.sync
                def _(sp):
                    def group(g, par):
                        for q in range(QG):
                            n = quad(g, q)
                            at = bases(sp, g * TG + 4 * q)
                            if not (skip(g) and q < 2):
                                sp.wait_ge(sem(tag + "qx"), n - 1)
                                settle(sp)
                            for j in range(4):
                                sp.dma_start(qwin[:, q % 2, j, :], q_tab[ds(at[j], P), :]
                                             ).then_inc(sem(f"{tag}qwin{q % 2}"), 16)
                    group(0, 0)
                    with sp.Fori(1, GROUPS) as g:
                        group(g, None)

                @block.tensor
                def _(pe):
                    def scores_turn(g, q, par):
                        n = quad(g, q)
                        pe.wait_ge(sem(tag + "S"), n + 1)
                        if not (skip(g) and q < 2):
                            pe.wait_ge(sem(tag + "ST"), n - 1)
                        for j in range(4):
                            last = nc.tensor.transpose(pT[q % 2][:, j, :], S[:, par * TG + 4 * q + j, :], ident[:, :])
                        last.then_inc(sem(tag + "turned"), 1)

                    def scores(g, q, par):
                        n = quad(g, q)
                        pe.wait_ge(sem(tag + "ST"), n + 1)
                        pe.wait_ge(sem(f"{tag}qwin{q % 2}"), 64 * ((l * GROUPS + g) * (QG // 2) + q // 2 + 1))
                        if not (skip(g) and q < 2):
                            pe.wait_ge(sem(tag + "prod"), n - 1)
                        for j in range(4):
                            last = nc.tensor.matmul(pQ[q % 2][:, j, :], ST[:, q % 2, j, :], qwin[:, q % 2, j, :],
                                                    start=True, stop=True)
                        last.then_inc(sem(tag + "qx"), 1)

                    def sums(g, q, par):
                        m = quad(g, q)
                        pe.wait_ge(sem(tag + "msg"), m + 1)
                        for u in range(2):
                            if not (skip(g) and q == 0):
                                pe.wait_ge(sem(tag + "acc"), 4 * m - 2 + 2 * u)
                            for k in range(2):
                                j = 2 * u + k
                                s = S[:, par * TG + 4 * q + j, :]
                                nc.tensor.matmul(pA[u][:, k, 0, :], msg[:, q % 2, j, :], s, start=True, stop=True)
                                last = nc.tensor.matmul(pA[u][:, k, 1, :], exb[:, q % 2, j, :], s, start=True, stop=True)
                            last.then_inc(sem(tag + "agg"), 1)

                    def turn(g, q, par):
                        after, late = parts(g, q, par)
                        if started(g):
                            G = l * GROUPS + g - 1
                            if q == 0:
                                turn_alpha(pe, sm, tag, 1 - par, G, pM)
                            if q == 1:
                                turn_tails(pe, sm, tag, G, pM)
                            if q == 2:
                                turn_carries(pe, sm, tag, G, pM)
                        if after:
                            scores_turn(*after)
                        if late:
                            sums(*late)
                        if after:
                            scores(*after)
                        if started(g) and q == 3:
                            turn_ex(pe, sm, tag, G, pX)
                    scores_turn(0, 0, 0)
                    scores(0, 0, 0)
                    all_turns(pe, turn)

                @block.scalar
                def _(act):
                    def st_copy(g, q):
                        n = quad(g, q)
                        act.wait_ge(sem(tag + "turned"), n + 1)
                        if not (skip(g) and q < 2):
                            act.wait_ge(sem(tag + "qx"), n - 1)
                        nc.scalar.activation(ST[:, q % 2, :, :], pT[q % 2][:, :, :], ACT.Copy
                                             ).then_inc(sem(tag + "ST"), 1)

                    def spread(g, q, par):
                        m = quad(g, q)
                        if q == 0:
                            act.wait_ge(sem(tag + "exE"), l * GROUPS + g + 1)
                        if not (skip(g) and q < 2):
                            act.wait_ge(sem(tag + "agg"), 2 * (m - 1))
                        src = sm["exE"][:, par, :, 4 * q:4 * q + 4].rearrange("p h t -> p t h")
                        nc.scalar.activation(exb[:, q % 2, :, :].rearrange("p t (h f) -> p t h f", h=H),
                                             src.unsqueeze(3).to_broadcast([P, 4, H, HD]), ACT.Copy
                                             ).then_inc(sem(tag + "exb"), 1)

                    def turn(g, q, par):
                        after, late = parts(g, q, par)
                        G = l * GROUPS + g - 1
                        if started(g) and q == 0:
                            copy_alpha(act, sm, tag, G, pM)
                        if late:
                            spread(*late)
                        if after:
                            st_copy(*after[:2])
                        if started(g) and q == 3:
                            exps(act, sm, tag, 1 - par, G, pX, SCALE)
                    st_copy(0, 0)
                    all_turns(act, turn)

                @block.vector
                def _(dve):
                    v = nc.vector

                    def build(g, q, par):
                        if not (isinstance(g, int) and g < 2):
                            dve.wait_ge(sem(tag + "agg"), 2 * (quad(g, q) - 2 * QG + 1))
                        for j in range(4):
                            last = v.tensor_scalar(S[:, par * TG + 4 * q + j, :], iota_row[:, :],
                                                   rel_now[:, 4 * q + j:4 * q + j + 1], None, ALU.is_equal)
                        last.then_inc(sem(tag + "S"), 1)

                    def weigh(g, q, par):
                        m = quad(g, q)
                        dve.wait_ge(sem(tag + "exb"), m + 1)
                        if not (skip(g) and q < 2):
                            dve.wait_ge(sem(tag + "agg"), 2 * (m - 1))
                        s = par * TG + 4 * q
                        v.tensor_tensor(msg[:, q % 2, :, :], kv[:, s:s + 4, D:2 * D], exb[:, q % 2, :, :],
                                        ALU.mult).then_inc(sem(tag + "msg"), 1)

                    def add(g, q):
                        m = quad(g, q)
                        at = bases(dve, g * TG + 4 * q)
                        for j in range(4):
                            dve.wait_ge(sem(tag + "agg"), 2 * m + j // 2 + 1)
                            if not (skip(g) and q == 0 and j == 0):
                                dve.wait_ge(sem(tag + "acc"), 4 * m + j)
                            win = acc[:, :, ds(at[j], P)]
                            v.tensor_tensor(win, win, pA[j // 2][:, j % 2, :, :], ALU.add).then_inc(sem(tag + "acc"), 1)

                    def score(g, q, par):
                        n = quad(g, q)
                        dve.wait_ge(sem(tag + "qx"), n + 1)
                        rows_there(dve, l, halved(g, par), par, q)
                        s = par * TG + 4 * q
                        if not (skip(g) and q == 0):
                            dve.wait_ge(sem(tag + "alpha"), n)
                        v.tensor_tensor(prodb[:, :, :], kv[:, s:s + 4, 0:D], pQ[q % 2][:, :, :],
                                        ALU.mult).then_inc(sem(tag + "prod"), 1)
                        dve.wait_ge(sem(tag + "prod"), n + 1)
                        v.tensor_reduce(sm["alpha"][:, par, :, 4 * q:4 * q + 4].rearrange("p h t -> p t h"),
                                        prodb[:, :, :].rearrange("p t (h f) -> p t h f", h=H), AX.X,
                                        ALU.add).then_inc(sem(tag + "alpha"), 1)

                    def rescale(g):
                        G = l * GROUPS + g
                        _, at = nc.values_load_multi_w_load_instructions(
                            base_i[0:1, ds(g * TG, 1)], engines=[dve.engine], min_val=0, max_val=N,
                            skip_runtime_bounds_check_because="a destination")
                        dve.wait_ge(sem(tag + "exE"), G + 1)
                        if not skip(g):
                            dve.wait_ge(sem(tag + "acc"), 4 * QG * G)
                        col = acc[:, :, ds(at[0], 1)]
                        v.tensor_scalar(col, col, pX[:, 128:129], None, ALU.mult).then_inc(sem(tag + "scaled"), 1)
                        dve.wait_ge(sem(tag + "scaled"), G + 1)
                        settle(dve)

                    def turn(g, q, par):
                        after, late = parts(g, q, par)
                        G = l * GROUPS + g - 1
                        if after:
                            if after[1] == 0:
                                take_group(dve, tag, l, after[0], [(rel_now[:, :], rel, 1)])
                            build(*after)
                        if late:
                            weigh(*late)
                        if scored(g):
                            score(g, q, par)
                        if late:
                            add(*late[:2])
                        if started(g):
                            if q == 0:
                                softmax_tails(dve, sm, tag, g - 1, G, None)
                            if q == 1:
                                softmax_carries(dve, sm, tag, g - 1, G, pM)
                            if q == 2:
                                softmax_maxima(dve, sm, tag, g - 1, G, pM)
                            if q == 3:
                                rescale(g - 1)

                    v.memset(acc[:, :, :], 0.0).then_inc(sem(tag + "clear"), 1)
                    v.memset(sm["rowF"][:, :, :], NEG)
                    v.memset(sm["rowB"][:, :, :], NEG).then_inc(sem(tag + "clear"), 1)
                    dve.wait_ge(sem(tag + "clear"), 2 * (l + 1))
                    settle(dve)
                    take_group(dve, tag, l, 0, [(rel_now[:, :], rel, 1)])
                    build(0, 0, 0)
                    all_turns(dve, turn)

        def node_stage(tag, l, kind, sb, pb, acc, extra):
            h = sb("ns_h", [P, NPAD])
            s = sb("ns_s", [P, NPAD])
            ps = [pb(f"ns_p{i}", [P, BW]) for i in range(3)]
            pm = [pb(f"ns_m{i}", [P, BW]) for i in range(4)]
            cols = sb("ns_cols", [P, 3])
            w = extra.get("w")
            v, a = nc.vector, nc.scalar
            S_ = lambda n: sem(tag + n)
            o = l * NB
            blk = lambda b: slice(b * BW, (b + 1) * BW)
            attn = kind in ("conv", "last")

            with nc.Block() as block:
                @block.sync
                def _(sp):
                    sp.dma_start(cols[:, :], extra["cols"]).then_inc(S_("cols"), 16)
                    sp.wait_ge(S_("cols"), 16 * (l + 1))
                    settle(sp)
                    if "fetch" in extra:
                        extra["fetch"](sp, S_)
                    if kind == "last":
                        sp.wait_ge(S_("skip"), o + NB)
                        sp.dma_start(xT[:, :], xT_in).then_inc(S_("x_again"), 16)
                        sp.wait_ge(S_("x_again"), 16)

                @block.tensor
                def _(pe):
                    if "pre" in extra:
                        extra["pre"](pe, "tensor", ps, S_, o, blk)
                    for b in range(NB):
                        pe.wait_ge(S_("h"), o + b + 1)
                        if b >= 4:
                            pe.wait_ge(S_("cent"), o + b - 3)
                        nc.tensor.matmul(pm[b % 4][:, :], mean_w[:, :], h[:, blk(b)], start=True,
                                         stop=True).then_inc(S_("mean"), 1)
                    for b in range(NB):
                        pe.wait_ge(S_("sq"), o + b + 1)
                        pe.wait_ge(S_("cent"), o + NB)
                        if b >= 4:
                            pe.wait_ge(S_("sd"), o + b - 3)
                        nc.tensor.matmul(pm[b % 4][:, :], mean_w[:, :], s[:, blk(b)], start=True,
                                         stop=True).then_inc(S_("var"), 1)

                @block.scalar
                def _(act):
                    if "pre" in extra:
                        extra["pre"](act, "scalar", ps, S_, o, blk)
                    for b in range(NB):
                        act.wait_ge(S_("cent"), o + b + 1)
                        a.activation(s[:, blk(b)], h[:, blk(b)], ACT.Square).then_inc(S_("sq"), 1)
                    for b in range(NB):
                        act.wait_ge(S_("var"), o + b + 1)
                        a.activation(s[:, blk(b)], pm[b % 4][:, :], ACT.Sqrt, bias=eps_col[:, :]).then_inc(S_("sd"), 1)
                    if kind == "conv":
                        for b in range(NB):
                            act.wait_ge(S_("cols"), 16 * (l + 1))
                            act.wait_ge(S_("norm"), o + b + 1)
                            a.activation(s[:, blk(b)], h[:, blk(b)], ACT.Gelu, bias=cols[:, 2:3],
                                         scale=cols[:, 1:2]).then_inc(S_("act"), 1)

                @block.vector
                def _(dve):
                    dve.wait_ge(S_("cols"), 16 * (l + 1))
                    extra["form"](dve, h, s, ps, cols, S_, o, blk)
                    for b in range(NB):
                        dve.wait_ge(S_("mean"), o + b + 1)
                        v.tensor_tensor(h[:, blk(b)], h[:, blk(b)], pm[b % 4][:, :], ALU.subtract).then_inc(S_("cent"), 1)
                    for b in range(NB):
                        dve.wait_ge(S_("sd"), o + b + 1)
                        v.reciprocal(s[:, blk(b)], s[:, blk(b)]).then_inc(S_("rs"), 1)
                        dve.wait_ge(S_("rs"), o + b + 1)
                        to = h if kind == "conv" else xT
                        v.tensor_tensor(to[:, blk(b)], h[:, blk(b)], s[:, blk(b)], ALU.mult).then_inc(S_("norm"), 1)
                    if kind == "conv":
                        for b in range(NB):
                            dve.wait_ge(S_("act"), o + b + 1)
                            v.tensor_tensor(xT[:, blk(b)], xT[:, blk(b)], s[:, blk(b)], ALU.add).then_inc(S_("x"), 1)

        def conv_nodes(l, kind, sb, pb, acc, w):
            tag = "n0_"
            v, a = nc.vector, nc.scalar

            def pre(eng, what, ps, S_, o, blk):
                if what == "tensor":
                    for b in range(NB):
                        if b >= 3:
                            eng.wait_ge(S_("sum"), o + b - 2)
                        nc.tensor.matmul(ps[b % 3][:, :], w[:, 3 * D:4 * D], xT[:, blk(b)], start=True,
                                         stop=True).then_inc(S_("skip"), 1)
                elif kind == "last":
                    for b in range(NB):
                        eng.wait_ge(S_("sum"), o + b + 1)
                        a.activation(acc[:, 0, blk(b)], acc[:, 0, blk(b)], ACT.Gelu).then_inc(S_("gelu"), 1)

            def form(dve, h, s, ps, cols, S_, o, blk):
                out_ = acc[:, 0, :] if kind == "last" else h
                for b in range(NB):
                    den, num = acc[:, 1, blk(b)], acc[:, 0, blk(b)]
                    v.tensor_scalar(den, den, 1e-16, None, ALU.add).then_inc(S_("d1"), 1)
                    dve.wait_ge(S_("d1"), 2 * (o + b) + 1)
                    v.reciprocal(den, den).then_inc(S_("d1"), 1)
                    dve.wait_ge(S_("d1"), 2 * (o + b) + 2)
                    v.tensor_tensor(num, num, den, ALU.mult).then_inc(S_("att"), 1)
                for b in range(NB):
                    dve.wait_ge(S_("skip"), o + b + 1)
                    dve.wait_ge(S_("att"), o + b + 1)
                    v.scalar_tensor_tensor(out=out_[:, blk(b)], in0=ps[b % 3][:, :], scalar=cols[:, 0:1],
                                           in1=acc[:, 0, blk(b)], op0=ALU.add, op1=ALU.add
                                           ).then_inc(S_("sum"), 1)
                    if kind == "conv":
                        dve.wait_ge(S_("sum"), o + b + 1)
                        dve.sem_inc(S_("h"), 1)
                if kind == "last":
                    dve.wait_ge(S_("x_again"), 16)
                    for b in range(NB):
                        dve.wait_ge(S_("gelu"), b + 1)
                        v.tensor_tensor(h[:, blk(b)], acc[:, 0, blk(b)], xT[:, blk(b)], ALU.add).then_inc(S_("h"), 1)

            node_stage(tag, l, kind, sb, pb, acc, dict(
                cols=col0[ds(l, 1), :, :].rearrange("l p n -> (l p) n"), pre=pre, form=form))

        def maker(scope, space, suffix):
            return lambda name, shape, dt=f32: scope.enter_context(space(name + suffix, shape, dt))

        def conv_layer(l, kind):
            with ExitStack() as keep:
                acc = maker(keep, nc.sbuf_tensor, kind)("acc", [P, 2, NPAD])
                with ExitStack() as part:
                    wide = maker(keep, nc.sbuf_tensor, kind)
                    narrow = maker(part, nc.sbuf_tensor, kind)
                    w = conv_project(l, lambda name, *a: (wide if name == "w" else narrow)(name, *a),
                                     maker(part, nc.psum_tensor, kind))
                with ExitStack() as part:
                    conv_edges(l, maker(part, nc.sbuf_tensor, kind), maker(part, nc.psum_tensor, kind), acc)
                with ExitStack() as part:
                    conv_nodes(l, kind, maker(part, nc.sbuf_tensor, kind), maker(part, nc.psum_tensor, kind), acc, w)

        def rel_project(sb, pb):
            wcat = sb("wcat", [P, R, RW])
            wt = sb("wt", [P, R, P])
            at = sb("at", [P, R, 2 * H])
            stage = sb("stage", [P, 2, 4, R, RW])
            ad = sb("ad", [P, 2, 4, R * H])
            pw = pb("pw", [P, R, 2 * H])
            pr = [pb(f"pr{i}", [P, 2, RW]) for i in range(4)]
            v, a = nc.vector, nc.scalar
            loaded, folded, put, prod = sem("rp_w"), sem("rp_folded"), sem("rp_put"), sem("rp_prod")
            copied, dsts = sem("rp_copied"), sem("rp_dsts")
            stored = [sem("rp_stored0"), sem("rp_stored1")]
            with nc.Block() as block:
                @block.sync
                def _(sp):
                    sp.dma_start(wcat[:, :, 0:D], w1).then_inc(loaded, 16)
                    sp.dma_start(wt[:, :, :], w1T).then_inc(loaded, 16)
                    sp.dma_start(at[:, :, :], a1.rearrange("o r k h -> o r (k h)")).then_inc(loaded, 16)
                    for b in range(NB):
                        sp.wait_ge(copied, 8 * (b + 1))
                        for r in range(R):
                            first = r * NPAD + b * BW
                            sp.dma_start(rel_tab[first:first + BW, :].rearrange("(j p) f -> p j f", p=P),
                                         stage[:, b % 2, :, r, :]).then_inc(stored[b % 2], 16)
                        sp.wait_ge(dsts, b + 1)
                        sp.dma_start(adst_tab[b * BW:(b + 1) * BW, :].rearrange("(j p) f -> p j f", p=P),
                                     ad[:, b % 2, :, :]).then_inc(stored[b % 2], 16)
                    sp.wait_ge(stored[0], 80 * ((NB + 1) // 2))
                    sp.wait_ge(stored[1], 80 * (NB // 2))

                @block.tensor
                def _(pe):
                    pe.wait_ge(loaded, 48)
                    for r in range(R):
                        last = nc.tensor.matmul(pw[:, r, :], wt[:, r, :], at[:, r, :], start=True, stop=True)
                    last.then_inc(folded, 1)
                    pe.wait_ge(put, 1)
                    for t in range(NT):
                        for u in range(2):
                            n = 2 * t + u
                            if n >= 4:
                                pe.wait_ge(copied, n - 3)
                            nc.tensor.matmul(pr[n % 4][:, :, :], xT[:, t * P:(t + 1) * P], wcat[:, 2 * u:2 * u + 2, :],
                                             start=True, stop=True).then_inc(prod, 1)

                @block.scalar
                def _(act):
                    act.wait_ge(folded, 1)
                    a.activation(wcat[:, :, D:RW], pw[:, :, :], ACT.Copy).then_inc(put, 1)
                    for n in range(2 * NT):
                        b = n // 8
                        if n % 8 == 0 and b >= 2:
                            act.wait_ge(stored[b % 2], 80 * (b // 2))
                            act.wait_ge(dsts, b - 1)
                        act.wait_ge(prod, n + 1)
                        u = n % 2
                        a.activation(stage[:, b % 2, (n // 2) % 4, 2 * u:2 * u + 2, :], pr[n % 4][:, :, :],
                                     ACT.Copy).then_inc(copied, 1)

                @block.vector
                def _(dve):
                    for b in range(NB):
                        dve.wait_ge(copied, 8 * (b + 1))
                        if b >= 2:
                            dve.wait_ge(stored[b % 2], 80 * (b // 2))
                        v.tensor_copy(ad[:, b % 2, :, :].rearrange("p j (r h) -> p j r h", h=H),
                                      stage[:, b % 2, :, :, D + H:RW]).then_inc(dsts, 1)

        def rel_edges(sb, pb, acc, den, type_f, tm, idx1):
            tag = "r_"
            rows = sb("rows", [P, 2 * TG, RW])
            S = sb("S", [P, 2, 4, P])
            S2 = sb("S2", [P, 4, P])
            St = sb("St", [P, 4, R, P])
            ST = sb("ST", [P, 2, 4, P])
            awin = sb("awin", [P, 2, 4, R * H])
            picked = sb("picked", [P, 4, R, H])
            al = sb("al", [P, 4, H])
            exb = sb("exb", [P, 2, 4, D])
            msg = sb("msg", [P, 2, 4, D])
            exm = sb("exm", [P, 2, 4, R * H + 1])
            idx_now = sb("idx_now", [P, 2, TG], i32)
            val_i = sb("val_i", [R * H, R], i32)
            val_f = sb("val_f", [R * H, R])
            csel = sb("csel", [R * H, R])
            hsel = sb("hsel", [P, R, H])
            fac = sb("fac", [R * H, R])
            fac1 = sb("fac1", [R * H, 1])
            rel_now, rel_late = sb("rel_now", [P, TG]), sb("rel_late", [P, TG])
            tm_now, tm_late = sb("tm_now", [P, TG * R]), sb("tm_late", [P, TG * R])
            sm = softmax_buffers(sb, R)
            pT = pb("pT", [P, 4, P])
            pQ = [pb(f"pQ{i}", [P, 4, R * H]) for i in range(2)]
            pA = [pb(f"pA{i}", [P, R, P]) for i in range(2)]
            pD = pb("pD", [R * H + 1, 4, P])
            pM = pb("pM", [P, 512])
            pX = pb("pX", [P, 512])
            quad = lambda g, q: g * QG + q
            skip = lambda g: isinstance(g, int) and g == 0

            with nc.Block() as block:
                @block.gpsimd
                def _(pool):
                    nc.gpsimd.iota(val_i[:, :], pattern=[[-H, R]], base=0, channel_multiplier=1
                                   ).then_inc(sem(tag + "iota"), 1)
                    gather_all(pool, lambda g, par: gather_group(pool, tag, 0, g, par, rel_tab, idx1, idx_now, rows))

                @block.sync
                def _(sp):
                    def group(g):
                        for q in range(QG):
                            n = quad(g, q)
                            at = bases(sp, g * TG + 4 * q)
                            if not (skip(g) and q < 2):
                                sp.wait_ge(sem(tag + "qx"), n - 1)
                                settle(sp)
                            for j in range(4):
                                sp.dma_start(awin[:, q % 2, j, :], adst_tab[ds(at[j], P), :]
                                             ).then_inc(sem(f"{tag}qwin{q % 2}"), 16)
                    group(0)
                    with sp.Fori(1, GROUPS) as g:
                        group(g)

                @block.tensor
                def _(pe):
                    def turn(g, q):
                        n = quad(g, q)
                        pe.wait_ge(sem(tag + "S"), n + 1)
                        if not (skip(g) and q == 0):
                            pe.wait_ge(sem(tag + "ST"), n)
                        for j in range(4):
                            last = nc.tensor.transpose(pT[:, j, :], S[:, q % 2, j, :], ident[:, :])
                        last.then_inc(sem(tag + "turned"), 1)

                    def scores(g, q):
                        n = quad(g, q)
                        pe.wait_ge(sem(tag + "ST"), n + 1)
                        pe.wait_ge(sem(f"{tag}qwin{q % 2}"), 64 * (g * (QG // 2) + q // 2 + 1))
                        if not (skip(g) and q < 2):
                            pe.wait_ge(sem(tag + "prod"), n - 1)
                        for j in range(4):
                            last = nc.tensor.matmul(pQ[q % 2][:, j, :], ST[:, q % 2, j, :], awin[:, q % 2, j, :],
                                                    start=True, stop=True)
                        last.then_inc(sem(tag + "qx"), 1)

                    def sums(g, q):
                        m = quad(g, q)
                        pe.wait_ge(sem(tag + "built"), m + 1)
                        if not (skip(g) and q == 0):
                            pe.wait_ge(sem(tag + "den"), 4 * m)
                        for j in range(4):
                            last = nc.tensor.matmul(pD[:, j, :], exm[:, q % 2, j, :], S2[:, j, :], start=True, stop=True)
                        last.then_inc(sem(tag + "counted"), 1)
                        for j in range(4):
                            if not (skip(g) and q == 0 and j < 2):
                                pe.wait_ge(sem(tag + "acc"), 4 * m + j - 1)
                            nc.tensor.matmul(pA[j % 2][:, :, :], msg[:, q % 2, j, :], St[:, j, :, :], start=True,
                                             stop=True).then_inc(sem(tag + "agg"), 1)

                    def step(g, q, par):
                        after, late = parts(g, q, par)
                        if started(g):
                            if q == 0:
                                turn_alpha(pe, sm, tag, 1 - par, g - 1, pM)
                            if q == 1:
                                turn_tails(pe, sm, tag, g - 1, pM)
                            if q == 2:
                                turn_carries(pe, sm, tag, g - 1, pM)
                        if after:
                            turn(*after[:2])
                            scores(*after[:2])
                        if late:
                            sums(*late[:2])
                        if started(g) and q == 3:
                            pe.wait_ge(sem(tag + "ex_ready"), g)
                            nc.tensor.matmul(pX[0:R * H, 136:136 + R], hsel[:, :, :].rearrange("p c h -> p (c h)"),
                                             sm["f"][:, :], start=True, stop=True)
                            turn_ex(pe, sm, tag, g - 1, pX)
                    pe.wait_ge(sem(tag + "made"), 1)
                    turn(0, 0)
                    scores(0, 0)
                    all_turns(pe, step)

                @block.scalar
                def _(act):
                    def st_copy(g, q):
                        n = quad(g, q)
                        act.wait_ge(sem(tag + "turned"), n + 1)
                        if not (skip(g) and q < 2):
                            act.wait_ge(sem(tag + "qx"), n - 1)
                        nc.scalar.activation(ST[:, q % 2, :, :], pT[:, :, :], ACT.Copy).then_inc(sem(tag + "ST"), 1)

                    def spread(g, q, par):
                        m = quad(g, q)
                        if q == 0:
                            act.wait_ge(sem(tag + "exE"), g + 1)
                        if not (skip(g) and q < 2):
                            act.wait_ge(sem(tag + "built"), m - 1)
                        src = sm["exE"][:, par, :, 4 * q:4 * q + 4].rearrange("p h t -> p t h")
                        nc.scalar.activation(exb[:, q % 2, :, :].rearrange("p t (h f) -> p t h f", h=H),
                                             src.unsqueeze(3).to_broadcast([P, 4, H, HD]), ACT.Copy
                                             ).then_inc(sem(tag + "exb"), 1)

                    def turn(g, q, par):
                        after, late = parts(g, q, par)
                        if started(g) and q == 0:
                            copy_alpha(act, sm, tag, g - 1, pM)
                        if late:
                            spread(*late)
                        if after:
                            st_copy(*after[:2])
                        if started(g) and q == 3:
                            exps(act, sm, tag, 1 - par, g - 1, pX, 1.0)
                    st_copy(0, 0)
                    all_turns(act, turn)

                @block.vector
                def _(dve):
                    v = nc.vector

                    def build(g, q, par):
                        if not (skip(g) and q < 2):
                            dve.wait_ge(sem(tag + "turned"), quad(g, q) - 1)
                        for j in range(4):
                            last = v.tensor_scalar(S[:, q % 2, j, :], iota_row[:, :],
                                                   rel_now[:, 4 * q + j:4 * q + j + 1], None, ALU.is_equal)
                        last.then_inc(sem(tag + "S"), 1)

                    def mask(tm_of, q):
                        return tm_of[:, 4 * q * R:4 * (q + 1) * R].rearrange("p (t c) -> p t c", c=R)

                    def weigh(g, q, par):
                        m = quad(g, q)
                        if not (skip(g) and q == 0):
                            dve.wait_ge(sem(tag + "agg"), 4 * m)
                        for j in range(4):
                            t = 4 * q + j
                            v.tensor_scalar(S2[:, j, :], iota_row[:, :], rel_late[:, t:t + 1], None, ALU.is_equal)
                            for c in range(R):
                                v.tensor_scalar(St[:, j, c, :], iota_row[:, :], rel_late[:, t:t + 1],
                                                tm_late[:, t * R + c:t * R + c + 1], ALU.is_equal, ALU.mult)
                        dve.wait_ge(sem(tag + "exE"), g + 1)
                        ex = sm["exE"][:, par, :, 4 * q:4 * q + 4].rearrange("p h t -> p t h")
                        v.tensor_tensor(exm[:, q % 2, :, 0:R * H].rearrange("p t (c h) -> p t c h", c=R),
                                        ex.unsqueeze(2).to_broadcast([P, 4, R, H]),
                                        mask(tm_late, q).unsqueeze(3).to_broadcast([P, 4, R, H]), ALU.mult)
                        dve.wait_ge(sem(tag + "exb"), m + 1)
                        s = par * TG + 4 * q
                        v.tensor_tensor(msg[:, q % 2, :, :], rows[:, s:s + 4, 0:D], exb[:, q % 2, :, :],
                                        ALU.mult).then_inc(sem(tag + "msg"), 1)
                        dve.wait_ge(sem(tag + "msg"), m + 1)
                        dve.sem_inc(sem(tag + "built"), 1)

                    def add(g, q):
                        m = quad(g, q)
                        at = bases(dve, g * TG + 4 * q)
                        dve.wait_ge(sem(tag + "counted"), m + 1)
                        for j in range(4):
                            if not (skip(g) and q == 0 and j == 0):
                                dve.wait_ge(sem(tag + "den"), 4 * m + j)
                            win = den[:, ds(at[j], P)]
                            v.tensor_tensor(win, win, pD[:, j, :], ALU.add).then_inc(sem(tag + "den"), 1)
                        for j in range(4):
                            dve.wait_ge(sem(tag + "agg"), 4 * m + j + 1)
                            if not (skip(g) and q == 0 and j == 0):
                                dve.wait_ge(sem(tag + "acc"), 4 * m + j)
                            win = acc[:, :, ds(at[j], P)]
                            v.tensor_tensor(win, win, pA[j % 2][:, :, :], ALU.add).then_inc(sem(tag + "acc"), 1)

                    def score(g, q, par):
                        n = quad(g, q)
                        dve.wait_ge(sem(tag + "qx"), n + 1)
                        if not (skip(g) and q == 0):
                            dve.wait_ge(sem(tag + "alpha"), n)
                        v.tensor_tensor(picked[:, :, :, :], pQ[q % 2][:, :, :].rearrange("p t (c h) -> p t c h", c=R),
                                        mask(tm_now, q).unsqueeze(3).to_broadcast([P, 4, R, H]), ALU.mult
                                        ).then_inc(sem(tag + "prod"), 1)
                        dve.wait_ge(sem(tag + "prod"), n + 1)
                        v.tensor_reduce(al[:, :, :], picked[:, :, :, :].rearrange("p t c h -> p t h c"), AX.X,
                                        ALU.add).then_inc(sem(tag + "al"), 1)
                        dve.wait_ge(sem(tag + "al"), 2 * n + 1)
                        rows_there(dve, CONVS, halved(g, par), par, q)
                        s = par * TG + 4 * q
                        v.tensor_tensor(al[:, :, :], al[:, :, :], rows[:, s:s + 4, D:D + H], ALU.add
                                        ).then_inc(sem(tag + "al"), 1)
                        dve.wait_ge(sem(tag + "al"), 2 * n + 2)
                        v.scalar_tensor_tensor(out=sm["alpha"][:, par, :, 4 * q:4 * q + 4].rearrange("p h t -> p t h"),
                                               in0=al[:, :, :], scalar=0.2, in1=al[:, :, :], op0=ALU.mult,
                                               op1=ALU.max).then_inc(sem(tag + "alpha"), 1)

                    def rescale(g):
                        _, at = nc.values_load_multi_w_load_instructions(
                            base_i[0:1, ds(g * TG, 1)], engines=[dve.engine], min_val=0, max_val=N,
                            skip_runtime_bounds_check_because="a destination")
                        dve.wait_ge(sem(tag + "exE"), g + 1)
                        if not skip(g):
                            dve.wait_ge(sem(tag + "acc"), 4 * QG * g)
                        col = acc[:, :, ds(at[0], 1)]
                        v.tensor_tensor(col, col, pX[:, 128:128 + R].unsqueeze(2), ALU.mult)
                        v.tensor_tensor(fac[:, :], pX[0:R * H, 136:136 + R], csel[:, :], ALU.mult).then_inc(sem(tag + "scaled"), 1)
                        dve.wait_ge(sem(tag + "scaled"), 3 * g + 1)
                        v.tensor_reduce(fac1[:, :], fac[:, :], AX.X, ALU.add).then_inc(sem(tag + "scaled"), 1)
                        dve.wait_ge(sem(tag + "scaled"), 3 * g + 2)
                        if not skip(g):
                            dve.wait_ge(sem(tag + "den"), 4 * QG * g)
                        col = den[0:R * H, ds(at[0], 1)]
                        v.tensor_scalar(col, col, fac1[:, :], None, ALU.mult).then_inc(sem(tag + "scaled"), 1)
                        dve.wait_ge(sem(tag + "scaled"), 3 * g + 3)
                        settle(dve)

                    def take_masks(g):
                        take_group(dve, tag + "mask_", 0, g, [(tm_now[:, :], tm, R)])

                    def turn(g, q, par):
                        after, late = parts(g, q, par)
                        if after:
                            if after[1] == 0:
                                take_group(dve, tag, 0, after[0], [(rel_now[:, :], rel, 1)])
                            build(*after)
                        if late:
                            if late[1] == 0:
                                take_group(dve, tag + "late_", 0, late[0], [(rel_late[:, :], rel, 1), (tm_late[:, :], tm, R)])
                            weigh(*late)
                        if scored(g):
                            if q == 0:
                                take_masks(g)
                            score(g, q, par)
                        if late:
                            add(*late[:2])
                        if started(g):
                            if q == 0:
                                softmax_tails(dve, sm, tag, g - 1, g - 1, type_f)
                            if q == 1:
                                softmax_carries(dve, sm, tag, g - 1, g - 1, pM)
                            if q == 2:
                                softmax_maxima(dve, sm, tag, g - 1, g - 1, pM)
                            if q == 3:
                                rescale(g - 1)

                    v.memset(acc[:, :, :], 0.0)
                    v.memset(den[:, :], 0.0)
                    v.memset(exm[:, :, :, R * H], 1.0)
                    v.memset(sm["rowF"][:, :, :], NEG)
                    v.memset(sm["rowB"][:, :, :], NEG)
                    for c in range(R):
                        for h in range(H):
                            v.tensor_copy(hsel[:, c, h:h + 1], head_sel[:, h * HD:h * HD + 1])
                    dve.wait_ge(sem(tag + "iota"), 1)
                    v.tensor_copy(val_f[:, :], val_i[:, :]).then_inc(sem(tag + "made0"), 1)
                    dve.wait_ge(sem(tag + "made0"), 1)
                    v.tensor_scalar(csel[:, :], val_f[:, :], 0.0, None, ALU.is_ge)
                    v.tensor_scalar(val_f[:, :], val_f[:, :], float(H - 1), None, ALU.is_le).then_inc(sem(tag + "made0"), 1)
                    dve.wait_ge(sem(tag + "made0"), 2)
                    v.tensor_tensor(csel[:, :], csel[:, :], val_f[:, :], ALU.mult).then_inc(sem(tag + "made"), 1)
                    dve.wait_ge(sem(tag + "made"), 1)
                    take_group(dve, tag, 0, 0, [(rel_now[:, :], rel, 1)])
                    build(0, 0, 0)
                    all_turns(dve, turn)

        def rel_prepare(sb, type_f, tm, idx1):
            tc_i = sb("tc_i", [P, T], i32)
            tr_i = sb("tr_i", [P, GROUPS * P], i32)
            t_f = sb("t_f", [P, T])
            s_f = sb("s_f", [P, T])
            with nc.Block() as block:
                @block.sync
                def _(sp):
                    sp.dma_start(tc_i[:, :], type_c).then_inc(sem("rt_in"), 16)
                    for h in range(H):
                        sp.dma_start(tr_i[h * TG:(h + 1) * TG, :], type_r).then_inc(sem("rt_in"), 16)

                @block.vector
                def _(dve):
                    v = nc.vector
                    dve.wait_ge(sem("rt_in"), 16 * (1 + H))
                    v.tensor_copy(type_f[:, :], tr_i[:, :])
                    v.tensor_copy(t_f[:, :], tc_i[:, :])
                    v.tensor_copy(s_f[:, :], src_all[:, :]).then_inc(sem("rt"), 1)
                    dve.wait_ge(sem("rt"), 1)
                    for c in range(R):
                        v.tensor_scalar(tm[:, :].rearrange("p (t c) -> p t c", c=R)[:, :, c], t_f[:, :], float(c), None, ALU.is_equal)
                    v.scalar_tensor_tensor(out=idx1[:, :], in0=t_f[:, :], scalar=float(NPAD), in1=s_f[:, :],
                                           op0=ALU.mult, op1=ALU.add)

        def rel_nodes(sb, pb, acc, den, dinv_f, dinv_n):
            tag = "n1_"
            v, a = nc.vector, nc.scalar
            K = R * H + 1
            sel_i = sb("sel_i", [K, R + 1, P], i32)
            sel = sb("sel", [K, R + 1, P])
            rden = sb("rden", [K, NPAD])
            pn = pb("pn", [P, NT])

            with nc.Block() as block:
                @block.gpsimd
                def _(pool):
                    nc.gpsimd.iota(sel_i[:, 0:R, :].rearrange("k c (h f) -> k c h f", h=H), pattern=[[H, R], [1, H], [0, HD]],
                                   base=0, channel_multiplier=-1)
                    nc.gpsimd.iota(sel_i[:, R, :], pattern=[[0, P]], base=R * H, channel_multiplier=-1
                                   ).then_inc(sem("rn_iota"), 1)

                @block.vector
                def _(dve):
                    dve.wait_ge(sem("rn_iota"), 1)
                    v.tensor_copy(sel[:, :, :], sel_i[:, :, :]).then_inc(sem("rn_sel"), 1)
                    dve.wait_ge(sem("rn_sel"), 1)
                    v.tensor_scalar(sel[:, :, :], sel[:, :, :], 0.0, None, ALU.is_equal).then_inc(sem("rn_sel"), 1)
                    v.tensor_scalar(rden[:, :], den[:, :], 1e-30, None, ALU.max).then_inc(sem("rn_max"), 1)
                    dve.wait_ge(sem("rn_max"), 1)
                    v.reciprocal(rden[:, :], rden[:, :]).then_inc(sem("rn_max"), 1)
                    dve.wait_ge(sem("rn_sd"), 2)
                    v.reciprocal(dinv_n[:, :], dinv_n[:, :])
                    v.reciprocal(dinv_f[:, :], dinv_f[:, :])

                @block.tensor
                def _(pe):
                    pe.wait_ge(sem("rn_sel"), 2)
                    for t in range(NT):
                        last = nc.tensor.matmul(pn[:, t:t + 1], den[:, t * P:(t + 1) * P], sel[:, R, 0:1], start=True, stop=True)
                    last.then_inc(sem("rn_n"), 1)
                    for b in range(NB):
                        if b >= 2:
                            pe.wait_ge(sem("rn_cnt"), b - 1)
                        nc.tensor.matmul(cnt_p[b % 2][:, :], sel[:, R, :], den[:, b * BW:(b + 1) * BW], start=True,
                                         stop=True).then_inc(sem("rn_f"), 1)

                @block.scalar
                def _(act):
                    act.wait_ge(sem("rn_n"), 1)
                    a.activation(dinv_n[:, :], pn[:, :], ACT.Sqrt, bias=ones[:, 0:1]).then_inc(sem("rn_sd"), 1)
                    for b in range(NB):
                        act.wait_ge(sem("rn_f"), b + 1)
                        last = a.activation(dinv_f[:, b * BW:(b + 1) * BW], cnt_p[b % 2][:, :], ACT.Sqrt,
                                            bias=ones[:, 0:1]).then_inc(sem("rn_cnt"), 1)
                    act.wait_ge(sem("rn_cnt"), NB)
                    act.sem_inc(sem("rn_sd"), 1)

            def pre(eng, what, ps, S_, o, blk):
                if what == "tensor":
                    for b in range(NB):
                        for c in range(R):
                            n = b * R + c
                            if n >= 3:
                                eng.wait_ge(S_("quot"), n - 2)
                            nc.tensor.matmul(ps[n % 3][:, :], sel[:, c, :], rden[:, blk(b)], start=True,
                                             stop=True).then_inc(S_("rden"), 1)

            def form(dve, h, s, ps, cols, S_, o, blk):
                for b in range(NB):
                    for c in range(R):
                        n = b * R + c
                        dve.wait_ge(S_("rden"), n + 1)
                        v.tensor_tensor(acc[:, c, blk(b)], acc[:, c, blk(b)], ps[n % 3][:, :], ALU.mult
                                        ).then_inc(S_("quot"), 1)
                    dve.wait_ge(S_("quot"), R * (b + 1))
                    v.tensor_tensor(acc[:, 0, blk(b)], acc[:, 0, blk(b)], acc[:, 1, blk(b)], ALU.add)
                    v.tensor_tensor(acc[:, 2, blk(b)], acc[:, 2, blk(b)], acc[:, 3, blk(b)], ALU.add).then_inc(S_("two"), 1)
                    dve.wait_ge(S_("two"), 2 * b + 1)
                    v.tensor_tensor(acc[:, 0, blk(b)], acc[:, 0, blk(b)], acc[:, 2, blk(b)], ALU.add).then_inc(S_("two"), 1)
                    dve.wait_ge(S_("two"), 2 * b + 2)
                    v.tensor_tensor(h[:, blk(b)], acc[:, 0, blk(b)], xT[:, blk(b)], ALU.add).then_inc(S_("h"), 1)
            return dict(cols=col0[0], pre=pre, form=form)

        def rel_layer(dinv_f, dinv_n):
            with ExitStack() as part:
                rel_project(maker(part, nc.sbuf_tensor, "_r"), maker(part, nc.psum_tensor, "_r"))
            with ExitStack() as keep:
                wide = maker(keep, nc.sbuf_tensor, "_r")
                acc = wide("acc", [P, R, NPAD])
                den = wide("den", [R * H + 1, NPAD])
                with ExitStack() as mid:
                    m = maker(mid, nc.sbuf_tensor, "_r")
                    type_f, tm, idx1 = m("type_f", [P, GROUPS * P], bf16), m("tm", [P, T * R], bf16), m("idx1", [P, T], i32)
                    with ExitStack() as part:
                        rel_prepare(maker(part, nc.sbuf_tensor, "_r"), type_f, tm, idx1)
                    with ExitStack() as part:
                        rel_edges(maker(part, nc.sbuf_tensor, "_r"), maker(part, nc.psum_tensor, "_r"), acc, den,
                                  type_f, tm, idx1)
                with ExitStack() as part:
                    sb, pb = maker(part, nc.sbuf_tensor, "_r"), maker(part, nc.psum_tensor, "_r")
                    with ExitStack() as few:
                        cnt_p[:] = [maker(few, nc.psum_tensor, "_r")(f"cnt{i}", [P, BW]) for i in range(2)]
                        extra = rel_nodes(sb, maker(few, nc.psum_tensor, "_r"), acc, den, dinv_f, dinv_n)
                    node_stage("n1_", 0, "rel", sb, pb, acc, extra)

        cnt_p = []

        def plain_project(tag, x, w, dinv_n, sb, pb):
            stage = sb("stage", [P, 2, 4, D])
            pp = [pb(f"pp{i}", [P, D]) for i in range(4)]
            prod, copied = sem(tag + "prod"), sem(tag + "copied")
            stored = [sem(tag + "stored0"), sem(tag + "stored1")]
            with nc.Block() as block:
                @block.sync
                def _(sp):
                    for b in range(NB):
                        sp.wait_ge(copied, 4 * (b + 1))
                        sp.dma_start(h_tab[b * BW:(b + 1) * BW, :].rearrange("(j p) f -> p j f", p=P),
                                     stage[:, b % 2, :, :]).then_inc(stored[b % 2], 16)
                    sp.wait_ge(stored[0], 16 * ((NB + 1) // 2))
                    sp.wait_ge(stored[1], 16 * (NB // 2))

                @block.tensor
                def _(pe):
                    for t in range(NT):
                        if t >= 4:
                            pe.wait_ge(copied, t - 3)
                        nc.tensor.matmul(pp[t % 4][:, :], x[:, t * P:(t + 1) * P], w[:, :], start=True,
                                         stop=True).then_inc(prod, 1)

                @block.scalar
                def _(act):
                    for t in range(NT):
                        b = t // 4
                        if t % 4 == 0 and b >= 2:
                            act.wait_ge(stored[b % 2], 16 * (b // 2))
                        act.wait_ge(prod, t + 1)
                        scale = dinv_n[:, t:t + 1] if dinv_n is not None else 1.0
                        nc.scalar.activation(stage[:, b % 2, t % 4, :], pp[t % 4][:, :], ACT.Copy,
                                             scale=scale).then_inc(copied, 1)

        def plain_edges(tag, turn, acc, sb, pb):
            rows = sb("rows", [P, 2 * TG, D])
            S = sb("S", [P, 2, 4, P])
            idx_now = sb("idx_now", [P, 2, TG], i32)
            rel_now = sb("rel_now", [P, TG])
            lists = [(rel_now[:, :], rel, 1)]
            pA = [pb(f"pA{i}", [P, 4, P]) for i in range(2)]
            quad = lambda g, q: g * QG + q
            skip = lambda g: isinstance(g, int) and g == 0
            with nc.Block() as block:
                @block.gpsimd
                def _(pool):
                    gather_all(pool, lambda g, par: gather_group(pool, tag, 0, g, par, h_tab, src_all, idx_now, rows,
                                                                 "agg", "agg"))

                @block.tensor
                def _(pe):
                    def group(g, par, half):
                        for q in range(QG):
                            n = quad(g, q)
                            pe.wait_ge(sem(tag + "S"), n + 1)
                            rows_there(pe, turn, half, par, q)
                            if not (skip(g) and q < 2):
                                pe.wait_ge(sem(tag + "acc"), 4 * (n - 1))
                            for j in range(4):
                                last = nc.tensor.matmul(pA[q % 2][:, j, :], rows[:, par * TG + 4 * q + j, :],
                                                        S[:, q % 2, j, :], start=True, stop=True)
                            last.then_inc(sem(tag + "agg"), 1)
                    group(0, 0, 0)
                    with pe.Fori(0, (GROUPS - 1) // 2) as k:
                        group(2 * k + 1, 1, k)
                        group(2 * k + 2, 0, k + 1)

                @block.vector
                def _(dve):
                    v = nc.vector

                    def build(g, q):
                        if not (skip(g) and q < 2):
                            dve.wait_ge(sem(tag + "agg"), quad(g, q) - 1)
                        for j in range(4):
                            t = 4 * q + j
                            last = v.tensor_scalar(S[:, q % 2, j, :], iota_row[:, :], rel_now[:, t:t + 1], None,
                                                   ALU.is_equal)
                        last.then_inc(sem(tag + "S"), 1)

                    def add(g, q, first):
                        n = quad(g, q)
                        at = bases(dve, g * TG + 4 * q)
                        dve.wait_ge(sem(tag + "agg"), n + 1)
                        for j in range(4):
                            if not (first and j == 0):
                                dve.wait_ge(sem(tag + "acc"), 4 * n + j)
                            win = acc[:, ds(at[j], P)]
                            v.tensor_tensor(win, win, pA[q % 2][:, j, :], ALU.add).then_inc(sem(tag + "acc"), 1)

                    v.memset(acc[:, :], 0.0).then_inc(sem(tag + "clear"), 1)
                    dve.wait_ge(sem(tag + "clear"), 1)
                    take_group(dve, tag, 0, 0, lists)
                    build(0, 0)
                    for q in range(1, QG):
                        build(0, q)
                        add(0, q - 1, q == 1)
                    with dve.Fori(1, GROUPS) as g:
                        take_group(dve, tag, 0, g, lists)
                        for q in range(QG):
                            build(g, q)
                            if q:
                                add(g, q - 1, False)
                            else:
                                add(g - 1, QG - 1, False)
                    add(GROUPS - 1, QG - 1, False)

        def load(tag, pairs):
            with nc.Block() as block:
                @block.sync
                def _(sp):
                    for to, source in pairs:
                        sp.dma_start(to, source).then_inc(sem(tag), 16)
                    sp.wait_ge(sem(tag), 16 * len(pairs))

        def gcn_form(w, acc, dinv_f):
            v = nc.vector

            def own(eng, x, ps, S_, blk):
                for b in range(NB):
                    if b >= 3:
                        eng.wait_ge(S_("own_read"), b - 2)
                    nc.tensor.matmul(ps[b % 3][:, :], w[:, :], x[:, blk(b)], start=True, stop=True).then_inc(S_("own"), 1)

            def combine(dve, b, ps, cols, S_, blk):
                dve.wait_ge(S_("own"), b + 1)
                t = acc[:, blk(b)]
                v.tensor_tensor(tmp[0][:, blk(b)], ps[b % 3][:, :], dinv_f[:, blk(b)], ALU.mult).then_inc(S_("own_read"), 1)
                dve.wait_ge(S_("own_read"), b + 1)
                v.tensor_tensor(t, t, tmp[0][:, blk(b)], ALU.add).then_inc(S_("gc"), 1)
                dve.wait_ge(S_("gc"), 3 * b + 1)
                v.tensor_tensor(t, t, dinv_f[:, blk(b)], ALU.mult).then_inc(S_("gc"), 1)
                dve.wait_ge(S_("gc"), 3 * b + 2)
                v.tensor_scalar(t, t, cols[:, 0:1], None, ALU.add).then_inc(S_("gc"), 1)
                dve.wait_ge(S_("gc"), 3 * b + 3)
            return own, combine

        tmp = [None]

        def gcn_layer(dinv_f, dinv_n):
            v, a = nc.vector, nc.scalar
            blk = lambda b: slice(b * BW, (b + 1) * BW)
            with ExitStack() as keep:
                wide = maker(keep, nc.sbuf_tensor, "_g")
                acc, y = wide("acc", [P, NPAD]), wide("y", [P, NPAD])
                wa, wb, cols1 = wide("wa", [P, D]), wide("wb", [P, D]), wide("cols1", [P, 3])
                tmp[0] = wide("tmp", [P, NPAD])
                load("g_in", [(wa[:, :], w2[0]), (wb[:, :], w2[1]), (cols1[:, :], b2[0])])
                for tag, x, w in (("g1_", xT, wa), ("g2_", y, wb)):
                    with ExitStack() as part:
                        plain_project(tag + "p", x, w, dinv_n, maker(part, nc.sbuf_tensor, tag), maker(part, nc.psum_tensor, tag))
                    with ExitStack() as part:
                        plain_edges(tag, CONVS + 1 + (tag == "g2_"), acc, maker(part, nc.sbuf_tensor, tag), maker(part, nc.psum_tensor, tag))
                    with ExitStack() as part:
                        sb, pb = maker(part, nc.sbuf_tensor, tag), maker(part, nc.psum_tensor, tag)
                        own, combine = gcn_form(w, acc, dinv_f)
                        if tag == "g1_":
                            ps = [pb(f"po{i}", [P, BW]) for i in range(3)]
                            S_ = lambda n: sem("g1n_" + n)
                            with nc.Block() as block:
                                @block.tensor
                                def _(pe):
                                    own(pe, xT, ps, S_, blk)

                                @block.vector
                                def _(dve):
                                    for b in range(NB):
                                        combine(dve, b, ps, cols1, S_, blk)
                                        v.tensor_scalar(tmp[0][:, blk(b)], acc[:, blk(b)], 0.0, None, ALU.min
                                                        ).then_inc(S_("neg"), 1)
                                    for b in range(NB):
                                        dve.wait_ge(S_("exp"), b + 1)
                                        v.scalar_tensor_tensor(out=acc[:, blk(b)], in0=acc[:, blk(b)], scalar=0.0,
                                                               in1=tmp[0][:, blk(b)], op0=ALU.max, op1=ALU.add
                                                               ).then_inc(S_("elu"), 1)
                                        dve.wait_ge(S_("elu"), b + 1)
                                        v.tensor_scalar(y[:, blk(b)], acc[:, blk(b)], -1.0, None, ALU.add)

                                @block.scalar
                                def _(act):
                                    for b in range(NB):
                                        act.wait_ge(S_("neg"), b + 1)
                                        a.activation(tmp[0][:, blk(b)], tmp[0][:, blk(b)], ACT.Exp).then_inc(S_("exp"), 1)
                        else:
                            def pre(eng, what, ps, S_, o, blk):
                                if what == "tensor":
                                    own(eng, y, ps, S_, blk)

                            def form(dve, h, s, ps, cols, S_, o, blk):
                                for b in range(NB):
                                    combine(dve, b, ps, cols, S_, blk)
                                    v.tensor_tensor(h[:, blk(b)], acc[:, blk(b)], xT[:, blk(b)], ALU.add
                                                    ).then_inc(S_("h"), 1)
                            node_stage("n2_", 0, "gcn", sb, pb, acc, dict(cols=b2[1], pre=pre, form=form))

        def scatter_edges(ew, sb, pb):
            tag = "s_"
            v, a = nc.vector, nc.scalar
            Sw = sb("Sw", [P, 2, 4, P])
            same = sb("same", [P, 2, 4, P])
            before = sb("before", [P, P])
            ahead = sb("ahead", [P, 4, P])
            cnt = sb("cnt", [P, 4])
            part_i = sb("part_i", [P, 1], i32)
            own_row = sb("own_row", [P, 1])
            src_f = sb("src_f", [P, T])
            src_d = sb("src_d", [P, T])
            srcb = sb("srcb", [P, 2, 4 * P], i32)
            hwin = sb("hwin", [P, 2, 4, D])
            Gs = sb("Gs", [P, 2, 4, P])
            ys = sb("ys", [P, TG, D])
            idx = sb("idx", [P, TG], i32)
            now = {k: sb(k + "_now", [P, TG]) for k in ("rel", "ew", "src", "srd")}
            pG = [pb(f"pG{i}", [P, 4, P]) for i in range(2)]
            pY = [pb(f"pY{i}", [P, 4, D]) for i in range(2)]
            quad = lambda g, q: g * QG + q
            skip = lambda g: isinstance(g, int) and g == 0

            def groups(eng, group):
                group(0)
                with eng.Fori(1, GROUPS) as g:
                    group(g)

            with nc.Block() as block:
                @block.gpsimd
                def _(pool):
                    nc.gpsimd.iota(part_i[:, :], pattern=[[0, 1]], base=NPAD, channel_multiplier=1
                                   ).then_inc(sem(tag + "iota"), 1)

                    def group(g):
                        for q in range(QG):
                            n = quad(g, q)
                            pool.wait_ge(sem(tag + "y_out"), n + 1)
                            pool.wait_ge(sem(tag + "idx"), n + 1)
                            settle(pool)
                            if not (skip(g) and q < 2):
                                pool.wait_ge(sem(f"{tag}added{(q - 2) % QG}"), 64 * (g + (1 if q >= 2 else 0)))
                                settle(pool)
                            for j in range(4):
                                t = 4 * q + j
                                nc.gpsimd.indirect_dma_start(
                                    sum_tab[q % 2 * 4 + j], bass.IndirectOffsetOnAxis(ap=idx[:, t:t + 1], axis=0),
                                    ys[:, t, :], None, compute_op=ALU.add).then_inc(sem(f"{tag}added{q}"), 16)
                    groups(pool, group)
                    for q in range(QG):
                        pool.wait_ge(sem(f"{tag}added{q}"), 64 * GROUPS)

                @block.sync
                def _(sp):
                    def group(g):
                        for q in range(QG):
                            n = quad(g, q)
                            at = bases(sp, g * TG + 4 * q)
                            if not (skip(g) and q < 2):
                                sp.wait_ge(sem(tag + "y"), n - 1)
                                settle(sp)
                                sp.wait_ge(sem(tag + "cnt"), n - 1)
                                settle(sp)
                            for j in range(4):
                                sp.dma_start(hwin[:, q % 2, j, :], h_tab[ds(at[j], P), :]
                                             ).then_inc(sem(f"{tag}in{q % 2}"), 16)
                            sp.dma_start(srcb[:, q % 2, :], src_row[:, ds((g * TG + 4 * q) * P, 4 * P)].to_broadcast([P, 4 * P])
                                         ).then_inc(sem(f"{tag}in{q % 2}"), 16)
                    groups(sp, group)

                @block.tensor
                def _(pe):
                    def group(g):
                        for q in range(QG):
                            n = quad(g, q)
                            pe.wait_ge(sem(tag + "built"), n + 1)
                            if not (skip(g) and q < 2):
                                pe.wait_ge(sem(tag + "g_out"), n - 1)
                            for j in range(4):
                                last = nc.tensor.matmul(pG[q % 2][:, j, :], Sw[:, q % 2, j, :], same[:, q % 2, j, :],
                                                        start=True, stop=True)
                            last.then_inc(sem(tag + "g"), 1)
                            pe.wait_ge(sem(tag + "g_out"), n + 1)
                            pe.wait_ge(sem(f"{tag}in{q % 2}"), 80 * (g * (QG // 2) + q // 2 + 1))
                            if not (skip(g) and q < 2):
                                pe.wait_ge(sem(tag + "y_out"), n - 1)
                            for j in range(4):
                                last = nc.tensor.matmul(pY[q % 2][:, j, :], Gs[:, q % 2, j, :], hwin[:, q % 2, j, :],
                                                        start=True, stop=True)
                            last.then_inc(sem(tag + "y"), 1)
                    groups(pe, group)

                @block.scalar
                def _(act):
                    def group(g):
                        for q in range(QG):
                            n = quad(g, q)
                            act.wait_ge(sem(tag + "g"), n + 1)
                            if not (skip(g) and q < 2):
                                act.wait_ge(sem(tag + "y"), n - 1)
                            a.activation(Gs[:, q % 2, :, :], pG[q % 2][:, :, :], ACT.Copy).then_inc(sem(tag + "g_out"), 1)
                            act.wait_ge(sem(tag + "y"), n + 1)
                            if not skip(g):
                                act.wait_ge(sem(f"{tag}added{q}"), 64 * g)
                            a.activation(ys[:, 4 * q:4 * q + 4, :], pY[q % 2][:, :, :], ACT.Copy).then_inc(sem(tag + "y_out"), 1)
                    groups(act, group)

                @block.vector
                def _(dve):
                    def group(g):
                        take_group(dve, tag, 0, g, [(now["rel"][:, :], rel, 1), (now["ew"][:, :], ew, 1),
                                                    (now["src"][:, :], src_f, 1), (now["srd"][:, :], src_d, 1)])
                        for q in range(QG):
                            n = quad(g, q)
                            dve.wait_ge(sem(f"{tag}in{q % 2}"), 80 * (g * (QG // 2) + q // 2 + 1))
                            if not (skip(g) and q < 2):
                                dve.wait_ge(sem(tag + "g"), n - 1)
                            for j in range(4):
                                t = 4 * q + j
                                v.tensor_scalar(Sw[:, q % 2, j, :], iota_row[:, :], now["rel"][:, t:t + 1],
                                                now["ew"][:, t:t + 1], ALU.is_equal, ALU.mult)
                                last = v.tensor_scalar(same[:, q % 2, j, :], srcb[:, q % 2, j * P:(j + 1) * P],
                                                       now["src"][:, t:t + 1], None, ALU.is_equal)
                            last.then_inc(sem(tag + "built"), 1)
                            dve.wait_ge(sem(tag + "built"), n + 1)
                            if not (skip(g) and q == 0):
                                dve.wait_ge(sem(tag + "cnt"), n)
                            v.tensor_tensor(ahead[:, :, :], same[:, q % 2, :, :],
                                            before[:, :].unsqueeze(1).to_broadcast([P, 4, P]), ALU.mult
                                            ).then_inc(sem(tag + "ahead"), 1)
                            dve.wait_ge(sem(tag + "ahead"), n + 1)
                            if not (skip(g) and q == 0):
                                dve.wait_ge(sem(tag + "first"), n)
                            v.tensor_reduce(cnt[:, :], ahead[:, :, :], AX.X, ALU.add).then_inc(sem(tag + "cnt"), 1)
                            dve.wait_ge(sem(tag + "cnt"), n + 1)
                            v.scalar_tensor_tensor(out=cnt[:, :], in0=cnt[:, :], scalar=0.0,
                                                   in1=now["srd"][:, 4 * q:4 * q + 4], op0=ALU.is_equal,
                                                   op1=ALU.mult).then_inc(sem(tag + "first"), 1)
                            dve.wait_ge(sem(tag + "first"), n + 1)
                            if not skip(g):
                                dve.wait_ge(sem(f"{tag}added{q}"), 64 * g)
                            v.tensor_scalar(idx[:, 4 * q:4 * q + 4], cnt[:, :], own_row[:, :], None, ALU.add
                                            ).then_inc(sem(tag + "idx"), 1)
                            dve.wait_ge(sem(tag + "idx"), n + 1)
                            settle(dve)
                    dve.wait_ge(sem(tag + "iota"), 1)
                    v.tensor_copy(own_row[:, :], part_i[:, :])
                    v.tensor_copy(src_f[:, :], src_all[:, :]).then_inc(sem(tag + "prep"), 1)
                    dve.wait_ge(sem(tag + "prep"), 1)
                    v.tensor_scalar(before[:, :], iota_row[:, :], float(NPAD), own_row[:, :], ALU.add, ALU.is_lt)
                    v.tensor_scalar(src_d[:, :], src_f[:, :], own_row[:, :], None, ALU.subtract).then_inc(sem(tag + "prep"), 1)
                    dve.wait_ge(sem(tag + "prep"), 2)
                    groups(dve, group)

        def scatter_layer():
            v = nc.vector
            tag = "w_"
            with ExitStack() as keep:
                wide = maker(keep, nc.sbuf_tensor, "_w")
                w, ew, zero = wide("w", [P, D]), wide("ew", [P, T]), wide("zero", [P, 4, D])
                with nc.Block() as block:
                    @block.vector
                    def _(dve):
                        v.memset(zero[:, :, :], 0.0).then_inc(sem("w_zero"), 1)

                    @block.sync
                    def _(sp):
                        sp.dma_start(w[:, :], w3).then_inc(sem("w_in"), 16)
                        sp.dma_start(ew[:, :], ew_c).then_inc(sem("w_in"), 16)
                        sp.wait_ge(sem("w_zero"), 1)
                        for tab in sum_tab:
                            for b in range(NB):
                                sp.dma_start(tab[b * BW:(b + 1) * BW, :].rearrange("(j p) f -> p j f", p=P), zero[:, :, :]
                                             ).then_inc(sem("w_in"), 16)
                            sp.dma_start(tab[NPAD:NPAD + P, :], zero[:, 0, :]).then_inc(sem("w_in"), 16)
                        sp.wait_ge(sem("w_in"), 16 * (2 + 8 * (NB + 1)))
                with ExitStack() as part:
                    plain_project(tag + "p", xT, w, None, maker(part, nc.sbuf_tensor, tag), maker(part, nc.psum_tensor, tag))
                with ExitStack() as part:
                    scatter_edges(ew, maker(part, nc.sbuf_tensor, tag), maker(part, nc.psum_tensor, tag))
                with ExitStack() as part:
                    sb = maker(part, nc.sbuf_tensor, tag)
                    parts = sb("parts", [P, 2, 8, 4, D])

                    def fetch(sp, S_):
                        for b in range(NB):
                            if b >= 2:
                                sp.wait_ge(S_("summed"), b - 1)
                            for k in range(8):
                                sp.dma_start(parts[:, b % 2, k, :, :],
                                             sum_tab[k][b * BW:(b + 1) * BW, :].rearrange("(j p) f -> p j f", p=P)
                                             ).then_inc(S_(f"parts{b % 2}"), 16)

                    def pre(eng, what, ps, S_, o, blk):
                        if what != "tensor":
                            return
                        for b in range(NB):
                            eng.wait_ge(S_(f"parts{b % 2}"), 128 * (b // 2 + 1))
                            if b >= 3:
                                eng.wait_ge(S_("z"), 2 * (b - 3) + 1)
                            for j in range(4):
                                for k in range(8):
                                    last = nc.tensor.matmul(ps[b % 3][:, j * P:(j + 1) * P], parts[:, b % 2, k, j, :],
                                                            ident[:, :], start=k == 0, stop=k == 7)
                            last.then_inc(S_("summed"), 1)

                    def form(dve, h, s, ps, cols, S_, o, blk):
                        for b in range(NB):
                            t = h[:, blk(b)]
                            dve.wait_ge(S_("summed"), b + 1)
                            v.tensor_scalar(t, ps[b % 3][:, :], cols[:, 0:1], None, ALU.add).then_inc(S_("z"), 1)
                            dve.wait_ge(S_("z"), 2 * b + 1)
                            v.scalar_tensor_tensor(out=t, in0=t, scalar=0.01, in1=t, op0=ALU.mult, op1=ALU.max
                                                   ).then_inc(S_("z"), 1)
                            dve.wait_ge(S_("z"), 2 * b + 2)
                            v.tensor_tensor(t, t, xT[:, blk(b)], ALU.add).then_inc(S_("h"), 1)
                    node_stage("n3_", 0, "weighted", sb, maker(part, nc.psum_tensor, tag), None,
                               dict(cols=b3, pre=pre, form=form, fetch=fetch))

        with nc.Fori(0, CONVS - 1) as l:
            conv_layer(l, "conv")
        conv_layer(CONVS - 1, "last")
        recycle()
        with ExitStack() as scope:
            dinv_f = scope.enter_context(nc.sbuf_tensor("dinv_f", [P, NPAD], f32))
            dinv_n = scope.enter_context(nc.sbuf_tensor("dinv_n", [P, NT], f32))
            rel_layer(dinv_f, dinv_n)
            recycle()
            gcn_layer(dinv_f, dinv_n)
            recycle()
        scatter_layer()
        with nc.Block() as block:
            @block.sync
            def _(sp):
                sp.dma_start(out, xT[:, 0:N]).then_inc(sem("stored"), 16)
                sp.wait_ge(sem("stored"), 16)


_INS = ["xT_in", "src_c", "src_row", "dst_c", "dst_row", "prev_row", "next_row", "first_row", "first_next", "last_row",
        "last_prev", "type_c", "type_r", "ew_c", "w0", "b0", "col0", "w1", "w1T", "a1", "w2", "b2", "w3", "b3"]


def kernel(**inputs):
    import numpy as np
    import concourse.bacc as bacc
    from concourse import mybir as mb
    from concourse.bass_utils import run_bass_kernel_spmd as run

    z = {k: np.asarray(v) for k, v in inputs.items()}
    pad = T * P - EDGES
    src = np.concatenate([z["src"], np.zeros(pad, np.int32)])
    dst = np.concatenate([z["dst"], np.full(pad, N, np.int32)])
    typ = np.concatenate([z["edge_type_4"], np.zeros(pad, np.int32)])
    ew = np.concatenate([z["edge_weight"], np.zeros(pad, np.float32)])
    prev = np.concatenate([np.full(1, -1, np.int32), dst[:-1]])
    nxt = np.concatenate([dst[1:], np.full(1, -1, np.int32)])

    def cols(a):
        return a.reshape(T, P).T

    def rows(a):
        return a.reshape(GROUPS, TG, P).transpose(1, 0, 2).reshape(TG, GROUPS * P)

    ln_g = np.concatenate([z["L0_gnn_ln_g"], np.ones((1, D), np.float32)])
    ln_b = np.concatenate([z["L0_gnn_ln_b"], np.zeros((1, D), np.float32)])
    a1 = np.zeros((R, 2, H, D), np.float32)
    for h in range(H):
        a1[:, :, h, h * HD:(h + 1) * HD] = z["L1_gnn_attn"].reshape(R, H, 2, HD)[:, h]
    zero = np.zeros((D, 2), np.float32)
    arrays = {
        "xT_in": np.concatenate([z["x"], np.zeros((NPAD - N, D), np.float32)]).T,
        "src_c": cols(src), "src_row": src.reshape(1, T * P), "dst_c": cols(dst), "dst_row": rows(dst), "prev_row": rows(prev), "next_row": rows(nxt),
        "first_row": dst[0::P].reshape(1, T), "first_next": np.concatenate([dst[P::P], [-1]]).reshape(1, T).astype(np.int32),
        "last_row": dst[P - 1::P].reshape(1, T), "last_prev": prev[0::P].reshape(1, T),
        "type_c": cols(typ), "type_r": rows(typ), "ew_c": cols(ew),
        "w0": np.concatenate([z["L0_gnn_Wk"], z["L0_gnn_Wv"], z["L0_gnn_Wq"], z["L0_gnn_Ws"]], axis=2),
        "b0": np.concatenate([z["L0_gnn_bk"], z["L0_gnn_bv"], z["L0_gnn_bq"]], axis=1),
        "col0": np.stack([z["L0_gnn_bs"], ln_g, ln_b], axis=2),
        "w1": z["L1_gnn_W"].transpose(1, 0, 2), "w1T": z["L1_gnn_W"].transpose(2, 0, 1),
        "a1": a1.transpose(3, 0, 1, 2),
        "w2": np.stack([z["L2_gnn_W1"], z["L2_gnn_W2"]]),
        "b2": np.stack([np.concatenate([z["L2_gnn_b1"][:, None], zero], 1), np.concatenate([z["L2_gnn_b2"][:, None], zero], 1)]),
        "w3": z["L3_gnn_weight"], "b3": np.concatenate([z["L3_gnn_bias"][:, None], zero], 1),
    }
    arrays = {k: np.ascontiguousarray(v) for k, v in arrays.items()}
    nc = bacc.Bacc("TRN2", target_bir_lowering=False, num_devices=1)
    args = [nc.dram_tensor("in_" + k, arrays[k].shape, mb.dt.from_np(arrays[k].dtype), kind="ExternalInput").ap()
            for k in _INS]
    args.append(nc.dram_tensor("out_0", (D, N), mb.dt.float32, kind="ExternalOutput").ap())
    gnn_kernel(nc, *args)
    r = run(nc, [{"in_" + k: v for k, v in arrays.items()}], core_ids=[0])
    return np.ascontiguousarray(r.results[0]["out_0"].T)
```

```python
import concourse.bass as bass
from concourse import mybir
from contextlib import ExitStack

NEG = -1.0e30
P = 128
N = 3125
D = 128
H = 4
HD = D // H
R = 4
CONVS = 5
EDGES = 53125
TG = 32
QG = TG // 4
GROUPS = -(-EDGES // (P * TG))
T = GROUPS * TG
BW = 512
NB = -(-(N + P) // BW)
NPAD = NB * BW
ROW = H * (TG + 1)
RW = D + 2 * H
NT = NPAD // P
SCALE = 1.0 / float(HD) ** 0.5
EPS = 1.0e-5


def gnn_kernel(nc, xT_in, src_c, src_row, dst_c, dst_row, prev_row, next_row, first_row, first_next, last_row,
               last_prev, type_c, type_r, ew_c, w0, b0, col0, w1, w1T, a1, w2, b2, w3, b3, out):
    f32, i32, bf16 = mybir.dt.float32, mybir.dt.int32, mybir.dt.bfloat16
    ALU, ACT, AX = mybir.AluOpType, mybir.ActivationFunctionType, mybir.AxisListType
    ds = bass.ds

    kv_tab = nc.dram_tensor("kv_tab", [NPAD, 2 * D], f32).ap()
    q_tab = nc.dram_tensor("q_tab", [NPAD, D], f32).ap()
    rel_tab = nc.dram_tensor("rel_tab", [R * NPAD, RW], f32).ap()
    adst_tab = nc.dram_tensor("adst_tab", [NPAD, R * H], f32).ap()
    h_tab = nc.dram_tensor("h_tab", [NPAD, D], f32).ap()

    sum_tab = [nc.dram_tensor(f"sum_tab{k}", [NPAD + P, D], f32).ap() for k in range(8)]

    root = ExitStack()
    sems = {}

    def sem(name):
        if name not in sems:
            sems[name] = nc.alloc_semaphore(name)
        return sems[name]

    def recycle():
        kept = [n for n in sems if n.startswith(("rows", "settled", "zeroed"))]
        nc.clear_and_free_semaphores([s for n, s in sems.items() if n not in kept])
        for n in list(sems):
            if n not in kept:
                del sems[n]
        with nc.Block():
            pass

    def settle(eng):
        eng.sem_inc(sem(f"settled_{eng.engine.name}"), 1)

    def bases(eng, first):
        _, v = nc.values_load_multi_w_load_instructions(
            base_i[0:1, ds(first, 4)], engines=[eng.engine], min_val=0, max_val=N,
            skip_runtime_bounds_check_because="a destination is at most N, the one of the padding")
        return v

    with root:
        def gsb(name, shape, dt=f32):
            return root.enter_context(nc.sbuf_tensor(name, shape, dt))

        xT = gsb("xT", [P, NPAD])
        src_all = gsb("src_all", [P, T], i32)
        base_i = gsb("base_i", [1, T], i32)
        rel = gsb("rel", [P, T])
        iota_row = gsb("iota_row", [P, P])
        ident = gsb("ident", [P, P])
        ones = gsb("ones", [P, P])
        mean_w = gsb("mean_w", [P, P])
        head_sel = gsb("head_sel", [P, P])
        eps_col = gsb("eps_col", [P, 1])
        zero = gsb("zero", [P, D])
        rstF = gsb("rstF", [P, GROUPS * P], bf16)
        rstB = gsb("rstB", [P, GROUPS * P], bf16)
        rowrF = gsb("rowrF", [R, GROUPS * H * (TG + 1)], bf16)
        rowrB = gsb("rowrB", [R, GROUPS * H * (TG + 1)], bf16)

        with ExitStack() as scope:
            def sb(name, shape, dt=f32):
                return scope.enter_context(nc.sbuf_tensor(name, shape, dt))

            dst_ci = sb("dst_ci", [P, T], i32)
            first_b = sb("first_b", [P, T], i32)
            dst_f = sb("dst_f", [P, T])
            first_f = sb("first_f", [P, T])
            seg_i = sb("seg_i", [P, 3, GROUPS * P], i32)
            seg_f = sb("seg_f", [P, 3, GROUPS * P])
            edge_i = sb("edge_i", [R, 4, T], i32)
            edge_f = sb("edge_f", [R, 4, T])
            iota_i = sb("iota_i", [P, P], i32)
            part_i = sb("part_i", [P, P], i32)
            part_f = sb("part_f", [P, P])
            in_sem = sem("setup_in")
            iota_done = sem("setup_iota")
            ch = sem("setup_chain")
            with nc.Block() as block:
                @block.sync
                def _(sp):
                    sp.dma_start(xT[:, :], xT_in).then_inc(in_sem, 16)
                    sp.dma_start(src_all[:, :], src_c).then_inc(in_sem, 16)
                    sp.dma_start(dst_ci[:, :], dst_c).then_inc(in_sem, 16)
                    sp.dma_start(base_i[:, :], first_row).then_inc(in_sem, 16)
                    sp.dma_start(first_b[:, :], first_row.to_broadcast([P, T])).then_inc(in_sem, 16)
                    for h in range(H):
                        for k, rows in enumerate((dst_row, prev_row, next_row)):
                            sp.dma_start(seg_i[h * TG:(h + 1) * TG, k, :], rows).then_inc(in_sem, 16)
                    for k, row in enumerate((first_row, first_next, last_row, last_prev)):
                        sp.dma_start(edge_i[:, k, :], row.to_broadcast([R, T])).then_inc(in_sem, 16)

                @block.scalar
                def _(act):
                    act.wait_ge(sem("setup_zero"), 1)
                    for tab in sum_tab:
                        for b in range(NB):
                            act.dma_start(tab[b * BW:(b + 1) * BW, :].rearrange("(j p) f -> p j f", p=P),
                                          zero[:, :].unsqueeze(1).to_broadcast([P, 4, D])).then_inc(sem("zeroed"), 16)
                        act.dma_start(tab[NPAD:NPAD + P, :], zero[:, :]).then_inc(sem("zeroed"), 16)

                @block.gpsimd
                def _(pool):
                    nc.gpsimd.iota(iota_i[:, :], pattern=[[1, P]], base=0, channel_multiplier=0)
                    nc.gpsimd.iota(part_i[:, :], pattern=[[0, P]], base=0,
                                   channel_multiplier=1).then_inc(iota_done, 1)

                @block.vector
                def _(dve):
                    v = nc.vector
                    n = [0]

                    def link(ins):
                        n[0] += 1
                        ins.then_inc(ch, 1)
                        dve.wait_ge(ch, n[0])

                    v.memset(zero[:, :], 0.0).then_inc(sem("setup_zero"), 1)
                    v.memset(ones[:, :], 1.0)
                    v.memset(mean_w[:, :], 1.0 / D)
                    v.memset(eps_col[:, :], EPS)
                    v.memset(rowrF[:, :], NEG)
                    link(v.memset(rowrB[:, :], NEG))
                    dve.wait_ge(iota_done, 1)
                    v.tensor_copy(iota_row[:, :], iota_i[:, :])
                    link(v.tensor_copy(part_f[:, :], part_i[:, :]))
                    link(v.tensor_tensor(ident[:, :], iota_row[:, :], part_f[:, :], ALU.is_equal))
                    for h in range(H):
                        last = v.tensor_scalar(head_sel[:, h * HD:(h + 1) * HD], part_f[:, 0:HD], float(h * TG),
                                               None, ALU.is_equal)
                    link(last)
                    dve.wait_ge(in_sem, 16 * (5 + 3 * H + 4))
                    v.tensor_copy(dst_f[:, :], dst_ci[:, :])
                    v.tensor_copy(seg_f[:, :, :], seg_i[:, :, :])
                    v.tensor_copy(edge_f[:, :, :], edge_i[:, :, :])
                    link(v.tensor_copy(first_f[:, :], first_b[:, :]))
                    link(v.tensor_tensor(rel[:, :], dst_f[:, :], first_f[:, :], ALU.subtract))
                    def blocks(t, n):
                        return t.rearrange("p (g e) -> p g e", e=n)

                    for o, k in ((blocks(rstF[:, :], P), 1), (blocks(rstB[:, :], P)[:, :, ::-1], 2)):
                        link(v.tensor_tensor(o, blocks(seg_f[:, 0, :], P), blocks(seg_f[:, k, :], P), ALU.not_equal))
                    for o in (rstF, rstB):
                        link(v.tensor_scalar(o[:, :], o[:, :], NEG, None, ALU.mult))
                    for o, a, b in ((blocks(rowrF[:, :], ROW), 2, 3), (blocks(rowrB[:, :], ROW)[:, :, ::-1], 0, 1)):
                        for h in range(H):
                            at = h * (TG + 1) + (1 if a == 2 else 0)
                            link(v.tensor_tensor(o[:, :, at:at + TG], blocks(edge_f[:, a, :], TG),
                                                 blocks(edge_f[:, b, :], TG), ALU.not_equal))
                            link(v.tensor_scalar(o[:, :, at:at + TG], o[:, :, at:at + TG], NEG, None, ALU.mult))

        def softmax_buffers(sb, C):
            few, many = ([C, H, TG + 1], f32), ([P, C, P], f32)
            shapes = dict(L=([P, P], f32), Lc=many if C > 1 else ([P, 1], f32), pen=([P, C, P] if C > 1 else [P, 1], bf16),
                          F=many, B=many, rowF=few, rowB=few, CF=few, CB=few, sumF=few, sumB=few,
                          ini_row=([C, 2, P], f32), ini=([P, 2, C], f32), m=([P, P], f32), d=([P, P], f32),
                          ex=([P, P], f32), keep=([P, 2, P], bf16), row_keep=([C, 2, ROW], bf16),
                          df=([P, C], f32), f=([P, C], f32), total=([P, C], f32), factor=([P, C], f32),
                          alpha=([P, 2, H, TG], f32), attE=([P, 2, H, TG], f32))
            return dict(C=C, **{k: sb("sm_" + k, *shape) for k, shape in shapes.items()})

        LINKS = {1: dict(tails=0, carries=0, maxima=3, sum_tails=9, sum_carries=10, weights=13, end=20),
                 R: dict(tails=0, carries=2, maxima=5, sum_tails=14, sum_carries=16, weights=19, end=29)}
        PIECES = ["tails", "carries", "maxima", "sum_tails", "sum_carries", "weights", "end"]
        LAG = QG + 4

        def linker(dve, tag, C, G, piece):
            count = [LINKS[C][piece]]

            def link(ins):
                count[0] += 1
                ins.then_inc(sem(tag + "sm_chain"), 1)
                dve.wait_ge(sem(tag + "sm_chain"), G * LINKS[C]["end"] + count[0])

            def done():
                after = PIECES[PIECES.index(piece) + 1]
                assert count[0] == LINKS[C][after], (piece, C, count)
            link.done = done
            return link

        def segment_scans(b, c, resets, data, starts, op):
            v = nc.vector
            last = ALU.max if op == ALU.add else ALU.add
            v.tensor_tensor_scan(out=b["F"][:, c, :], data0=resets[0], data1=data, initial=starts[0], op0=op, op1=last)
            return v.tensor_tensor_scan(out=b["B"][:, c, ::-1], data0=resets[1], data1=data[:, ::-1],
                                        initial=starts[1], op0=op, op1=last)

        def scores_of(b, c):
            return b["Lc"][:, c, :] if b["C"] > 1 else b["L"][:, :]

        def exps_of(b, c):
            return b["Lc"][:, c, :] if b["C"] > 1 else b["ex"][:, :]

        def flat(a):
            return a.rearrange("c h t -> c (h t)")

        def softmax_tails(dve, b, tag, g, G, types):
            v, C = nc.vector, b["C"]
            link = linker(dve, tag, C, G, "tails")
            dve.wait_ge(sem(tag + "L_ready"), G + 1)
            if C > 1:
                for c in range(C):
                    last = v.tensor_scalar(b["pen"][:, c, :], types[:, ds(g * P, P)], float(c), NEG, ALU.not_equal, ALU.mult)
                link(last)
                link(v.tensor_tensor(b["Lc"][:, :, :], b["pen"][:, :, :],
                                     b["L"][:, :].unsqueeze(1).to_broadcast([P, C, P]), ALU.add))
            for c in range(C):
                last = segment_scans(b, c, (rstF[:, ds(g * P, P)], rstB[:, ds(g * P, P)]), scores_of(b, c),
                                     (NEG, NEG), ALU.add)
            last.then_inc(sem(tag + "tails_ready"), 1)
            link.done()

        def carry_scans(b, rowF, rowB, resets, start, op):
            v = nc.vector
            last = ALU.max if op == ALU.add else ALU.add
            v.tensor_tensor_scan(out=flat(b["CF"][:, :, :]), data0=resets[0], data1=flat(rowF[:, :, :]),
                                 initial=start, op0=op, op1=last)
            return v.tensor_tensor_scan(out=flat(b["CB"][:, :, :])[:, ::-1], data0=resets[1],
                                        data1=flat(rowB[:, :, :])[:, ::-1], initial=start, op0=op, op1=last)

        def carries_out(dve, b, tag, rowF, link):
            v = nc.vector
            v.tensor_copy(rowF[:, :, 0:1], b["CF"][:, :, TG:TG + 1])
            v.tensor_copy(b["ini_row"][:, 0, :].rearrange("c (h t) -> c h t", h=H), b["CF"][:, :, 0:TG])
            link(v.tensor_copy(b["ini_row"][:, 1, :].rearrange("c (h t) -> c h t", h=H), b["CB"][:, :, 1:TG + 1]))
            dve.sem_inc(sem(tag + "ini_rows"), 1)

        def softmax_carries(dve, b, tag, g, G, pM):
            v, C = nc.vector, b["C"]
            link = linker(dve, tag, C, G, "carries")
            dve.wait_ge(sem(tag + "rows_ready"), 2 * G + 1)
            v.tensor_copy(b["rowF"][:, :, 1:TG + 1], pM[0:C, 128:256].rearrange("c (h t) -> c h t", h=H))
            link(v.tensor_copy(b["rowB"][:, :, 0:TG], pM[0:C, 256:384].rearrange("c (h t) -> c h t", h=H)))
            link(carry_scans(b, b["rowF"], b["rowB"], (rowrF[0:C, ds(g * ROW, ROW)], rowrB[0:C, ds(g * ROW, ROW)]),
                             NEG, ALU.add))
            carries_out(dve, b, tag, b["rowF"], link)
            link.done()

        def scans_with_carries(dve, b, tag, G, pM, resets, data, op, link, nth):
            v, C = nc.vector, b["C"]
            dve.wait_ge(sem(tag + "ini_ready"), 2 * G + nth)
            link(v.tensor_copy(b["ini"][:, :, :], pM[:, 384:384 + 2 * C].rearrange("p (k c) -> p k c", k=2)))
            for c in range(C):
                last = segment_scans(b, c, resets, data(b, c), (b["ini"][:, 0, c:c + 1], b["ini"][:, 1, c:c + 1]), op)
            link(last)

        def softmax_maxima(dve, b, tag, g, G, pM):
            v, C, F, B = nc.vector, b["C"], b["F"], b["B"]
            link = linker(dve, tag, C, G, "maxima")
            scans_with_carries(dve, b, tag, G, pM, (rstF[:, ds(g * P, P)], rstB[:, ds(g * P, P)]), scores_of,
                               ALU.add, link, 1)
            link(v.tensor_tensor(F[:, :, :], F[:, :, :], B[:, :, :], ALU.max))
            link(v.tensor_tensor(b["df"][:, :], b["ini"][:, 0, :], F[:, :, 0:1].rearrange("p c o -> p (c o)"), ALU.subtract))
            link(v.tensor_scalar(b["df"][:, :], b["df"][:, :], 0.0, None, ALU.min))
            top = F[:, 0, :]
            if C > 1:
                link(v.tensor_tensor(F[:, :, :], F[:, :, :], b["pen"][:, :, :], ALU.add))
                link(v.tensor_tensor(B[:, 0:2, :], F[:, 0:2, :], F[:, 2:4, :], ALU.max))
                link(v.tensor_tensor(b["m"][:, :], B[:, 0, :], B[:, 1, :], ALU.max))
                top = b["m"][:, :]
            link(v.tensor_tensor(b["d"][:, :], b["L"][:, :], top, ALU.subtract))
            dve.sem_inc(sem(tag + "d_ready"), 1)
            link.done()

        def softmax_sum_tails(dve, b, tag, g, G):
            v, C = nc.vector, b["C"]
            link = linker(dve, tag, C, G, "sum_tails")
            v.tensor_scalar(b["keep"][:, 0, :], rstF[:, ds(g * P, P)], 0.0, None, ALU.is_equal)
            v.tensor_scalar(b["keep"][:, 1, :], rstB[:, ds(g * P, P)], 0.0, None, ALU.is_equal)
            v.tensor_scalar(b["row_keep"][:, 0, :], rowrF[0:C, ds(g * ROW, ROW)], 0.0, None, ALU.is_equal)
            link(v.tensor_scalar(b["row_keep"][:, 1, :], rowrB[0:C, ds(g * ROW, ROW)], 0.0, None, ALU.is_equal))
            dve.wait_ge(sem(tag + "ex_ready"), G + 1)
            if C > 1:
                link(v.scalar_tensor_tensor(out=b["Lc"][:, :, :], in0=b["pen"][:, :, :], scalar=0.0,
                                            in1=b["ex"][:, :].unsqueeze(1).to_broadcast([P, C, P]),
                                            op0=ALU.is_equal, op1=ALU.mult))
            for c in range(C):
                last = segment_scans(b, c, (b["keep"][:, 0, :], b["keep"][:, 1, :]), exps_of(b, c), (0.0, 0.0), ALU.mult)
            last.then_inc(sem(tag + "sum_tails_ready"), 1)
            link.done()

        def softmax_sum_carries(dve, b, tag, G, pM):
            v, C = nc.vector, b["C"]
            link = linker(dve, tag, C, G, "sum_carries")
            dve.wait_ge(sem(tag + "rows_ready"), 2 * G + 2)
            v.tensor_copy(b["sumF"][:, :, 1:TG + 1], pM[0:C, 128:256].rearrange("c (h t) -> c h t", h=H))
            v.tensor_copy(b["sumB"][:, :, 0:TG], pM[0:C, 256:384].rearrange("c (h t) -> c h t", h=H))
            link(v.tensor_tensor(b["sumF"][:, :, 0:1], b["sumF"][:, :, 0:1],
                                 pM[0:C, 0:128].rearrange("c (h t) -> c h t", h=H)[:, :, 0:1], ALU.mult))
            link(carry_scans(b, b["sumF"], b["sumB"], (b["row_keep"][:, 0, :], b["row_keep"][:, 1, :]), 0.0, ALU.mult))
            carries_out(dve, b, tag, b["sumF"], link)
            link.done()

        def softmax_weights(dve, b, tag, G, pM):
            v, C, F, B = nc.vector, b["C"], b["F"], b["B"]
            link = linker(dve, tag, C, G, "weights")
            scans_with_carries(dve, b, tag, G, pM, (b["keep"][:, 0, :], b["keep"][:, 1, :]), exps_of, ALU.mult, link, 2)
            link(v.tensor_tensor(F[:, :, :], F[:, :, :], B[:, :, :], ALU.add))
            own = b["Lc"][:, :, 0:1] if C > 1 else b["ex"][:, 0:1].unsqueeze(1)
            v.tensor_tensor(b["total"][:, :].unsqueeze(2), F[:, :, 0:1], own, ALU.subtract)
            both = F[:, 0, :]
            if C > 1:
                link(v.scalar_tensor_tensor(out=B[:, :, :], in0=b["pen"][:, :, :], scalar=0.0, in1=F[:, :, :],
                                            op0=ALU.is_equal, op1=ALU.mult))
                link(v.tensor_tensor(B[:, 0:2, :], B[:, 0:2, :], B[:, 2:4, :], ALU.add))
                link(v.tensor_tensor(b["m"][:, :], B[:, 0, :], B[:, 1, :], ALU.add))
                both = b["m"][:, :]
            link(v.tensor_tensor(b["d"][:, :], both, b["ex"][:, :], ALU.subtract))
            v.tensor_scalar(b["total"][:, :], b["total"][:, :], 1e-16, None, ALU.add)
            link(v.tensor_scalar(b["d"][:, :], b["d"][:, :], 1e-16, None, ALU.add))
            v.reciprocal(b["total"][:, :], b["total"][:, :])
            link(v.reciprocal(b["d"][:, :], b["d"][:, :]))
            v.tensor_tensor(b["factor"][:, :], b["total"][:, :], b["ini"][:, 0, :], ALU.mult)
            link(v.tensor_tensor(b["ex"][:, :], b["ex"][:, :], b["d"][:, :], ALU.mult))
            dve.sem_inc(sem(tag + "att_ready"), 1)
            link.done()

        def turn_alpha(pe, b, tag, par, G, pM):
            pe.wait_ge(sem(tag + "alpha"), (G + 1) * QG)
            nc.tensor.transpose(pM[:, 0:128], b["alpha"][:, par, :, :].rearrange("p h t -> p (h t)"),
                                ident[:, :]).then_inc(sem(tag + "lt"), 1)

        def tails_to_rows(b, tag, pM):
            C = b["C"]
            nc.tensor.matmul(pM[0:C, 128:256], b["F"][:, :, P - 1], ident[:, :], start=True, stop=True)
            nc.tensor.matmul(pM[0:C, 256:384], b["B"][:, :, 0], ident[:, :], start=True,
                             stop=True).then_inc(sem(tag + "rows_ready"), 1)

        def turn_tails(pe, b, tag, G, pM):
            pe.wait_ge(sem(tag + "tails_ready"), G + 1)
            tails_to_rows(b, tag, pM)

        def turn_sum_tails(pe, b, tag, G, pM):
            pe.wait_ge(sem(tag + "sum_tails_ready"), G + 1)
            nc.tensor.matmul(pM[0:b["C"], 0:128], b["f"][:, :], ident[:, :], start=True, stop=True)
            tails_to_rows(b, tag, pM)

        def turn_carries(pe, b, tag, G, pM, nth):
            C = b["C"]
            pe.wait_ge(sem(tag + "ini_rows"), 2 * G + nth)
            nc.tensor.matmul(pM[:, 384:384 + C], b["ini_row"][:, 0, :], ident[0:C, 0:C], start=True, stop=True)
            nc.tensor.matmul(pM[:, 384 + C:384 + 2 * C], b["ini_row"][:, 1, :], ident[0:C, 0:C], start=True,
                             stop=True).then_inc(sem(tag + "ini_ready"), 1)

        def copy_alpha(act, b, tag, G, pM):
            act.wait_ge(sem(tag + "lt"), G + 1)
            nc.scalar.activation(b["L"][:, :], pM[:, 0:128], ACT.Copy).then_inc(sem(tag + "L_ready"), 1)

        def exps(act, b, tag, G, scale):
            a = nc.scalar
            act.wait_ge(sem(tag + "d_ready"), G + 1)
            a.activation(b["f"][:, :], b["df"][:, :], ACT.Exp, scale=scale)
            a.activation(b["ex"][:, :], b["d"][:, :], ACT.Exp, scale=scale).then_inc(sem(tag + "ex_ready"), 1)

        def turn_weights(pe, b, tag, G, pX):
            C = b["C"]
            pe.wait_ge(sem(tag + "att_ready"), G + 1)
            nc.tensor.matmul(pX[:, 128:128 + C], head_sel[:, :], b["factor"][:, :], start=True, stop=True)
            nc.tensor.transpose(pX[:, 0:128], b["ex"][:, :], ident[:, :]).then_inc(sem(tag + "att_turned"), 1)

        def copy_weights(act, b, tag, par, G, pX):
            act.wait_ge(sem(tag + "att_turned"), G + 1)
            nc.scalar.activation(b["attE"][:, par, :, :], pX[:, 0:128].rearrange("p (h t) -> p h t", h=H),
                                 ACT.Copy).then_inc(sem(tag + "attE"), 1)

        def softmax_early(dve, b, tag, q, g, G, pM):
            if q == 1:
                softmax_carries(dve, b, tag, g, G, pM)
            if q == 2:
                softmax_sum_tails(dve, b, tag, g, G)
            if q == 3:
                softmax_weights(dve, b, tag, G, pM)

        def softmax_late(dve, b, tag, q, g, G, pM, types):
            if q == 0:
                softmax_tails(dve, b, tag, g, G, types)
            if q == 1:
                softmax_maxima(dve, b, tag, g, G, pM)
            if q == 2:
                softmax_sum_carries(dve, b, tag, G, pM)

        def turns_first(pe, b, tag, q, par, G, pM):
            if q == 0:
                turn_alpha(pe, b, tag, 1 - par, G, pM)
            if q == 1:
                turn_tails(pe, b, tag, G, pM)
            if q == 3:
                turn_carries(pe, b, tag, G, pM, 2)

        def turns_between(pe, b, tag, q, G, pM, pX):
            if q == 1:
                turn_carries(pe, b, tag, G, pM, 1)
            if q == 2:
                turn_sum_tails(pe, b, tag, G, pM)
            if q == 3:
                turn_weights(pe, b, tag, G, pX)

        def shifted(g, q, par, by):
            step, q = divmod(q + by, QG)
            g = g + step if step else g
            if isinstance(g, int) and not 0 <= g < GROUPS:
                return None
            return g, q, par if step % 2 == 0 else 1 - par

        def started(g):
            return not isinstance(g, int) or 1 <= g <= GROUPS

        def scored(g):
            return not isinstance(g, int) or g < GROUPS

        def halved(g, par):
            return (g - par) // 2

        LAST = GROUPS - 1

        def all_turns(eng, turn, tail=LAG):
            def group(g, par):
                for q in range(QG):
                    turn(g, q, par)
            for g in range(3):
                group(g, g % 2)
            with eng.Fori(1, (GROUPS - 1) // 2 - 1) as k:
                group(2 * k + 1, 1)
                group(2 * k + 2, 0)
            group(GROUPS - 2, 1)
            group(LAST, 0)
            for q in range(tail):
                turn(GROUPS + q // QG, q % QG, (1 + q // QG) % 2)

        def gather_group(pool, tag, l, g, par, tab, idx_all, idx_now, rows, read="alpha", used="msg"):
            if isinstance(g, int) and g < 2:
                pass
            else:
                pool.wait_ge(sem(tag + read), (l * GROUPS + g - 1) * QG)
                settle(pool)
            nc.gpsimd.tensor_copy(idx_now[:, par, :], idx_all[:, ds(g * TG, TG)]).then_inc(sem(tag + "idx"), 1)
            pool.wait_ge(sem(tag + "idx"), l * GROUPS + g + 1)
            settle(pool)
            for q in range(QG):
                if not (isinstance(g, int) and g < 2):
                    pool.wait_ge(sem(tag + used), (l * GROUPS + g - 2) * QG + q + 1)
                    settle(pool)
                for j in range(4):
                    t = 4 * q + j
                    nc.gpsimd.indirect_dma_start(
                        rows[:, par * TG + t, :], None, tab,
                        bass.IndirectOffsetOnAxis(ap=idx_now[:, par, t:t + 1], axis=0)
                    ).then_inc(sem(f"rows{par}_{q}"), 16)

        def take_group(dve, tag, l, g, pairs):
            for now, whole, per in pairs:
                last = nc.vector.tensor_copy(now, whole[:, ds(g * (TG * per), TG * per)])
            last.then_inc(sem(tag + "taken"), 1)
            dve.wait_ge(sem(tag + "taken"), l * GROUPS + g + 1)
            settle(dve)

        def rows_there(eng, turn, half, par, q):
            eng.wait_ge(sem(f"rows{par}_{q}"), 64 * (turn * ((GROUPS + 1) // 2 - par) + half + 1))

        def gather_all(pool, group):
            group(0, 0)
            group(1, 1)
            with pool.Fori(0, (GROUPS - 3) // 2) as k:
                group(2 * k + 2, 0)
                group(2 * k + 3, 1)
            group(GROUPS - 1, 0)

        def conv_project(l, sb, pb):
            w = sb("w", [P, 4 * D])
            bias = sb("bias", [P, 3 * D])
            stage = sb("stage", [P, 2, 4, 3 * D])
            pp = [pb(f"pp{i}", [P, 512]) for i in range(4)]
            loaded, prod, copied = sem("proj_w"), sem("proj_prod"), sem("proj_copied")
            stored = [sem("proj_stored0"), sem("proj_stored1")]
            nt = NPAD // P
            even, odd = (NB + 1) // 2, NB // 2
            with nc.Block() as block:
                @block.sync
                def _(sp):
                    sp.dma_start(w[:, :], w0[ds(l, 1), :, :].rearrange("l p n -> (l p) n")).then_inc(loaded, 16)
                    sp.dma_start(bias[:, :], b0[ds(l, 1), :].to_broadcast([P, 3 * D])).then_inc(loaded, 16)
                    for b in range(NB):
                        sp.wait_ge(copied, l * nt + 4 * (b + 1))
                        rows = slice(b * BW, (b + 1) * BW)
                        sp.dma_start(kv_tab[rows, :].rearrange("(j p) f -> p j f", p=P),
                                     stage[:, b % 2, :, 0:2 * D]).then_inc(stored[b % 2], 16)
                        sp.dma_start(q_tab[rows, :].rearrange("(j p) f -> p j f", p=P),
                                     stage[:, b % 2, :, 2 * D:3 * D]).then_inc(stored[b % 2], 16)
                    sp.wait_ge(stored[0], (l + 1) * 32 * even)
                    settle(sp)
                    sp.wait_ge(stored[1], (l + 1) * 32 * odd)
                    settle(sp)

                @block.tensor
                def _(pe):
                    pe.wait_ge(loaded, 32 * (l + 1))
                    for t in range(nt):
                        if t >= 4:
                            pe.wait_ge(copied, l * nt + t - 3)
                        nc.tensor.matmul(pp[t % 4][:, 0:3 * D], xT[:, t * P:(t + 1) * P], w[:, 0:3 * D],
                                         start=True, stop=True).then_inc(prod, 1)

                @block.vector
                def _(dve):
                    dve.wait_ge(loaded, 32 * (l + 1))
                    for t in range(nt):
                        b = t // 4
                        if t % 4 == 0 and b >= 2:
                            n = even if b % 2 == 0 else odd
                            dve.wait_ge(stored[b % 2], l * 32 * n + 32 * (b // 2))
                        dve.wait_ge(prod, l * nt + t + 1)
                        nc.vector.tensor_tensor(stage[:, b % 2, t % 4, :], pp[t % 4][:, 0:3 * D], bias[:, :],
                                                ALU.add).then_inc(copied, 1)
            return w

        def conv_edges(l, sb, pb, acc):
            tag = "c_"
            kv = sb("kv", [P, 2 * TG, 2 * D])
            S = sb("S", [P, 2 * TG, P])
            ST = sb("ST", [P, 2, 4, P])
            qwin = sb("qwin", [P, 4, 4, D])
            prodb = sb("prodb", [P, 4, D])
            wide = sb("wide", [P, 2, 4, D])
            msg = sb("msg", [P, 2, 4, D])
            idx_now = sb("idx_now", [P, 2, TG], i32)
            minus_rel = sb("minus_rel", [P, 2, TG])
            away = sb("away", [P, 2, 4, P])
            sm = softmax_buffers(sb, 1)
            pT = [pb(f"pT{i}", [P, 4, P]) for i in range(2)]
            pQ = [pb(f"pQ{i}", [P, 4, D]) for i in range(2)]
            pA = [pb(f"pA{i}", [P, 4, P]) for i in range(2)]
            pM = pb("pM", [P, 512])
            pX = pb("pX", [P, 512])

            def quad(g, q):
                return (l * GROUPS + g) * QG + q

            def skip(g):
                return isinstance(g, int) and g == 0

            with nc.Block() as block:
                @block.gpsimd
                def _(pool):
                    gather_all(pool, lambda g, par: gather_group(pool, tag, l, g, par, kv_tab, src_all, idx_now, kv))

                @block.sync
                def _(sp):
                    def group(g, par):
                        for q in range(QG):
                            n = quad(g, q)
                            at = bases(sp, g * TG + 4 * q)
                            if not (skip(g) and q < 4):
                                sp.wait_ge(sem(tag + "qx"), n - 3)
                                settle(sp)
                            for j in range(4):
                                sp.dma_start(qwin[:, q % 4, j, :], q_tab[ds(at[j], P), :]
                                             ).then_inc(sem(f"{tag}qwin{q % 4}"), 16)
                    group(0, 0)
                    with sp.Fori(1, GROUPS) as g:
                        group(g, None)

                @block.tensor
                def _(pe):
                    def scores_turn(g, q, par):
                        n = quad(g, q)
                        pe.wait_ge(sem(tag + "S"), n + 1)
                        if not (skip(g) and q < 2):
                            pe.wait_ge(sem(tag + "ST"), n - 1)
                        for j in range(4):
                            last = nc.tensor.transpose(pT[q % 2][:, j, :], S[:, par * TG + 4 * q + j, :], ident[:, :])
                        last.then_inc(sem(tag + "turned"), 1)

                    def scores(g, q, par):
                        n = quad(g, q)
                        pe.wait_ge(sem(tag + "ST"), n + 1)
                        pe.wait_ge(sem(f"{tag}qwin{q % 4}"), 64 * ((l * GROUPS + g) * (QG // 4) + q // 4 + 1))
                        if not (skip(g) and q < 2):
                            pe.wait_ge(sem(tag + "prod"), n - 1)
                        for j in range(4):
                            last = nc.tensor.matmul(pQ[q % 2][:, j, :], ST[:, q % 2, j, :], qwin[:, q % 4, j, :],
                                                    start=True, stop=True)
                        last.then_inc(sem(tag + "qx"), 1)

                    def sums(g, q, par):
                        m = quad(g, q)
                        pe.wait_ge(sem(tag + "msg"), m + 1)
                        if not (skip(g) and q < 2):
                            pe.wait_ge(sem(tag + "acc"), 4 * (m - 1))
                        for j in range(4):
                            last = nc.tensor.matmul(pA[q % 2][:, j, :], msg[:, q % 2, j, :],
                                                    S[:, par * TG + 4 * q + j, :], start=True, stop=True)
                        last.then_inc(sem(tag + "agg"), 1)

                    def turn(g, q, par):
                        nxt, after, late = (shifted(g, q, par, by) for by in (2, 1, -LAG))
                        if started(g):
                            G = l * GROUPS + g - 1
                            turns_first(pe, sm, tag, q, par, G, pM)
                        if after:
                            scores(*after)
                        if nxt:
                            scores_turn(*nxt)
                        if started(g):
                            turns_between(pe, sm, tag, q, G, pM, pX)
                        if late:
                            sums(*late)
                    scores_turn(0, 0, 0)
                    scores_turn(0, 1, 0)
                    scores(0, 0, 0)
                    all_turns(pe, turn, LAG + 1)

                @block.scalar
                def _(act):
                    def build(g, q, par):
                        n = quad(g, q)
                        if q == 0:
                            act.wait_ge(sem(tag + "taken"), l * GROUPS + g + 1)
                        for j in range(4):
                            last = nc.scalar.activation(away[:, q % 2, j, :], iota_row[:, :], ACT.Abs,
                                                        bias=minus_rel[:, par, 4 * q + j:4 * q + j + 1])
                        last.then_inc(sem(tag + "away"), 1)
                        act.wait_ge(sem(tag + "away"), n + 1)
                        if not (isinstance(g, int) and g < 2):
                            act.wait_ge(sem(tag + "agg"), n - 2 * QG + 1)
                        s = par * TG + 4 * q
                        nc.scalar.activation(S[:, s:s + 4, :], away[:, q % 2, :, :], ACT.Relu, bias=ones[:, 0:1],
                                             scale=-1.0).then_inc(sem(tag + "S"), 1)

                    def st_copy(g, q):
                        n = quad(g, q)
                        act.wait_ge(sem(tag + "turned"), n + 1)
                        if not (skip(g) and q < 2):
                            act.wait_ge(sem(tag + "qx"), n - 1)
                        nc.scalar.activation(ST[:, q % 2, :, :], pT[q % 2][:, :, :], ACT.Copy
                                             ).then_inc(sem(tag + "ST"), 1)

                    def spread(g, q, par):
                        m = quad(g, q)
                        if q == 0:
                            act.wait_ge(sem(tag + "attE"), l * GROUPS + g + 1)
                        if not (skip(g) and q < 2):
                            act.wait_ge(sem(tag + "msg"), m - 1)
                        src = sm["attE"][:, par, :, 4 * q:4 * q + 4].rearrange("p h t -> p t h")
                        nc.scalar.activation(wide[:, q % 2, :, :].rearrange("p t (h f) -> p t h f", h=H),
                                             src.unsqueeze(3).to_broadcast([P, 4, H, HD]), ACT.Copy
                                             ).then_inc(sem(tag + "wide"), 1)

                    def turn(g, q, par):
                        far, nxt, late = (shifted(g, q, par, by) for by in (3, 2, -LAG))
                        G = l * GROUPS + g - 1
                        if started(g) and q == 0:
                            copy_alpha(act, sm, tag, G, pM)
                        if started(g) and q == 2:
                            exps(act, sm, tag, G, SCALE)
                        if late:
                            spread(*late)
                        if nxt:
                            st_copy(*nxt[:2])
                        if started(g) and q == 3:
                            copy_weights(act, sm, tag, 1 - par, G, pX)
                        if far:
                            build(*far)
                    build(0, 0, 0)
                    build(0, 1, 0)
                    st_copy(0, 0)
                    st_copy(0, 1)
                    build(0, 2, 0)
                    all_turns(act, turn, LAG + 1)

                @block.vector
                def _(dve):
                    v = nc.vector

                    def weigh(g, q, par):
                        m = quad(g, q)
                        dve.wait_ge(sem(tag + "wide"), m + 1)
                        if not (skip(g) and q < 2):
                            dve.wait_ge(sem(tag + "agg"), m - 1)
                        s = par * TG + 4 * q
                        v.tensor_tensor(msg[:, q % 2, :, :], kv[:, s:s + 4, D:2 * D], wide[:, q % 2, :, :],
                                        ALU.mult).then_inc(sem(tag + "msg"), 1)

                    def take(g, par):
                        v.tensor_scalar(minus_rel[:, par, :], rel[:, ds(g * TG, TG)], -1.0, None, ALU.mult
                                        ).then_inc(sem(tag + "taken"), 1)

                    def add(g, q, at, j):
                        m = quad(g, q)
                        if j == 0:
                            dve.wait_ge(sem(tag + "agg"), m + 1)
                        if not (skip(g) and q == 0 and j == 0):
                            dve.wait_ge(sem(tag + "acc"), 4 * m + j)
                        win = acc[:, ds(at[j], P)]
                        v.tensor_tensor(win, win, pA[q % 2][:, j, :], ALU.add).then_inc(sem(tag + "acc"), 1)

                    def products(g, q, par):
                        n = quad(g, q)
                        dve.wait_ge(sem(tag + "qx"), n + 1)
                        rows_there(dve, l, halved(g, par), par, q)
                        s = par * TG + 4 * q
                        if not (skip(g) and q == 0):
                            dve.wait_ge(sem(tag + "alpha"), n)
                        v.tensor_tensor(prodb[:, :, :], kv[:, s:s + 4, 0:D], pQ[q % 2][:, :, :],
                                        ALU.mult).then_inc(sem(tag + "prod"), 1)

                    def score(g, q, par):
                        dve.wait_ge(sem(tag + "prod"), quad(g, q) + 1)
                        v.tensor_reduce(sm["alpha"][:, par, :, 4 * q:4 * q + 4].rearrange("p h t -> p t h"),
                                        prodb[:, :, :].rearrange("p t (h f) -> p t h f", h=H), AX.X,
                                        ALU.add).then_inc(sem(tag + "alpha"), 1)

                    def rescale(g):
                        G = l * GROUPS + g
                        _, at = nc.values_load_multi_w_load_instructions(
                            base_i[0:1, ds(g * TG, 1)], engines=[dve.engine], min_val=0, max_val=N,
                            skip_runtime_bounds_check_because="a destination")
                        dve.wait_ge(sem(tag + "attE"), G + 1)
                        if not skip(g):
                            dve.wait_ge(sem(tag + "acc"), 4 * QG * G)
                        col = acc[:, ds(at[0], 1)]
                        v.tensor_scalar(col, col, pX[:, 128:129], None, ALU.mult).then_inc(sem(tag + "scaled"), 1)
                        dve.wait_ge(sem(tag + "scaled"), G + 1)
                        settle(dve)

                    def turn(g, q, par):
                        nxt, late, last = (shifted(g, q, par, by) for by in (4, -LAG, -LAG - 1))
                        G = l * GROUPS + g - 1
                        at = bases(dve, last[0] * TG + 4 * last[1]) if last else None
                        if last:
                            add(last[0], last[1], at, 0)
                        if scored(g):
                            products(g, q, par)
                        if started(g):
                            softmax_early(dve, sm, tag, q, g - 1, G, pM)
                        if last:
                            add(last[0], last[1], at, 1)
                        if late:
                            weigh(*late)
                        if last:
                            add(last[0], last[1], at, 2)
                        if scored(g):
                            score(g, q, par)
                        if last:
                            add(last[0], last[1], at, 3)
                        if nxt and nxt[1] == 0:
                            take(nxt[0], nxt[2])
                        if started(g):
                            softmax_late(dve, sm, tag, q, g - 1, G, pM, None)
                            if q == 4:
                                rescale(g - 1)

                    v.memset(acc[:, :], 0.0).then_inc(sem(tag + "clear"), 1)
                    v.memset(sm["rowF"][:, :, :], NEG)
                    v.memset(sm["sumF"][:, :, :], 0.0)
                    v.memset(sm["sumB"][:, :, :], 0.0)
                    v.memset(sm["rowB"][:, :, :], NEG).then_inc(sem(tag + "clear"), 1)
                    dve.wait_ge(sem(tag + "clear"), 2 * (l + 1))
                    settle(dve)
                    take(0, 0)
                    all_turns(dve, turn, LAG + 1)

        def node_stage(tag, l, kind, sb, pb, extra):
            h = sb("ns_h", [P, NPAD])
            s = sb("ns_s", [P, NPAD])
            ps = [pb(f"ns_p{i}", [P, BW]) for i in range(3)]
            pm = [pb(f"ns_m{i}", [P, BW]) for i in range(4)]
            pv = pb("ns_v", [NB, BW])
            inv = sb("ns_inv", [NB, BW])
            to_row = sb("ns_to_row", [P, NB, NB])
            from_row = sb("ns_from_row", [NB, NB, P])
            cols = sb("ns_cols", [P, 3])
            v, a = nc.vector, nc.scalar
            S_ = lambda n: sem(tag + n)
            o = l * NB
            blk = lambda b: slice(b * BW, (b + 1) * BW)

            with nc.Block() as block:
                @block.sync
                def _(sp):
                    sp.dma_start(cols[:, :], extra["cols"]).then_inc(S_("cols"), 16)
                    sp.wait_ge(S_("cols"), 16 * (l + 1))
                    settle(sp)
                    if "fetch" in extra:
                        extra["fetch"](sp, S_, range(0, 8, 2))
                    if kind == "last":
                        sp.wait_ge(S_("skip"), o + NB)
                        sp.dma_start(xT[:, :], xT_in).then_inc(S_("x_again"), 16)
                        sp.wait_ge(S_("x_again"), 16)

                @block.tensor
                def _(pe):
                    if "pre" in extra:
                        extra["pre"](pe, "tensor", ps, S_, o, blk)
                    for b in range(NB):
                        pe.wait_ge(S_("h"), o + b + 1)
                        if b >= 4:
                            pe.wait_ge(S_("cent"), o + b - 3)
                        nc.tensor.matmul(pm[b % 4][:, :], mean_w[:, :], h[:, blk(b)], start=True,
                                         stop=True).then_inc(S_("mean"), 1)
                    pe.wait_ge(S_("sel"), l + 1)
                    for b in range(NB):
                        pe.wait_ge(S_("sq"), o + b + 1)
                        last = nc.tensor.matmul(pv[:, :], to_row[:, b, :], s[:, blk(b)], start=b == 0, stop=b == NB - 1)
                    last.then_inc(S_("var"), 1)
                    pe.wait_ge(S_("inv"), 2 * (l + 1))
                    pe.wait_ge(S_("cent"), o + NB)
                    for b in range(NB):
                        if b >= 4:
                            pe.wait_ge(S_("norm"), o + b - 3)
                        nc.tensor.matmul(pm[b % 4][:, :], from_row[:, b, :], inv[:, :], start=True,
                                         stop=True).then_inc(S_("spread"), 1)

                @block.scalar
                def _(act):
                    if "fetch" in extra:
                        extra["fetch"](act, S_, range(1, 8, 2))
                    if "pre" in extra:
                        extra["pre"](act, "scalar", ps, S_, o, blk)
                    for b in range(NB):
                        act.wait_ge(S_("cent"), o + b + 1)
                        a.activation(s[:, blk(b)], h[:, blk(b)], ACT.Square).then_inc(S_("sq"), 1)
                    act.wait_ge(S_("var"), l + 1)
                    a.activation(inv[:, :], pv[:, :], ACT.Sqrt, bias=eps_col[0:NB, :]).then_inc(S_("inv"), 1)
                    if kind == "conv":
                        for b in range(NB):
                            act.wait_ge(S_("cols"), 16 * (l + 1))
                            act.wait_ge(S_("norm"), o + b + 1)
                            a.activation(s[:, blk(b)], h[:, blk(b)], ACT.Gelu, bias=cols[:, 2:3],
                                         scale=cols[:, 1:2]).then_inc(S_("act"), 1)

                @block.vector
                def _(dve):
                    v.memset(to_row[:, :, :], 0.0).then_inc(S_("sel0"), 1)
                    for b in range(NB):
                        v.tensor_copy(from_row[:, b, :], ident[0:NB, b:b + 1].to_broadcast([NB, P]))
                    dve.wait_ge(S_("sel0"), l + 1)
                    settle(dve)
                    for b in range(NB):
                        last = v.memset(to_row[:, b, b:b + 1], 1.0 / D)
                    last.then_inc(S_("sel"), 1)
                    dve.wait_ge(S_("cols"), 16 * (l + 1))
                    extra["form"](dve, h, s, ps, cols, S_, o, blk)
                    for b in range(NB):
                        dve.wait_ge(S_("mean"), o + b + 1)
                        v.tensor_tensor(h[:, blk(b)], h[:, blk(b)], pm[b % 4][:, :], ALU.subtract).then_inc(S_("cent"), 1)
                    dve.wait_ge(S_("inv"), 2 * l + 1)
                    v.reciprocal(inv[:, :], inv[:, :]).then_inc(S_("inv"), 1)
                    for b in range(NB):
                        dve.wait_ge(S_("spread"), o + b + 1)
                        to = h if kind == "conv" else xT
                        v.tensor_tensor(to[:, blk(b)], h[:, blk(b)], pm[b % 4][:, :], ALU.mult).then_inc(S_("norm"), 1)
                    if kind == "conv":
                        for b in range(NB):
                            dve.wait_ge(S_("act"), o + b + 1)
                            v.tensor_tensor(xT[:, blk(b)], xT[:, blk(b)], s[:, blk(b)], ALU.add).then_inc(S_("x"), 1)

        def conv_nodes(l, kind, sb, pb, acc, w):
            tag = "n0_"
            v, a = nc.vector, nc.scalar

            def pre(eng, what, ps, S_, o, blk):
                if what == "tensor":
                    for b in range(NB):
                        if b >= 3:
                            eng.wait_ge(S_("sum"), o + b - 2)
                        nc.tensor.matmul(ps[b % 3][:, :], w[:, 3 * D:4 * D], xT[:, blk(b)], start=True,
                                         stop=True).then_inc(S_("skip"), 1)
                elif kind == "last":
                    for b in range(NB):
                        eng.wait_ge(S_("sum"), o + b + 1)
                        a.activation(acc[:, blk(b)], acc[:, blk(b)], ACT.Gelu).then_inc(S_("gelu"), 1)

            def form(dve, h, s, ps, cols, S_, o, blk):
                out_ = acc if kind == "last" else h
                for b in range(NB):
                    dve.wait_ge(S_("skip"), o + b + 1)
                    v.scalar_tensor_tensor(out=out_[:, blk(b)], in0=ps[b % 3][:, :], scalar=cols[:, 0:1],
                                           in1=acc[:, blk(b)], op0=ALU.add, op1=ALU.add
                                           ).then_inc(S_("sum"), 1)
                    if kind == "conv":
                        dve.wait_ge(S_("sum"), o + b + 1)
                        dve.sem_inc(S_("h"), 1)
                if kind == "last":
                    dve.wait_ge(S_("x_again"), 16)
                    for b in range(NB):
                        dve.wait_ge(S_("gelu"), b + 1)
                        v.tensor_tensor(h[:, blk(b)], acc[:, blk(b)], xT[:, blk(b)], ALU.add).then_inc(S_("h"), 1)

            node_stage(tag, l, kind, sb, pb, dict(
                cols=col0[ds(l, 1), :, :].rearrange("l p n -> (l p) n"), pre=pre, form=form))

        def maker(scope, space, suffix):
            return lambda name, shape, dt=f32: scope.enter_context(space(name + suffix, shape, dt))

        def conv_layer(l, kind):
            with ExitStack() as keep:
                acc = maker(keep, nc.sbuf_tensor, kind)("acc", [P, NPAD])
                with ExitStack() as part:
                    wide = maker(keep, nc.sbuf_tensor, kind)
                    narrow = maker(part, nc.sbuf_tensor, kind)
                    w = conv_project(l, lambda name, *a: (wide if name == "w" else narrow)(name, *a),
                                     maker(part, nc.psum_tensor, kind))
                with ExitStack() as part:
                    conv_edges(l, maker(part, nc.sbuf_tensor, kind), maker(part, nc.psum_tensor, kind), acc)
                with ExitStack() as part:
                    conv_nodes(l, kind, maker(part, nc.sbuf_tensor, kind), maker(part, nc.psum_tensor, kind), acc, w)

        def rel_project(sb, pb):
            wcat = sb("wcat", [P, R, RW])
            wt = sb("wt", [P, R, P])
            at = sb("at", [P, R, 2 * H])
            stage = sb("stage", [P, 2, 4, R, RW])
            ad = sb("ad", [P, 2, 4, R * H])
            pw = pb("pw", [P, R, 2 * H])
            pr = [pb(f"pr{i}", [P, 2, RW]) for i in range(4)]
            v, a = nc.vector, nc.scalar
            loaded, folded, put, prod = sem("rp_w"), sem("rp_folded"), sem("rp_put"), sem("rp_prod")
            copied, dsts = sem("rp_copied"), sem("rp_dsts")
            stored = [sem("rp_stored0"), sem("rp_stored1")]
            with nc.Block() as block:
                @block.sync
                def _(sp):
                    sp.dma_start(wcat[:, :, 0:D], w1).then_inc(loaded, 16)
                    sp.dma_start(wt[:, :, :], w1T).then_inc(loaded, 16)
                    sp.dma_start(at[:, :, :], a1.rearrange("o r k h -> o r (k h)")).then_inc(loaded, 16)
                    for b in range(NB):
                        sp.wait_ge(copied, 8 * (b + 1))
                        for r in range(R):
                            first = r * NPAD + b * BW
                            sp.dma_start(rel_tab[first:first + BW, :].rearrange("(j p) f -> p j f", p=P),
                                         stage[:, b % 2, :, r, :]).then_inc(stored[b % 2], 16)
                        sp.wait_ge(dsts, b + 1)
                        sp.dma_start(adst_tab[b * BW:(b + 1) * BW, :].rearrange("(j p) f -> p j f", p=P),
                                     ad[:, b % 2, :, :]).then_inc(stored[b % 2], 16)
                    sp.wait_ge(stored[0], 80 * ((NB + 1) // 2))
                    sp.wait_ge(stored[1], 80 * (NB // 2))

                @block.tensor
                def _(pe):
                    pe.wait_ge(loaded, 48)
                    for r in range(R):
                        last = nc.tensor.matmul(pw[:, r, :], wt[:, r, :], at[:, r, :], start=True, stop=True)
                    last.then_inc(folded, 1)
                    pe.wait_ge(put, 1)
                    for t in range(NT):
                        for u in range(2):
                            n = 2 * t + u
                            if n >= 4:
                                pe.wait_ge(copied, n - 3)
                            nc.tensor.matmul(pr[n % 4][:, :, :], xT[:, t * P:(t + 1) * P], wcat[:, 2 * u:2 * u + 2, :],
                                             start=True, stop=True).then_inc(prod, 1)

                @block.scalar
                def _(act):
                    act.wait_ge(folded, 1)
                    a.activation(wcat[:, :, D:RW], pw[:, :, :], ACT.Copy).then_inc(put, 1)
                    for n in range(2 * NT):
                        b = n // 8
                        if n % 8 == 0 and b >= 2:
                            act.wait_ge(stored[b % 2], 80 * (b // 2))
                            act.wait_ge(dsts, b - 1)
                        act.wait_ge(prod, n + 1)
                        u = n % 2
                        a.activation(stage[:, b % 2, (n // 2) % 4, 2 * u:2 * u + 2, :], pr[n % 4][:, :, :],
                                     ACT.Copy).then_inc(copied, 1)

                @block.vector
                def _(dve):
                    for b in range(NB):
                        dve.wait_ge(copied, 8 * (b + 1))
                        if b >= 2:
                            dve.wait_ge(stored[b % 2], 80 * (b // 2))
                        v.tensor_copy(ad[:, b % 2, :, :].rearrange("p j (r h) -> p j r h", h=H),
                                      stage[:, b % 2, :, :, D + H:RW]).then_inc(dsts, 1)

        def rel_edges(sb, pb, acc, deg, type_f, mask, last_mask, cuts, idx1):
            tag = "r_"
            rows = sb("rows", [P, 2 * TG, RW])
            S = sb("S", [P, 2 * TG, P])
            minus_rel = sb("minus_rel", [P, 2, TG])
            away = sb("away", [P, 2, 4, P])
            ST = sb("ST", [P, 2, 4, P])
            awin = sb("awin", [P, 4, 4, R * H])
            picked = sb("picked", [P, 4, R, H])
            al = sb("al", [P, 4, H])
            wide = sb("wide", [P, 2, 4, D])
            msg = sb("msg", [P, 2, 4, D])
            idx_now = sb("idx_now", [P, 2, TG], i32)
            mask_now = sb("mask_now", [P, TG * R])
            last_now = sb("last_now", [P, 2, TG * R])
            cuts_now = sb("cuts_now", [P, 2, 1])
            carry = sb("carry", [P, R])
            carried = sb("carried", [P, R])
            added = sb("added", [P, 2, R])
            sm = softmax_buffers(sb, R)
            pT = pb("pT", [P, 4, P])
            pQ = [pb(f"pQ{i}", [P, 2, 4 * R * H]) for i in range(2)]
            pA = [pb(f"pA{i}", [P, 4, P]) for i in range(2)]
            pN = [pb(f"pN{i}", [1, 4, P]) for i in range(2)]
            pM = pb("pM", [P, 512])
            quad = lambda g, q: g * QG + q
            skip = lambda g: isinstance(g, int) and g == 0

            with nc.Block() as block:
                @block.gpsimd
                def _(pool):
                    gather_all(pool, lambda g, par: gather_group(pool, tag, 0, g, par, rel_tab, idx1, idx_now, rows))

                @block.sync
                def _(sp):
                    def group(g):
                        for q in range(QG):
                            n = quad(g, q)
                            at = bases(sp, g * TG + 4 * q)
                            if not (skip(g) and q < 4):
                                sp.wait_ge(sem(tag + "qx"), n - 3)
                                settle(sp)
                            for j in range(4):
                                sp.dma_start(awin[:, q % 4, j, :], adst_tab[ds(at[j], P), :]
                                             ).then_inc(sem(f"{tag}qwin{q % 4}"), 16)
                    group(0)
                    with sp.Fori(1, GROUPS) as g:
                        group(g)

                @block.tensor
                def _(pe):
                    def scores_turn(g, q, par):
                        n = quad(g, q)
                        pe.wait_ge(sem(tag + "S"), n + 1)
                        if not (skip(g) and q == 0):
                            pe.wait_ge(sem(tag + "ST"), n)
                        for j in range(4):
                            last = nc.tensor.transpose(pT[:, j, :], S[:, par * TG + 4 * q + j, :], ident[:, :])
                        last.then_inc(sem(tag + "turned"), 1)

                    def scores(g, q, par):
                        n = quad(g, q)
                        pe.wait_ge(sem(tag + "ST"), n + 1)
                        pe.wait_ge(sem(f"{tag}qwin{q % 4}"), 64 * (g * (QG // 4) + q // 4 + 1))
                        if not (skip(g) and q < 2):
                            pe.wait_ge(sem(tag + "prod"), n - 1)
                        for j in range(4):
                            last = nc.tensor.matmul(pQ[q % 2][:, 0, j * R * H:(j + 1) * R * H], ST[:, q % 2, j, :],
                                                    awin[:, q % 4, j, :], start=True, stop=True)
                        last.then_inc(sem(tag + "qx"), 1)

                    def sums(g, q, par):
                        m = quad(g, q)
                        pe.wait_ge(sem(tag + "msg"), m + 1)
                        if not (skip(g) and q < 2):
                            pe.wait_ge(sem(tag + "acc"), 4 * (m - 1))
                        for j in range(4):
                            nc.tensor.matmul(pA[q % 2][:, j, :], msg[:, q % 2, j, :], S[:, par * TG + 4 * q + j, :],
                                             start=True, stop=True)
                        if not (skip(g) and q < 2):
                            pe.wait_ge(sem(tag + "deg"), 4 * (m - 1))
                        for j in range(4):
                            nc.tensor.matmul(pN[q % 2][0:1, j, :], ones[:, 0:1], S[:, par * TG + 4 * q + j, :], start=True,
                                             stop=True)
                        there = shifted(g, q, par, LAG) is not None
                        pe.wait_ge(sem(tag + "prod"), m + LAG + 1 if there else GROUPS * QG)
                        if q < 2 and not skip(g):
                            pe.wait_ge(sem(tag + "added"), 2 * (g - 1) + q + 1)
                        for j in range(4):
                            at = ((q // 2) * 4 + j) * R
                            t = 4 * q + j
                            last = nc.tensor.matmul(pQ[q % 2][:, 1, at:at + R], msg[:, q % 2, j, :],
                                                    last_now[:, par, t * R:(t + 1) * R], start=True, stop=True)
                        last.then_inc(sem(tag + "agg"), 1)

                    def turn(g, q, par):
                        nxt, after, late = (shifted(g, q, par, by) for by in (2, 1, -LAG))
                        if started(g):
                            turns_first(pe, sm, tag, q, par, g - 1, pM)
                        if after:
                            scores(*after)
                        if nxt:
                            scores_turn(*nxt)
                        if started(g):
                            turns_between(pe, sm, tag, q, g - 1, pM, pM)
                        if late:
                            sums(*late)
                    scores_turn(0, 0, 0)
                    scores(0, 0, 0)
                    scores_turn(0, 1, 0)
                    all_turns(pe, turn, LAG + 1)

                @block.scalar
                def _(act):
                    def build(g, q, par):
                        n = quad(g, q)
                        if q == 0:
                            act.wait_ge(sem(tag + "taken"), g + 1)
                        for j in range(4):
                            last = nc.scalar.activation(away[:, q % 2, j, :], iota_row[:, :], ACT.Abs,
                                                        bias=minus_rel[:, par, 4 * q + j:4 * q + j + 1])
                        last.then_inc(sem(tag + "away"), 1)
                        act.wait_ge(sem(tag + "away"), n + 1)
                        if not (isinstance(g, int) and g < 2):
                            act.wait_ge(sem(tag + "agg"), n - 2 * QG + 1)
                        s = par * TG + 4 * q
                        nc.scalar.activation(S[:, s:s + 4, :], away[:, q % 2, :, :], ACT.Relu, bias=ones[:, 0:1],
                                             scale=-1.0).then_inc(sem(tag + "S"), 1)

                    def st_copy(g, q):
                        n = quad(g, q)
                        act.wait_ge(sem(tag + "turned"), n + 1)
                        if not (skip(g) and q < 2):
                            act.wait_ge(sem(tag + "qx"), n - 1)
                        nc.scalar.activation(ST[:, q % 2, :, :], pT[:, :, :], ACT.Copy
                                             ).then_inc(sem(tag + "ST"), 1)

                    def spread(g, q, par):
                        m = quad(g, q)
                        if q == 0:
                            act.wait_ge(sem(tag + "attE"), g + 1)
                        if not (skip(g) and q < 2):
                            act.wait_ge(sem(tag + "msg"), m - 1)
                        src = sm["attE"][:, par, :, 4 * q:4 * q + 4].rearrange("p h t -> p t h")
                        nc.scalar.activation(wide[:, q % 2, :, :].rearrange("p t (h f) -> p t h f", h=H),
                                             src.unsqueeze(3).to_broadcast([P, 4, H, HD]), ACT.Copy
                                             ).then_inc(sem(tag + "wide"), 1)

                    def turn(g, q, par):
                        far, nxt, late = (shifted(g, q, par, by) for by in (3, 2, -LAG))
                        if started(g) and q == 0:
                            copy_alpha(act, sm, tag, g - 1, pM)
                        if started(g) and q == 2:
                            exps(act, sm, tag, g - 1, 1.0)
                        if late:
                            spread(*late)
                        if nxt:
                            st_copy(*nxt[:2])
                        if started(g) and q == 3:
                            copy_weights(act, sm, tag, 1 - par, g - 1, pM)
                        if far:
                            build(*far)
                    build(0, 0, 0)
                    build(0, 1, 0)
                    st_copy(0, 0)
                    st_copy(0, 1)
                    build(0, 2, 0)
                    all_turns(act, turn, LAG + 1)

                @block.vector
                def _(dve):
                    v = nc.vector

                    def weigh(g, q, par):
                        m = quad(g, q)
                        if q == 0:
                            take_group(dve, tag + "last_", 0, g, [(last_now[:, par, :], last_mask, R)])
                        dve.wait_ge(sem(tag + "wide"), m + 1)
                        if not (skip(g) and q < 2):
                            dve.wait_ge(sem(tag + "agg"), m - 1)
                        s = par * TG + 4 * q
                        v.tensor_tensor(msg[:, q % 2, :, :], rows[:, s:s + 4, 0:D], wide[:, q % 2, :, :],
                                        ALU.mult).then_inc(sem(tag + "msg"), 1)

                    def take(g, par):
                        v.tensor_scalar(minus_rel[:, par, :], rel[:, ds(g * TG, TG)], -1.0, None, ALU.mult
                                        ).then_inc(sem(tag + "taken"), 1)

                    def add(g, q, at, j):
                        m = quad(g, q)
                        if j == 0:
                            dve.wait_ge(sem(tag + "agg"), m + 1)
                        if not (skip(g) and q == 0 and j == 0):
                            dve.wait_ge(sem(tag + "acc"), 4 * m + j)
                            dve.wait_ge(sem(tag + "deg"), 4 * m + j)
                        win = acc[:, ds(at[j], P)]
                        v.tensor_tensor(win, win, pA[q % 2][:, j, :], ALU.add).then_inc(sem(tag + "acc"), 1)
                        win = deg[:, ds(at[j], P)]
                        v.tensor_tensor(win, win, pN[q % 2][0:1, j, :], ALU.add).then_inc(sem(tag + "deg"), 1)

                    def picks(g, q, par):
                        n = quad(g, q)
                        if q == 0:
                            take_group(dve, tag + "mask_", 0, g, [(mask_now[:, :], mask, R)])
                        if not (skip(g) and q == 0):
                            dve.wait_ge(sem(tag + "alpha"), n)
                        own = mask_now[:, 4 * q * R:4 * (q + 1) * R].rearrange("p (t c) -> p t c", c=R)
                        v.tensor_tensor(picked[:, :, :, :], pQ[q % 2][:, 0, :].rearrange("p (t c h) -> p t c h", c=R, h=H),
                                        own.unsqueeze(3).to_broadcast([P, 4, R, H]), ALU.mult
                                        ).then_inc(sem(tag + "prod"), 1)

                    def pick(g, q):
                        n = quad(g, q)
                        dve.wait_ge(sem(tag + "prod"), n + 1)
                        v.tensor_reduce(al[:, :, :], picked[:, :, :, :].rearrange("p t c h -> p t h c"), AX.X,
                                        ALU.add).then_inc(sem(tag + "al"), 1)

                    def score(g, q, par):
                        n = quad(g, q)
                        rows_there(dve, CONVS, halved(g, par), par, q)
                        dve.wait_ge(sem(tag + "al"), 2 * n + 1)
                        s = par * TG + 4 * q
                        v.tensor_tensor(al[:, :, :], al[:, :, :], rows[:, s:s + 4, D:D + H], ALU.add
                                        ).then_inc(sem(tag + "al"), 1)

                    def leak(g, q, par):
                        n = quad(g, q)
                        dve.wait_ge(sem(tag + "al"), 2 * n + 2)
                        v.scalar_tensor_tensor(out=sm["alpha"][:, par, :, 4 * q:4 * q + 4].rearrange("p h t -> p t h"),
                                               in0=al[:, :, :], scalar=0.2, in1=al[:, :, :], op0=ALU.mult,
                                               op1=ALU.max).then_inc(sem(tag + "alpha"), 1)

                    def read_added(g, k):
                        dve.wait_ge(sem(tag + "agg"), g * QG + 7 + k)
                        v.tensor_reduce(added[:, k, :], pQ[k][:, 1, :].rearrange("p (t c) -> p c t", c=R), AX.X,
                                        ALU.add).then_inc(sem(tag + "added"), 1)

                    def rescale(G):
                        _, at = nc.values_load_multi_w_load_instructions(
                            base_i[0:1, ds(G * TG, 1)], engines=[dve.engine], min_val=0, max_val=N,
                            skip_runtime_bounds_check_because="a destination")
                        steps = [0]

                        def link(ins):
                            steps[0] += 1
                            ins.then_inc(sem(tag + "carry"), 1)
                            dve.wait_ge(sem(tag + "carry"), 6 * (G - 1) + steps[0])
                        link(v.tensor_copy(cuts_now[:, :, :], cuts[:, :, ds(G, 1)]))
                        dve.wait_ge(sem(tag + "added"), 2 * G)
                        link(v.tensor_tensor(carried[:, :], carry[:, :], added[:, 0, :], ALU.add))
                        link(v.tensor_tensor(carried[:, :], carried[:, :], added[:, 1, :], ALU.add))
                        dve.wait_ge(sem(tag + "attE"), G + 1)
                        link(v.tensor_tensor(carried[:, :], carried[:, :], pM[:, 128:128 + R], ALU.mult))
                        link(v.tensor_scalar(carried[:, :], carried[:, :], cuts_now[:, 0, :], None, ALU.mult))
                        dve.wait_ge(sem(tag + "acc"), 4 * QG * G)
                        v.tensor_scalar(carry[:, :], carried[:, :], cuts_now[:, 1, :], None, ALU.mult)
                        link(v.tensor_reduce(acc[:, ds(at[0], 1)], carried[:, :], AX.X, ALU.add))
                        settle(dve)

                    def turn(g, q, par):
                        nxt, late, last = (shifted(g, q, par, by) for by in (4, -LAG, -LAG - 1))
                        reads = q in (4, 5) and not (isinstance(g, int) and g < 2)
                        if late:
                            weigh(*late)
                        at = bases(dve, last[0] * TG + 4 * last[1]) if last else None
                        if scored(g):
                            dve.wait_ge(sem(tag + "qx"), quad(g, q) + 1)
                        if reads:
                            if scored(g):
                                settle(dve)
                            read_added(g - 2, q - 4)
                        if scored(g):
                            picks(g, q, par)
                        if q == 5 and reads:
                            rescale(g - 1)
                        if last:
                            add(last[0], last[1], at, 0)
                        if started(g):
                            softmax_early(dve, sm, tag, q, g - 1, g - 1, pM)
                        if scored(g):
                            pick(g, q)
                        if last:
                            add(last[0], last[1], at, 1)
                        if scored(g):
                            score(g, q, par)
                        if last:
                            add(last[0], last[1], at, 2)
                        if scored(g):
                            leak(g, q, par)
                        if last:
                            add(last[0], last[1], at, 3)
                        if nxt and nxt[1] == 0:
                            take(nxt[0], nxt[2])
                        if started(g):
                            softmax_late(dve, sm, tag, q, g - 1, g - 1, pM, type_f)

                    v.memset(acc[:, :], 0.0)
                    v.memset(deg[:, :], 0.0)
                    v.memset(carry[:, :], 0.0)
                    v.memset(sm["rowF"][:, :, :], NEG)
                    v.memset(sm["sumF"][:, :, :], 0.0)
                    v.memset(sm["sumB"][:, :, :], 0.0)
                    v.memset(sm["rowB"][:, :, :], NEG).then_inc(sem(tag + "clear"), 1)
                    dve.wait_ge(sem(tag + "clear"), 1)
                    settle(dve)
                    take(0, 0)
                    all_turns(dve, turn, LAG + 1)

        def rel_prepare(sb, type_f, mask, last_mask, cuts, idx1):
            tc_i = sb("tc_i", [P, T], i32)
            tr_i = sb("tr_i", [P, GROUPS * P], i32)
            ends_i = sb("ends_i", [P, 4, T], i32)
            ends_f = sb("ends_f", [P, 4, T])
            t_f = sb("t_f", [P, T])
            s_f = sb("s_f", [P, T])
            at_end = sb("at_end", [P, T])
            with nc.Block() as block:
                @block.sync
                def _(sp):
                    sp.dma_start(tc_i[:, :], type_c).then_inc(sem("rt_in"), 16)
                    sp.dma_start(ends_i[:, 0, :], dst_c).then_inc(sem("rt_in"), 16)
                    for k, row in enumerate((first_row, last_row, last_prev)):
                        sp.dma_start(ends_i[:, 1 + k, :], row.to_broadcast([P, T])).then_inc(sem("rt_in"), 16)
                    for h in range(H):
                        sp.dma_start(tr_i[h * TG:(h + 1) * TG, :], type_r).then_inc(sem("rt_in"), 16)

                @block.vector
                def _(dve):
                    v = nc.vector
                    dve.wait_ge(sem("rt_in"), 16 * (5 + H))
                    v.tensor_copy(type_f[:, :], tr_i[:, :])
                    v.tensor_copy(t_f[:, :], tc_i[:, :])
                    v.tensor_copy(ends_f[:, :, :], ends_i[:, :, :])
                    v.tensor_copy(s_f[:, :], src_all[:, :]).then_inc(sem("rt"), 1)
                    dve.wait_ge(sem("rt"), 1)
                    tiles = lambda k: ends_f[:, k, :].rearrange("p (g t) -> p g t", t=TG)
                    end = tiles(2)[:, :, TG - 1:TG]
                    v.tensor_tensor(at_end[:, :].rearrange("p (g t) -> p g t", t=TG), tiles(0),
                                    end.to_broadcast([P, GROUPS, TG]), ALU.is_equal)
                    v.tensor_tensor(cuts[:, 0, :].unsqueeze(2), tiles(1)[:, :, 0:1], tiles(3)[:, :, 0:1], ALU.is_equal)
                    v.tensor_tensor(cuts[:, 1, :].unsqueeze(2), tiles(1)[:, :, 0:1], end, ALU.is_equal
                                    ).then_inc(sem("rt"), 1)
                    dve.wait_ge(sem("rt"), 2)
                    v.tensor_tensor(cuts[:, 1, :], cuts[:, 1, :], cuts[:, 0, :], ALU.mult)
                    for c in range(R):
                        own, last = (m[:, :].rearrange("p (t c) -> p t c", c=R)[:, :, c] for m in (mask, last_mask))
                        v.tensor_scalar(own, t_f[:, :], float(c), None, ALU.is_equal)
                        v.scalar_tensor_tensor(out=last, in0=t_f[:, :], scalar=float(c), in1=at_end[:, :],
                                               op0=ALU.is_equal, op1=ALU.mult)
                    v.scalar_tensor_tensor(out=idx1[:, :], in0=t_f[:, :], scalar=float(NPAD), in1=s_f[:, :],
                                           op0=ALU.mult, op1=ALU.add)

        def rel_nodes(sb, pb, acc, deg, dinv_f, dinv_n):
            v, a = nc.vector, nc.scalar
            pn = pb("pn", [P, NT])
            with nc.Block() as block:
                @block.vector
                def _(dve):
                    dve.wait_ge(sem("rn_sd"), 2)
                    v.reciprocal(dinv_n[:, :], dinv_n[:, :])
                    v.reciprocal(dinv_f[:, :], dinv_f[:, :])

                @block.tensor
                def _(pe):
                    for t in range(NT):
                        last = nc.tensor.matmul(pn[:, t:t + 1], deg[:, t * P:(t + 1) * P], ones[0:1, 0:1], start=True, stop=True)
                    last.then_inc(sem("rn_n"), 1)
                    for b in range(NB):
                        if b >= 2:
                            pe.wait_ge(sem("rn_cnt"), b - 1)
                        nc.tensor.matmul(cnt_p[b % 2][:, :], ones[0:1, :], deg[:, b * BW:(b + 1) * BW], start=True,
                                         stop=True).then_inc(sem("rn_f"), 1)

                @block.scalar
                def _(act):
                    act.wait_ge(sem("rn_n"), 1)
                    a.activation(dinv_n[:, :], pn[:, :], ACT.Sqrt, bias=ones[:, 0:1]).then_inc(sem("rn_sd"), 1)
                    for b in range(NB):
                        act.wait_ge(sem("rn_f"), b + 1)
                        a.activation(dinv_f[:, b * BW:(b + 1) * BW], cnt_p[b % 2][:, :], ACT.Sqrt,
                                     bias=ones[:, 0:1]).then_inc(sem("rn_cnt"), 1)
                    act.wait_ge(sem("rn_cnt"), NB)
                    act.sem_inc(sem("rn_sd"), 1)

            def form(dve, h, s, ps, cols, S_, o, blk):
                for b in range(NB):
                    v.tensor_tensor(h[:, blk(b)], acc[:, blk(b)], xT[:, blk(b)], ALU.add).then_inc(S_("h"), 1)
            return dict(cols=col0[0], form=form)

        def rel_layer(dinv_f, dinv_n):
            with ExitStack() as part:
                rel_project(maker(part, nc.sbuf_tensor, "_r"), maker(part, nc.psum_tensor, "_r"))
            with ExitStack() as keep:
                wide = maker(keep, nc.sbuf_tensor, "_r")
                acc = wide("acc", [P, NPAD])
                deg = wide("deg", [1, NPAD])
                with ExitStack() as mid:
                    m = maker(mid, nc.sbuf_tensor, "_r")
                    edges = (m("type_f", [P, GROUPS * P], bf16), m("mask", [P, T * R], bf16),
                             m("last_mask", [P, T * R], bf16), m("cuts", [P, 2, GROUPS]), m("idx1", [P, T], i32))
                    with ExitStack() as part:
                        rel_prepare(maker(part, nc.sbuf_tensor, "_r"), *edges)
                    with ExitStack() as part:
                        rel_edges(maker(part, nc.sbuf_tensor, "_r"), maker(part, nc.psum_tensor, "_r"), acc, deg,
                                  *edges)
                with ExitStack() as part:
                    sb, pb = maker(part, nc.sbuf_tensor, "_r"), maker(part, nc.psum_tensor, "_r")
                    with ExitStack() as few:
                        cnt_p[:] = [maker(few, nc.psum_tensor, "_r")(f"cnt{i}", [P, BW]) for i in range(2)]
                        extra = rel_nodes(sb, maker(few, nc.psum_tensor, "_r"), acc, deg, dinv_f, dinv_n)
                    node_stage("n1_", 0, "rel", sb, pb, extra)

        cnt_p = []

        def plain_project(tag, x, w, dinv_n, sb, pb):
            stage = sb("stage", [P, 2, 4, D])
            pp = [pb(f"pp{i}", [P, D]) for i in range(4)]
            prod, copied = sem(tag + "prod"), sem(tag + "copied")
            stored = [sem(tag + "stored0"), sem(tag + "stored1")]
            with nc.Block() as block:
                @block.sync
                def _(sp):
                    for b in range(NB):
                        sp.wait_ge(copied, 4 * (b + 1))
                        sp.dma_start(h_tab[b * BW:(b + 1) * BW, :].rearrange("(j p) f -> p j f", p=P),
                                     stage[:, b % 2, :, :]).then_inc(stored[b % 2], 16)
                    sp.wait_ge(stored[0], 16 * ((NB + 1) // 2))
                    sp.wait_ge(stored[1], 16 * (NB // 2))

                @block.tensor
                def _(pe):
                    for t in range(NT):
                        if t >= 4:
                            pe.wait_ge(copied, t - 3)
                        nc.tensor.matmul(pp[t % 4][:, :], x[:, t * P:(t + 1) * P], w[:, :], start=True,
                                         stop=True).then_inc(prod, 1)

                @block.scalar
                def _(act):
                    for t in range(NT):
                        b = t // 4
                        if t % 4 == 0 and b >= 2:
                            act.wait_ge(stored[b % 2], 16 * (b // 2))
                        act.wait_ge(prod, t + 1)
                        scale = dinv_n[:, t:t + 1] if dinv_n is not None else 1.0
                        nc.scalar.activation(stage[:, b % 2, t % 4, :], pp[t % 4][:, :], ACT.Copy,
                                             scale=scale).then_inc(copied, 1)

        def plain_edges(tag, turn, acc, sb, pb):
            rows = sb("rows", [P, 2 * TG, D])
            S = sb("S", [P, 2, 4, P])
            idx_now = sb("idx_now", [P, 2, TG], i32)
            rel_now = sb("rel_now", [P, TG])
            lists = [(rel_now[:, :], rel, 1)]
            pA = [pb(f"pA{i}", [P, 4, P]) for i in range(2)]
            quad = lambda g, q: g * QG + q
            skip = lambda g: isinstance(g, int) and g == 0
            with nc.Block() as block:
                @block.gpsimd
                def _(pool):
                    gather_all(pool, lambda g, par: gather_group(pool, tag, 0, g, par, h_tab, src_all, idx_now, rows,
                                                                 "agg", "agg"))

                @block.tensor
                def _(pe):
                    def group(g, par, half):
                        for q in range(QG):
                            n = quad(g, q)
                            pe.wait_ge(sem(tag + "S"), n + 1)
                            rows_there(pe, turn, half, par, q)
                            if not (skip(g) and q < 2):
                                pe.wait_ge(sem(tag + "acc"), 4 * (n - 1))
                            for j in range(4):
                                last = nc.tensor.matmul(pA[q % 2][:, j, :], rows[:, par * TG + 4 * q + j, :],
                                                        S[:, q % 2, j, :], start=True, stop=True)
                            last.then_inc(sem(tag + "agg"), 1)
                    group(0, 0, 0)
                    with pe.Fori(0, (GROUPS - 1) // 2) as k:
                        group(2 * k + 1, 1, k)
                        group(2 * k + 2, 0, k + 1)

                @block.vector
                def _(dve):
                    v = nc.vector

                    def build(g, q):
                        if not (skip(g) and q < 2):
                            dve.wait_ge(sem(tag + "agg"), quad(g, q) - 1)
                        for j in range(4):
                            t = 4 * q + j
                            last = v.tensor_scalar(S[:, q % 2, j, :], iota_row[:, :], rel_now[:, t:t + 1], None,
                                                   ALU.is_equal)
                        last.then_inc(sem(tag + "S"), 1)

                    def add(g, q, first):
                        n = quad(g, q)
                        at = bases(dve, g * TG + 4 * q)
                        dve.wait_ge(sem(tag + "agg"), n + 1)
                        for j in range(4):
                            if not (first and j == 0):
                                dve.wait_ge(sem(tag + "acc"), 4 * n + j)
                            win = acc[:, ds(at[j], P)]
                            v.tensor_tensor(win, win, pA[q % 2][:, j, :], ALU.add).then_inc(sem(tag + "acc"), 1)

                    v.memset(acc[:, :], 0.0).then_inc(sem(tag + "clear"), 1)
                    dve.wait_ge(sem(tag + "clear"), 1)
                    take_group(dve, tag, 0, 0, lists)
                    build(0, 0)
                    for q in range(1, QG):
                        build(0, q)
                        add(0, q - 1, q == 1)
                    with dve.Fori(1, GROUPS) as g:
                        take_group(dve, tag, 0, g, lists)
                        for q in range(QG):
                            build(g, q)
                            if q:
                                add(g, q - 1, False)
                            else:
                                add(g - 1, QG - 1, False)
                    add(GROUPS - 1, QG - 1, False)

        def load(tag, pairs):
            with nc.Block() as block:
                @block.sync
                def _(sp):
                    for to, source in pairs:
                        sp.dma_start(to, source).then_inc(sem(tag), 16)
                    sp.wait_ge(sem(tag), 16 * len(pairs))

        def gcn_form(w, acc, dinv_f):
            v = nc.vector

            def own(eng, x, ps, S_, blk):
                for b in range(NB):
                    if b >= 3:
                        eng.wait_ge(S_("own_read"), b - 2)
                    nc.tensor.matmul(ps[b % 3][:, :], w[:, :], x[:, blk(b)], start=True, stop=True).then_inc(S_("own"), 1)

            def combine(dve, b, ps, cols, S_, blk):
                dve.wait_ge(S_("own"), b + 1)
                t = acc[:, blk(b)]
                v.tensor_tensor(tmp[0][:, blk(b)], ps[b % 3][:, :], dinv_f[:, blk(b)], ALU.mult).then_inc(S_("own_read"), 1)
                dve.wait_ge(S_("own_read"), b + 1)
                v.tensor_tensor(t, t, tmp[0][:, blk(b)], ALU.add).then_inc(S_("gc"), 1)
                dve.wait_ge(S_("gc"), 3 * b + 1)
                v.tensor_tensor(t, t, dinv_f[:, blk(b)], ALU.mult).then_inc(S_("gc"), 1)
                dve.wait_ge(S_("gc"), 3 * b + 2)
                v.tensor_scalar(t, t, cols[:, 0:1], None, ALU.add).then_inc(S_("gc"), 1)
                dve.wait_ge(S_("gc"), 3 * b + 3)
            return own, combine

        tmp = [None]

        def gcn_layer(dinv_f, dinv_n):
            v, a = nc.vector, nc.scalar
            blk = lambda b: slice(b * BW, (b + 1) * BW)
            with ExitStack() as keep:
                wide = maker(keep, nc.sbuf_tensor, "_g")
                acc, y = wide("acc", [P, NPAD]), wide("y", [P, NPAD])
                wa, wb, cols1 = wide("wa", [P, D]), wide("wb", [P, D]), wide("cols1", [P, 3])
                tmp[0] = wide("tmp", [P, NPAD])
                load("g_in", [(wa[:, :], w2[0]), (wb[:, :], w2[1]), (cols1[:, :], b2[0])])
                for tag, x, w in (("g1_", xT, wa), ("g2_", y, wb)):
                    with ExitStack() as part:
                        plain_project(tag + "p", x, w, dinv_n, maker(part, nc.sbuf_tensor, tag), maker(part, nc.psum_tensor, tag))
                    with ExitStack() as part:
                        plain_edges(tag, CONVS + 1 + (tag == "g2_"), acc, maker(part, nc.sbuf_tensor, tag), maker(part, nc.psum_tensor, tag))
                    with ExitStack() as part:
                        sb, pb = maker(part, nc.sbuf_tensor, tag), maker(part, nc.psum_tensor, tag)
                        own, combine = gcn_form(w, acc, dinv_f)
                        if tag == "g1_":
                            ps = [pb(f"po{i}", [P, BW]) for i in range(3)]
                            S_ = lambda n: sem("g1n_" + n)
                            with nc.Block() as block:
                                @block.tensor
                                def _(pe):
                                    own(pe, xT, ps, S_, blk)

                                @block.vector
                                def _(dve):
                                    for b in range(NB):
                                        combine(dve, b, ps, cols1, S_, blk)
                                        v.tensor_scalar(tmp[0][:, blk(b)], acc[:, blk(b)], 0.0, None, ALU.min
                                                        ).then_inc(S_("neg"), 1)
                                    for b in range(NB):
                                        dve.wait_ge(S_("exp"), b + 1)
                                        v.scalar_tensor_tensor(out=acc[:, blk(b)], in0=acc[:, blk(b)], scalar=0.0,
                                                               in1=tmp[0][:, blk(b)], op0=ALU.max, op1=ALU.add
                                                               ).then_inc(S_("elu"), 1)
                                        dve.wait_ge(S_("elu"), b + 1)
                                        v.tensor_scalar(y[:, blk(b)], acc[:, blk(b)], -1.0, None, ALU.add)

                                @block.scalar
                                def _(act):
                                    for b in range(NB):
                                        act.wait_ge(S_("neg"), b + 1)
                                        a.activation(tmp[0][:, blk(b)], tmp[0][:, blk(b)], ACT.Exp).then_inc(S_("exp"), 1)
                        else:
                            def pre(eng, what, ps, S_, o, blk):
                                if what == "tensor":
                                    own(eng, y, ps, S_, blk)

                            def form(dve, h, s, ps, cols, S_, o, blk):
                                for b in range(NB):
                                    combine(dve, b, ps, cols, S_, blk)
                                    v.tensor_tensor(h[:, blk(b)], acc[:, blk(b)], xT[:, blk(b)], ALU.add
                                                    ).then_inc(S_("h"), 1)
                            node_stage("n2_", 0, "gcn", sb, pb, dict(cols=b2[1], pre=pre, form=form))

        def scatter_edges(ew, sb, pb):
            tag = "s_"
            v, a = nc.vector, nc.scalar
            Sw = sb("Sw", [P, 2, 4, P])
            same = sb("same", [P, 2, 4, P])
            before = sb("before", [P, P])
            ahead = sb("ahead", [P, 4, P])
            cnt = sb("cnt", [P, 4])
            part_i = sb("part_i", [P, 1], i32)
            own_row = sb("own_row", [P, 1])
            src_f = sb("src_f", [P, T])
            src_d = sb("src_d", [P, T])
            srcb = sb("srcb", [P, 4, 4 * P], i32)
            hwin = sb("hwin", [P, 4, 4, D])
            Gs = sb("Gs", [P, 2, 4, P])
            ys = sb("ys", [P, TG, D])
            idx = sb("idx", [P, TG], i32)
            now = {k: sb(k + "_now", [P, TG]) for k in ("rel", "ew", "src", "srd")}
            pG = [pb(f"pG{i}", [P, 4, P]) for i in range(2)]
            pY = [pb(f"pY{i}", [P, 4, D]) for i in range(2)]
            quad = lambda g, q: g * QG + q
            skip = lambda g: isinstance(g, int) and g == 0

            def groups(eng, group):
                group(0)
                with eng.Fori(1, GROUPS) as g:
                    group(g)

            with nc.Block() as block:
                @block.gpsimd
                def _(pool):
                    nc.gpsimd.iota(part_i[:, :], pattern=[[0, 1]], base=NPAD, channel_multiplier=1
                                   ).then_inc(sem(tag + "iota"), 1)

                    def group(g):
                        for q in range(QG):
                            n = quad(g, q)
                            pool.wait_ge(sem(tag + "y_out"), n + 1)
                            pool.wait_ge(sem(tag + "idx"), n + 1)
                            settle(pool)
                            if not (skip(g) and q < 2):
                                pool.wait_ge(sem(f"{tag}added{(q - 2) % QG}"), 64 * (g + (1 if q >= 2 else 0)))
                                settle(pool)
                            for j in range(4):
                                t = 4 * q + j
                                nc.gpsimd.indirect_dma_start(
                                    sum_tab[q % 2 * 4 + j], bass.IndirectOffsetOnAxis(ap=idx[:, t:t + 1], axis=0),
                                    ys[:, t, :], None, compute_op=ALU.add).then_inc(sem(f"{tag}added{q}"), 16)
                    groups(pool, group)
                    for q in range(QG):
                        pool.wait_ge(sem(f"{tag}added{q}"), 64 * GROUPS)

                @block.sync
                def _(sp):
                    def group(g):
                        for q in range(QG):
                            n = quad(g, q)
                            at = bases(sp, g * TG + 4 * q)
                            if not (skip(g) and q < 4):
                                sp.wait_ge(sem(tag + "y"), n - 3)
                                settle(sp)
                                sp.wait_ge(sem(tag + "cnt"), n - 3)
                                settle(sp)
                            for j in range(4):
                                sp.dma_start(hwin[:, q % 4, j, :], h_tab[ds(at[j], P), :]
                                             ).then_inc(sem(f"{tag}in{q % 4}"), 16)
                            sp.dma_start(srcb[:, q % 4, :], src_row[:, ds((g * TG + 4 * q) * P, 4 * P)].to_broadcast([P, 4 * P])
                                         ).then_inc(sem(f"{tag}in{q % 4}"), 16)
                    groups(sp, group)

                @block.tensor
                def _(pe):
                    def group(g):
                        for q in range(QG):
                            n = quad(g, q)
                            pe.wait_ge(sem(tag + "built"), n + 1)
                            if not (skip(g) and q < 2):
                                pe.wait_ge(sem(tag + "g_out"), n - 1)
                            for j in range(4):
                                last = nc.tensor.matmul(pG[q % 2][:, j, :], Sw[:, q % 2, j, :], same[:, q % 2, j, :],
                                                        start=True, stop=True)
                            last.then_inc(sem(tag + "g"), 1)
                            pe.wait_ge(sem(tag + "g_out"), n + 1)
                            pe.wait_ge(sem(f"{tag}in{q % 4}"), 80 * (g * (QG // 4) + q // 4 + 1))
                            if not (skip(g) and q < 2):
                                pe.wait_ge(sem(tag + "y_out"), n - 1)
                            for j in range(4):
                                last = nc.tensor.matmul(pY[q % 2][:, j, :], Gs[:, q % 2, j, :], hwin[:, q % 4, j, :],
                                                        start=True, stop=True)
                            last.then_inc(sem(tag + "y"), 1)
                    groups(pe, group)

                @block.scalar
                def _(act):
                    def group(g):
                        for q in range(QG):
                            n = quad(g, q)
                            act.wait_ge(sem(tag + "g"), n + 1)
                            if not (skip(g) and q < 2):
                                act.wait_ge(sem(tag + "y"), n - 1)
                            a.activation(Gs[:, q % 2, :, :], pG[q % 2][:, :, :], ACT.Copy).then_inc(sem(tag + "g_out"), 1)
                            act.wait_ge(sem(tag + "y"), n + 1)
                            if not skip(g):
                                act.wait_ge(sem(f"{tag}added{q}"), 64 * g)
                            a.activation(ys[:, 4 * q:4 * q + 4, :], pY[q % 2][:, :, :], ACT.Copy).then_inc(sem(tag + "y_out"), 1)
                    groups(act, group)

                @block.vector
                def _(dve):
                    def take(g):
                        take_group(dve, tag, 0, g, [(now["rel"][:, :], rel, 1), (now["ew"][:, :], ew, 1),
                                                    (now["src"][:, :], src_f, 1)])

                    def build(g, q, j):
                        n = quad(g, q)
                        if j == 0:
                            dve.wait_ge(sem(f"{tag}in{q % 4}"), 80 * (g * (QG // 4) + q // 4 + 1))
                            if not (skip(g) and q < 2):
                                dve.wait_ge(sem(tag + "g"), n - 1)
                        t = 4 * q + j
                        v.tensor_scalar(Sw[:, q % 2, j, :], iota_row[:, :], now["rel"][:, t:t + 1],
                                        now["ew"][:, t:t + 1], ALU.is_equal, ALU.mult)
                        ins = v.tensor_scalar(same[:, q % 2, j, :], srcb[:, q % 4, j * P:(j + 1) * P],
                                              now["src"][:, t:t + 1], None, ALU.is_equal)
                        if j == 3:
                            ins.then_inc(sem(tag + "built"), 1)

                    def group(g):
                        take_group(dve, tag + "srd_", 0, g, [(now["srd"][:, :], src_d, 1)])
                        for q in range(QG):
                            n = quad(g, q)
                            last = isinstance(g, int) and g == GROUPS - 1 and q == QG - 1
                            nxt = None if last else (g, q + 1) if q < QG - 1 else (g + 1, 0)
                            dve.wait_ge(sem(tag + "built"), n + 1)
                            if nxt and nxt[1] == 0:
                                settle(dve)
                                take(nxt[0])
                            if not (skip(g) and q == 0):
                                dve.wait_ge(sem(tag + "cnt"), n)
                            v.tensor_tensor(ahead[:, :, :], same[:, q % 2, :, :],
                                            before[:, :].unsqueeze(1).to_broadcast([P, 4, P]), ALU.mult
                                            ).then_inc(sem(tag + "ahead"), 1)
                            if nxt:
                                build(*nxt, 0)
                            dve.wait_ge(sem(tag + "ahead"), n + 1)
                            if not (skip(g) and q == 0):
                                dve.wait_ge(sem(tag + "idx"), n)
                            v.tensor_reduce(cnt[:, :], ahead[:, :, :], AX.X, ALU.add).then_inc(sem(tag + "cnt"), 1)
                            if nxt:
                                build(*nxt, 1)
                            dve.wait_ge(sem(tag + "cnt"), n + 1)
                            v.scalar_tensor_tensor(out=cnt[:, :], in0=cnt[:, :], scalar=0.0,
                                                   in1=now["srd"][:, 4 * q:4 * q + 4], op0=ALU.is_equal,
                                                   op1=ALU.mult).then_inc(sem(tag + "first"), 1)
                            if nxt:
                                build(*nxt, 2)
                            dve.wait_ge(sem(tag + "first"), n + 1)
                            if not skip(g):
                                dve.wait_ge(sem(f"{tag}added{q}"), 64 * g)
                            v.tensor_scalar(idx[:, 4 * q:4 * q + 4], cnt[:, :], own_row[:, :], None, ALU.add
                                            ).then_inc(sem(tag + "idx"), 1)
                            if nxt:
                                build(*nxt, 3)
                        settle(dve)
                    dve.wait_ge(sem(tag + "iota"), 1)
                    v.tensor_copy(own_row[:, :], part_i[:, :])
                    v.tensor_copy(src_f[:, :], src_all[:, :]).then_inc(sem(tag + "prep"), 1)
                    dve.wait_ge(sem(tag + "prep"), 1)
                    v.tensor_scalar(before[:, :], iota_row[:, :], float(NPAD), own_row[:, :], ALU.add, ALU.is_lt)
                    v.tensor_scalar(src_d[:, :], src_f[:, :], own_row[:, :], None, ALU.subtract).then_inc(sem(tag + "prep"), 1)
                    dve.wait_ge(sem(tag + "prep"), 2)
                    take(0)
                    for j in range(4):
                        build(0, 0, j)
                    group(0)
                    with dve.Fori(1, GROUPS - 1) as g:
                        group(g)
                    group(GROUPS - 1)

        def scatter_layer():
            v = nc.vector
            tag = "w_"
            with ExitStack() as keep:
                wide = maker(keep, nc.sbuf_tensor, "_w")
                w, ew = wide("w", [P, D]), wide("ew", [P, T])
                with nc.Block() as block:
                    @block.sync
                    def _(sp):
                        sp.dma_start(w[:, :], w3).then_inc(sem("w_in"), 16)
                        sp.dma_start(ew[:, :], ew_c).then_inc(sem("w_in"), 16)
                        sp.wait_ge(sem("w_in"), 32)
                        sp.wait_ge(sem("zeroed"), 16 * 8 * (NB + 1))
                with ExitStack() as part:
                    plain_project(tag + "p", xT, w, None, maker(part, nc.sbuf_tensor, tag), maker(part, nc.psum_tensor, tag))
                with ExitStack() as part:
                    scatter_edges(ew, maker(part, nc.sbuf_tensor, tag), maker(part, nc.psum_tensor, tag))
                with ExitStack() as part:
                    sb = maker(part, nc.sbuf_tensor, tag)
                    parts = sb("parts", [P, 2, 8, 4, D])

                    def fetch(eng, S_, tables):
                        for b in range(NB):
                            if b >= 2:
                                eng.wait_ge(S_("summed"), b - 1)
                            for k in tables:
                                eng.dma_start(parts[:, b % 2, k, :, :],
                                             sum_tab[k][b * BW:(b + 1) * BW, :].rearrange("(j p) f -> p j f", p=P)
                                             ).then_inc(S_(f"parts{b % 2}"), 16)

                    def pre(eng, what, ps, S_, o, blk):
                        if what != "tensor":
                            return
                        for b in range(NB):
                            eng.wait_ge(S_(f"parts{b % 2}"), 128 * (b // 2 + 1))
                            if b >= 3:
                                eng.wait_ge(S_("z"), 2 * (b - 3) + 1)
                            for j in range(4):
                                for k in range(8):
                                    last = nc.tensor.matmul(ps[b % 3][:, j * P:(j + 1) * P], parts[:, b % 2, k, j, :],
                                                            ident[:, :], start=k == 0, stop=k == 7)
                            last.then_inc(S_("summed"), 1)

                    def form(dve, h, s, ps, cols, S_, o, blk):
                        for b in range(NB):
                            t = h[:, blk(b)]
                            dve.wait_ge(S_("summed"), b + 1)
                            v.tensor_scalar(t, ps[b % 3][:, :], cols[:, 0:1], None, ALU.add).then_inc(S_("z"), 1)
                            dve.wait_ge(S_("z"), 2 * b + 1)
                            v.scalar_tensor_tensor(out=t, in0=t, scalar=0.01, in1=t, op0=ALU.mult, op1=ALU.max
                                                   ).then_inc(S_("z"), 1)
                            dve.wait_ge(S_("z"), 2 * b + 2)
                            v.tensor_tensor(t, t, xT[:, blk(b)], ALU.add).then_inc(S_("h"), 1)
                    node_stage("n3_", 0, "weighted", sb, maker(part, nc.psum_tensor, tag),
                               dict(cols=b3, pre=pre, form=form, fetch=fetch))

        with nc.Fori(0, CONVS - 1) as l:
            conv_layer(l, "conv")
        conv_layer(CONVS - 1, "last")
        recycle()
        with ExitStack() as scope:
            dinv_f = scope.enter_context(nc.sbuf_tensor("dinv_f", [P, NPAD], f32))
            dinv_n = scope.enter_context(nc.sbuf_tensor("dinv_n", [P, NT], f32))
            rel_layer(dinv_f, dinv_n)
            recycle()
            gcn_layer(dinv_f, dinv_n)
            recycle()
        scatter_layer()
        with nc.Block() as block:
            @block.sync
            def _(sp):
                sp.dma_start(out, xT[:, 0:N]).then_inc(sem("stored"), 16)
                sp.wait_ge(sem("stored"), 16)


_INS = ["xT_in", "src_c", "src_row", "dst_c", "dst_row", "prev_row", "next_row", "first_row", "first_next", "last_row",
        "last_prev", "type_c", "type_r", "ew_c", "w0", "b0", "col0", "w1", "w1T", "a1", "w2", "b2", "w3", "b3"]


def kernel(**inputs):
    import numpy as np
    import concourse.bacc as bacc
    from concourse import mybir as mb
    from concourse.bass_utils import run_bass_kernel_spmd as run

    z = {k: np.asarray(v) for k, v in inputs.items()}
    pad = T * P - EDGES
    src = np.concatenate([z["src"], np.zeros(pad, np.int32)])
    dst = np.concatenate([z["dst"], np.full(pad, N, np.int32)])
    typ = np.concatenate([z["edge_type_4"], np.zeros(pad, np.int32)])
    ew = np.concatenate([z["edge_weight"], np.zeros(pad, np.float32)])
    prev = np.concatenate([np.full(1, -1, np.int32), dst[:-1]])
    nxt = np.concatenate([dst[1:], np.full(1, -1, np.int32)])

    def cols(a):
        return a.reshape(T, P).T

    def rows(a):
        return a.reshape(GROUPS, TG, P).transpose(1, 0, 2).reshape(TG, GROUPS * P)

    ln_g = np.concatenate([z["L0_gnn_ln_g"], np.ones((1, D), np.float32)])
    ln_b = np.concatenate([z["L0_gnn_ln_b"], np.zeros((1, D), np.float32)])
    a1 = np.zeros((R, 2, H, D), np.float32)
    for h in range(H):
        a1[:, :, h, h * HD:(h + 1) * HD] = z["L1_gnn_attn"].reshape(R, H, 2, HD)[:, h]
    zero = np.zeros((D, 2), np.float32)
    arrays = {
        "xT_in": np.concatenate([z["x"], np.zeros((NPAD - N, D), np.float32)]).T,
        "src_c": cols(src), "src_row": src.reshape(1, T * P), "dst_c": cols(dst), "dst_row": rows(dst), "prev_row": rows(prev), "next_row": rows(nxt),
        "first_row": dst[0::P].reshape(1, T), "first_next": np.concatenate([dst[P::P], [-1]]).reshape(1, T).astype(np.int32),
        "last_row": dst[P - 1::P].reshape(1, T), "last_prev": prev[0::P].reshape(1, T),
        "type_c": cols(typ), "type_r": rows(typ), "ew_c": cols(ew),
        "w0": np.concatenate([z["L0_gnn_Wk"], z["L0_gnn_Wv"], z["L0_gnn_Wq"], z["L0_gnn_Ws"]], axis=2),
        "b0": np.concatenate([z["L0_gnn_bk"], z["L0_gnn_bv"], z["L0_gnn_bq"]], axis=1),
        "col0": np.stack([z["L0_gnn_bs"], ln_g, ln_b], axis=2),
        "w1": z["L1_gnn_W"].transpose(1, 0, 2), "w1T": z["L1_gnn_W"].transpose(2, 0, 1),
        "a1": a1.transpose(3, 0, 1, 2),
        "w2": np.stack([z["L2_gnn_W1"], z["L2_gnn_W2"]]),
        "b2": np.stack([np.concatenate([z["L2_gnn_b1"][:, None], zero], 1), np.concatenate([z["L2_gnn_b2"][:, None], zero], 1)]),
        "w3": z["L3_gnn_weight"], "b3": np.concatenate([z["L3_gnn_bias"][:, None], zero], 1),
    }
    arrays = {k: np.ascontiguousarray(v) for k, v in arrays.items()}
    nc = bacc.Bacc("TRN2", target_bir_lowering=False, num_devices=1)
    args = [nc.dram_tensor("in_" + k, arrays[k].shape, mb.dt.from_np(arrays[k].dtype), kind="ExternalInput").ap()
            for k in _INS]
    args.append(nc.dram_tensor("out_0", (D, N), mb.dt.float32, kind="ExternalOutput").ap())
    gnn_kernel(nc, *args)
    r = run(nc, [{"in_" + k: v for k, v in arrays.items()}], core_ids=[0])
    return np.ascontiguousarray(r.results[0]["out_0"].T)
```
